# Optimizing a Trainium2 kernel written in Bass

```python
import numpy as np
import jax
import jax.numpy as jnp

def _softmax(x, axis=-1):
    return jax.nn.softmax(x, axis=axis)

def _gelu(x):
    return jax.nn.gelu(x, approximate=True)

def _silu(x):
    return jax.nn.silu(x)

def _sigmoid(x):
    return jax.nn.sigmoid(x)

def _layernorm(x, axis=-1, eps=1e-05):
    m = jnp.mean(x, axis=axis, keepdims=True)
    v = jnp.var(x, axis=axis, keepdims=True)
    return (x - m) / jnp.sqrt(v + eps)

def _scatter_add(tgt, idx, src, axis=0):
    return tgt.at[idx].add(src)

def _segment_sum(src, seg, n):
    return jax.ops.segment_sum(src, seg, n)
kernel_name = 'mk_early_fusion_d1_tok_img1024_r4_20f143'

def setup_inputs(seed: int=0):
    np.random.seed(seed)
    _w = jnp.asarray

    def _rec_inputs():
        import jax
        import jax.numpy as jnp
        _rk = jax.random.key(seed)
        x = -0.00150118 + 0.499729 * jax.random.normal(jax.random.fold_in(_rk, 1), (16, 256, 64, 2), jnp.float32)
        txt = 0.00326275 + 2.8086 * jax.random.normal(jax.random.fold_in(_rk, 2), (16, 128, 256), jnp.float32)
        return (x, txt)
    x, txt = _rec_inputs()

    def _L0_tok_setup():
        import jax, jax.numpy as jnp
        import numpy as np
        import math
        H = 256
        N = 64
        CH = 1
        SEQ_L = 256
        key = jax.random.key(seed)
        k1, k2, k3, k4 = jax.random.split(key, 4)
        log_dt = jax.random.uniform(k1, (H,), dtype=jnp.float32, minval=math.log(0.001), maxval=math.log(0.1))
        inv_A_real = jnp.log(0.5 * jnp.ones((H, N), jnp.float32)) + 0.1 * jax.random.normal(k2, (H, N), dtype=jnp.float32)
        A_imag = jnp.broadcast_to(math.pi * jnp.arange(N, dtype=jnp.float32), (H, N)).copy()
        B_ri = jax.random.normal(k3, (H, N, 2), dtype=jnp.float32) * 0.5
        C_ri = jax.random.normal(k4, (CH, H, N, 2), dtype=jnp.float32) * 0.5
        return {'log_dt': log_dt, 'inv_A_real': inv_A_real, 'A_imag': A_imag, 'B_ri': B_ri, 'C_ri': C_ri, 'L': SEQ_L}
    _L0_tok_all = _L0_tok_setup()
    _L0_tok_in = {k: v for k, v in _L0_tok_all.items() if k in ('log_dt', 'inv_A_real', 'A_imag', 'B_ri')}
    del _L0_tok_all

    def _L0_attn_setup():
        import jax, jax.numpy as jnp
        import numpy as np
        import math
        D_MODEL = 256
        N_HEADS = 16
        D_K = D_MODEL // N_HEADS
        BATCH = 4
        SEQ = 512
        TRAINING_PROGRESS = 0.25
        CONVERGENCE_PHASE = 0.5
        TENSION = abs(1.0 - 1.0)

        def _pos_encoding(seq_len, d, yellow):
            phase_mod = 0.1 * math.sin(2.0 * math.pi * TRAINING_PROGRESS)
            i_even = jnp.arange(0, d, 2, dtype=jnp.float32)
            denom = jnp.power(10000.0, 2.0 * i_even / d) * (1.0 + yellow * phase_mod)
            pos = jnp.arange(seq_len, dtype=jnp.float32)
            ang = pos[:, None] / denom[None, :]
            pe = jnp.zeros((seq_len, d), jnp.float32)
            pe = pe.at[:, 0::2].set(jnp.sin(ang))
            pe = pe.at[:, 1::2].set(jnp.cos(ang))
            return pe
        key = jax.random.key(seed)
        ks = jax.random.split(key, 8)
        x = jax.random.normal(ks[0], (BATCH, SEQ, D_MODEL), dtype=jnp.float32)
        rby = jax.random.uniform(ks[1], (3,), dtype=jnp.float32)
        s = 0.02
        Wq = jax.random.normal(ks[2], (D_MODEL, D_MODEL), dtype=jnp.float32) * s
        Wk = jax.random.normal(ks[3], (D_MODEL, D_MODEL), dtype=jnp.float32) * s
        Wv = jax.random.normal(ks[4], (D_MODEL, D_MODEL), dtype=jnp.float32) * s
        Wo = jax.random.normal(ks[5], (D_MODEL, D_MODEL), dtype=jnp.float32) * s
        bq = jnp.zeros((D_MODEL,), jnp.float32)
        bk = jnp.zeros((D_MODEL,), jnp.float32)
        bv = jnp.zeros((D_MODEL,), jnp.float32)
        bo = jnp.zeros((D_MODEL,), jnp.float32)
        ln_gamma = jnp.ones((D_MODEL,), jnp.float32)
        ln_beta = jnp.zeros((D_MODEL,), jnp.float32)
        return {'x': x, 'rby': rby, 'Wq': Wq, 'bq': bq, 'Wk': Wk, 'bk': bk, 'Wv': Wv, 'bv': bv, 'Wo': Wo, 'bo': bo, 'ln_gamma': ln_gamma, 'ln_beta': ln_beta}
    _L0_attn_all = _L0_attn_setup()
    _L0_attn_in = {k: v for k, v in _L0_attn_all.items() if k in ('rby', 'Wq', 'bq', 'Wk', 'bk', 'Wv', 'bv', 'Wo', 'bo', 'ln_gamma', 'ln_beta')}
    del _L0_attn_all

    def _L0_ffn_setup():
        import jax, jax.numpy as jnp
        import numpy as np
        H_DIM, E_DIM = (256, 128)
        N_SHARED, N_ROUTED, TOP_K = (2, 16, 4)
        B, S = (4, 512)
        key = jax.random.key(seed)
        ks = jax.random.split(key, 6)
        sc = 1.0 / np.sqrt(H_DIM)
        ec = 1.0 / np.sqrt(E_DIM)
        return {'x': jax.random.normal(ks[0], (B, S, H_DIM), dtype=jnp.float32), 'shared_up': jax.random.uniform(ks[1], (N_SHARED, E_DIM, H_DIM), jnp.float32, -sc, sc), 'shared_down': jax.random.uniform(ks[2], (N_SHARED, H_DIM, E_DIM), jnp.float32, -ec, ec), 'routed_up': jax.random.uniform(ks[3], (N_ROUTED, E_DIM, H_DIM), jnp.float32, -sc, sc), 'routed_down': jax.random.uniform(ks[4], (N_ROUTED, H_DIM, E_DIM), jnp.float32, -ec, ec), 'router_w': jax.random.uniform(ks[5], (N_ROUTED, H_DIM), jnp.float32, -sc, sc)}
    _L0_ffn_all = _L0_ffn_setup()
    _L0_ffn_in = {k: v for k, v in _L0_ffn_all.items() if k in ('shared_up', 'shared_down', 'routed_up', 'routed_down', 'router_w')}
    del _L0_ffn_all
    return {'x': x, 'txt': txt, 'L0_tok_log_dt': _L0_tok_in['log_dt'], 'L0_tok_inv_A_real': _L0_tok_in['inv_A_real'], 'L0_tok_A_imag': _L0_tok_in['A_imag'], 'L0_tok_B_ri': _L0_tok_in['B_ri'], 'L0_attn_rby': _L0_attn_in['rby'], 'L0_attn_Wq': _L0_attn_in['Wq'], 'L0_attn_bq': _L0_attn_in['bq'], 'L0_attn_Wk': _L0_attn_in['Wk'], 'L0_attn_bk': _L0_attn_in['bk'], 'L0_attn_Wv': _L0_attn_in['Wv'], 'L0_attn_bv': _L0_attn_in['bv'], 'L0_attn_Wo': _L0_attn_in['Wo'], 'L0_attn_bo': _L0_attn_in['bo'], 'L0_attn_ln_gamma': _L0_attn_in['ln_gamma'], 'L0_attn_ln_beta': _L0_attn_in['ln_beta'], 'L0_ffn_shared_up': _L0_ffn_in['shared_up'], 'L0_ffn_shared_down': _L0_ffn_in['shared_down'], 'L0_ffn_routed_up': _L0_ffn_in['routed_up'], 'L0_ffn_routed_down': _L0_ffn_in['routed_down'], 'L0_ffn_router_w': _L0_ffn_in['router_w']}

def reference(x, txt, L0_tok_log_dt, L0_tok_inv_A_real, L0_tok_A_imag, L0_tok_B_ri, L0_attn_rby, L0_attn_Wq, L0_attn_bq, L0_attn_Wk, L0_attn_bk, L0_attn_Wv, L0_attn_bv, L0_attn_Wo, L0_attn_bo, L0_attn_ln_gamma, L0_attn_ln_beta, L0_ffn_shared_up, L0_ffn_shared_down, L0_ffn_routed_up, L0_ffn_routed_down, L0_ffn_router_w):
    import jax
    import jax.numpy as jnp

    def _L0_tok_ref(log_dt, inv_A_real, A_imag, B_ri, C_ri, L):
        import jax, jax.numpy as jnp
        import numpy as np
        import math
        H = 256
        N = 64
        CH = 1
        SEQ_L = 256
        dt = jnp.exp(log_dt)
        A = -jnp.exp(inv_A_real) + 1j * A_imag
        B = B_ri[..., 0] + 1j * B_ri[..., 1]
        C = C_ri[..., 0] + 1j * C_ri[..., 1]
        dtA = A * dt[:, None]
        dA = (1.0 + dtA / 2) / (1.0 - dtA / 2)
        C_term = C * B[None]
        log_dA = jnp.log(dA)
        V = jnp.exp(log_dA[:, :, None] * jnp.arange(L))
        K = 2.0 * jnp.einsum('chn,hnl->chl', C_term, V).real
        return K.astype(jnp.float32)

    def _L0_attn_ref(x, rby, Wq, bq, Wk, bk, Wv, bv, Wo, bo, ln_gamma, ln_beta):
        import jax, jax.numpy as jnp
        import numpy as np
        import math
        D_MODEL = 256
        N_HEADS = 16
        D_K = D_MODEL // N_HEADS
        BATCH = 4
        SEQ = 512
        TRAINING_PROGRESS = 0.25
        CONVERGENCE_PHASE = 0.5
        TENSION = abs(1.0 - 1.0)

        def _pos_encoding(seq_len, d, yellow):
            phase_mod = 0.1 * math.sin(2.0 * math.pi * TRAINING_PROGRESS)
            i_even = jnp.arange(0, d, 2, dtype=jnp.float32)
            denom = jnp.power(10000.0, 2.0 * i_even / d) * (1.0 + yellow * phase_mod)
            pos = jnp.arange(seq_len, dtype=jnp.float32)
            ang = pos[:, None] / denom[None, :]
            pe = jnp.zeros((seq_len, d), jnp.float32)
            pe = pe.at[:, 0::2].set(jnp.sin(ang))
            pe = pe.at[:, 1::2].set(jnp.cos(ang))
            return pe
        B, S, d = x.shape
        red, blue, yellow = (rby[0], rby[1], rby[2])
        x = x + _pos_encoding(S, d, yellow)[None, :, :]

        def proj(W, b):
            return (x @ W.T + b).reshape(B, S, N_HEADS, D_K).transpose(0, 2, 1, 3)
        Q, K, V = (proj(Wq, bq), proj(Wk, bk), proj(Wv, bv))
        scale = jnp.sqrt(D_K * (1.0 + TENSION * red))
        logits = jnp.einsum('bhqd,bhkd->bhqk', Q, K) / scale
        scale_matrix = 1.0 + red * 0.1 + blue * 0.05 + yellow * 0.15
        logits = logits * scale_matrix
        attn = jax.nn.softmax(logits, axis=-1)
        eps_adaptive = 0.1 * math.sin(2.0 * math.pi * CONVERGENCE_PHASE)
        out = jnp.einsum('bhqk,bhkd->bhqd', attn, V) * (1.0 + yellow * eps_adaptive)
        out = out.transpose(0, 2, 1, 3).reshape(B, S, d)
        out = out @ Wo.T + bo
        x = x + out
        mean = jnp.mean(x, axis=-1, keepdims=True)
        var = jnp.var(x, axis=-1, keepdims=True)
        eps_rby = 1e-05 * (1.0 + blue * 0.1)
        gamma_rby = ln_gamma * (1.0 + red * 0.1 + yellow * 0.05)
        normalized = (x - mean) / jnp.sqrt(var + eps_rby)
        return normalized * gamma_rby + ln_beta

    def _L0_ffn_ref(x, shared_up, shared_down, routed_up, routed_down, router_w):
        import jax, jax.numpy as jnp
        import numpy as np
        H_DIM, E_DIM = (256, 128)
        N_SHARED, N_ROUTED, TOP_K = (2, 16, 4)
        B, S = (4, 512)
        b, s, h = x.shape
        xt = x.reshape(-1, h)
        up_s = jnp.einsum('th,seh->tse', xt, shared_up)
        shared = jnp.einsum('tse,she->th', jax.nn.gelu(up_s, approximate=False), shared_down)
        probs = jax.nn.softmax(xt @ router_w.T, axis=-1)
        topk_p, topk_i = jax.lax.top_k(probs, TOP_K)
        gate = jnp.zeros_like(probs).at[jnp.arange(xt.shape[0])[:, None], topk_i].add(topk_p)
        up_r = jnp.einsum('th,reh->tre', xt, routed_up)
        act = jax.nn.gelu(up_r, approximate=False) * gate[:, :, None]
        routed = jnp.einsum('tre,rhe->th', act, routed_down)
        return (shared + routed).reshape(b, s, h)
    h = _L0_tok_ref(L0_tok_log_dt, L0_tok_inv_A_real, L0_tok_A_imag, L0_tok_B_ri, x, 256)
    h = jnp.concatenate([h, txt], axis=1)
    h = h + _L0_attn_ref(_layernorm(h, axis=-1), L0_attn_rby, L0_attn_Wq, L0_attn_bq, L0_attn_Wk, L0_attn_bk, L0_attn_Wv, L0_attn_bv, L0_attn_Wo, L0_attn_bo, L0_attn_ln_gamma, L0_attn_ln_beta)
    h = h + _L0_ffn_ref(_layernorm(h, axis=-1), L0_ffn_shared_up, L0_ffn_shared_down, L0_ffn_routed_up, L0_ffn_routed_down, L0_ffn_router_w)
    return h

_drawn_inputs = setup_inputs


def setup_inputs(seed=0):
    import zlib

    import numpy as np

    out = dict(_drawn_inputs(seed))
    spreads = {'L0_attn_bq': (0.0, 0.8),
     'L0_attn_bk': (0.0, 0.8),
     'L0_attn_bv': (0.0, 0.8),
     'L0_attn_bo': (0.0, 0.434),
     'L0_attn_ln_gamma': (1.0, 0.2),
     'L0_attn_ln_beta': (0.0, 0.347)}
    factors = {'L0_attn_Wq': 8.0,
     'L0_attn_Wk': 8.0,
     'L0_attn_Wv': 4.475,
     'L0_attn_Wo': 4.488,
     'L0_ffn_routed_up': 6.153,
     'L0_ffn_routed_down': 5.781,
     'L0_ffn_router_w': 6.536}
    for name, (base, spread) in spreads.items():
        noise = np.random.default_rng([zlib.crc32(name.encode()), seed]).standard_normal(out[name].shape)
        drawn = base * np.exp(spread * noise) if base else spread * noise
        out[name] = jnp.asarray(drawn.astype(out[name].dtype))
    for name, factor in factors.items():
        out[name] = (out[name] * factor).astype(out[name].dtype)
    return out
```

```python
import math
from contextlib import ExitStack

import numpy as np

import concourse.bass as bass
from concourse import mybir

P = 128
BATCH, HID, NST, SEQ_L = 16, 256, 64, 256
TXT = 128
D = 256
TOK = HID + TXT
NT = TOK // P
KT = D // P
HEADS, DK = 16, 16
PAIRS = HEADS // 2
EXPERTS, SHARED, TOPK, EDIM = 16, 2, 4, 128
NEXP = EXPERTS + SHARED
AHEAD, POWERS, FINE = 4, 64, 8
CH = 16
NCH = HID // CH
BANK = 512
LN_EPS = 1e-5
PHASE_MOD = 0.1 * math.sin(2.0 * math.pi * 0.25)
EPS_ADAPTIVE = 0.1 * math.sin(2.0 * math.pi * 0.5)
TENSION = abs(1.0 - 1.0)
MAGIC = 1.5 * 2.0 ** 23
LOG2E, LN2_HI, LN2_LO = 1.4426950408889634, 0.693359375, -2.12194440054690581e-4
TWO_PI_HI = 6.28125
TWO_PI_LO = 2.0 * math.pi - TWO_PI_HI
WSMALL = 4 * KT * D + KT * EXPERTS

C_LOGIT, C_EPS, C_OUT, C_GAMMA, C_FREQ = range(5)
TOP, BOT, SIGN, NTOP, ONES_ROW, POS = range(6)
NCOLS = POS + NT

SEL_QH, SEL_QL, SEL_KH, SEL_KL = range(4)
MROW = 48

ROUNDS = PAIRS * NT
STEPS = ROUNDS // 2
RING = ["xT", "qk0", "qk1", "v"] + [f"sel{p}" for p in range(PAIRS)] + [f"s{r}" for r in range(ROUNDS)] + ["mT"]
for _k in range(STEPS + 2):
    if _k < STEPS:
        RING += [f"st{2 * _k}", f"st{2 * _k + 1}"]
    if _k >= 2 and (_k - 2) % NT == NT - 1:
        RING += [f"o{(_k - 2) // NT}"]
RING += ["oT", "wo", "hT", "logit", "gT"]
USES = len(RING) // 2
assert len(RING) % 2 == 0

PLAN = [("f", 0), ("f", 1), ("f", 2), ("xT", 0), ("f", 3), ("qk", 0), ("f", 4), ("qk", 1), ("f", 5), ("v", 0)]
PLAN += [("sel", p) for p in range(4)] + [("f", 6)] + [("sel", p) for p in range(4, 8)]
for _r in range(ROUNDS):
    PLAN += [("s", _r)]
    if _r % 2 == 1 and 7 + _r // 2 < NEXP:
        PLAN += [("f", 7 + _r // 2)]
FFN_PLAN = [("f", n) for n in range(NEXP)]


def slot(tag):
    return RING.index(tag) % 2


def full_at(tag, b):
    return b * USES + (RING.index(tag) // 2 + 1)


def drained_at(tag, b):
    return b * (2 * USES) + (2 * (RING.index(tag) // 2) + 2)


def half_at(tag, b):
    return b * (2 * USES) + (2 * (RING.index(tag) // 2) + 1)


def before_at(tag, b):
    return b * (2 * USES) + 2 * (RING.index(tag) // 2)


def fusion_kernel(nc, cT, bT, log_dt, inv_a, a_imag, txt, rby, qk_bias, rows, freq, w_up, w_down, w_small,
                  ident_c, sel_c, cols_c, out):
    f32, f32r, i32 = mybir.dt.float32, mybir.dt.float32r, mybir.dt.int32
    ALU, ACT, AX = mybir.AluOpType, mybir.ActivationFunctionType, mybir.AxisListType

    ctx = ExitStack()
    with ctx:
        def sb(name, shape, dt=f32, where=ctx):
            return where.enter_context(nc.sbuf_tensor(name, shape, dt))

        def ps(name, shape, where=ctx):
            return where.enter_context(nc.psum_tensor(name, shape, f32))

        def sem(name):
            return ctx.enter_context(nc.semaphore(name))

        tok_dram = nc.dram_tensor("tok_dram", (BATCH, HID, SEQ_L), f32).ap()
        gate_dram = nc.dram_tensor("gate_dram", (EXPERTS, TOK), f32).ap()

        up_h, up_l = sb("up_h", [P, KT, NEXP, EDIM], f32r), sb("up_l", [P, KT, NEXP, EDIM], f32r)
        dn_h, dn_l = sb("dn_h", [P, NEXP, D], f32r), sb("dn_l", [P, NEXP, D], f32r)
        ws_h, ws_l = sb("ws_h", [P, WSMALL], f32r), sb("ws_l", [P, WSMALL], f32r)
        ident = sb("ident", [P, P])
        sel = sb("sel", [P, 4, P], f32r)
        pe_tab = sb("pe_tab", [P, NT, D])
        row_b = sb("row_b", [P, 4, D])
        cols = sb("cols", [P, NCOLS])
        scal = sb("scal", [P, 8])
        qkb = sb("qkb", [P, 2, 2])
        minus_half = sb("minus_half", [P, NT])

        def weight(t, n):
            return t[:, n * KT * D:(n + 1) * KT * D].rearrange("p (k o) -> p k o", k=KT)

        wq, wk, wv, wo = ((weight(ws_h, n), weight(ws_l, n)) for n in range(4))
        rw = tuple(t[:, 4 * KT * D:].rearrange("p (k o) -> p k o", k=KT) for t in (ws_h, ws_l))

        params_in, cst_in, stage_in = sem("params_in"), sem("cst_in"), sem("stage_in")
        inv_exp, dve_step, pool_step, base_ready = sem("inv_exp"), sem("dve_step"), sem("pool_step"), sem("base_ready")
        prod_re, prod_im, powers_done = sem("prod_re"), sem("prod_im"), sem("powers_done")
        c_in = [sem("c_in0"), sem("c_in1")]
        v_done, g_done, v_pool, g_pool = sem("v_done"), sem("g_done"), sem("v_pool"), sem("g_pool")
        k_full, k_copied, k_stored = sem("k_full"), sem("k_copied"), [sem("k_stored0"), sem("k_stored1")]
        hi_split, lo_split, wo_scaled = sem("hi_split"), sem("lo_split"), sem("wo_scaled")
        root_in, root_done, scal_ready, pe_arg, pe_done = (sem(n) for n in (
            "root_in", "root_done", "scal_ready", "pe_arg", "pe_done"))

        tok = ExitStack()
        with tok:
            par = sb("par", [P, 5, HID], f32, tok)
            t = sb("t", [P, 6, HID], f32, tok)
            ti = sb("ti", [P, HID], i32, tok)
            frq = sb("frq", [P, 2, D], f32, tok)
            PR, PI = sb("PR", [P, 9, HID], f32, tok), sb("PI", [P, 9, HID], f32, tok)
            QR, QI = sb("QR", [P, 9, HID], f32, tok), sb("QI", [P, 9, HID], f32, tok)
            P1, P2 = sb("P1", [P, FINE, HID], f32, tok), sb("P2", [P, FINE, HID], f32, tok)
            FR, FI = sb("FR", [P, AHEAD, HID], f32, tok), sb("FI", [P, AHEAD, HID], f32, tok)
            E1, E2 = sb("E1", [P, AHEAD, HID], f32, tok), sb("E2", [P, AHEAD, HID], f32, tok)
            X1, X2 = sb("X1", [P, 4 * HID], f32, tok), sb("X2", [P, 4 * HID], f32, tok)
            C = sb("C", [P, 2, 2, CH, BATCH], f32, tok)
            kout = sb("kout", [P, 2, CH // 2, POWERS], f32, tok)
            stage = sb("stage", [P, NEXP * EDIM], f32, tok)
            kps = ps("kps", [P, 2, BANK], tok)

            def flat(z):
                return z.rearrange("p i h -> p (i h)")

            def v_of(ring):
                return flat(QR[:, 4 * ring:4 * ring + 4, :])

            def g_of(ring):
                return flat(QI[:, 4 * ring:4 * ring + 4, :])

            def as_v(z):
                return z.rearrange("p (h i j) -> p h i j", h=CH, i=FINE)

            def as_g(z):
                return z.rearrange("p (h a c) -> p h a c", h=CH, a=AHEAD)

            def coarse(z, c):
                return z[:, 0:FINE, bass.ds(c * CH, CH)].rearrange("p i h -> p h i").unsqueeze(3) \
                    .to_broadcast([P, CH, FINE, FINE])

            def fine(z, c):
                return z[:, 0:FINE, bass.ds(c * CH, CH)].rearrange("p j h -> p h j").unsqueeze(2) \
                    .to_broadcast([P, CH, FINE, FINE])

            def chan(swapped, ring):
                return C[:, ring, swapped].unsqueeze(2).to_broadcast([P, CH, AHEAD, BATCH])

            def ahead(z, c):
                return z[:, :, bass.ds(c * CH, CH)].rearrange("p a h -> p h a").unsqueeze(3) \
                    .to_broadcast([P, CH, AHEAD, BATCH])

            Pw, Qw, Fw, Ew = (PR, PI), (QR, QI), (FR, FI), (E1, E2)
            Bw = (par[:, 3:4], par[:, 4:5])
            PRODUCTS = [(Pw, 1, 2, Pw, 1, Pw, 2), (Pw, 1, 3, Pw, 2, Pw, 3), (Pw, 1, 5, Pw, 4, Pw, 5),
                        (Pw, 4, 5, Pw, 4, Qw, 1), (Qw, 1, 2, Qw, 1, Qw, 2), (Qw, 1, 3, Qw, 2, Qw, 3),
                        (Qw, 1, 5, Qw, 4, Qw, 5), (Qw, 4, 5, Qw, 4, Fw, 1), (Fw, 1, 2, Fw, 1, Fw, 2),
                        (Fw, 1, 2, Fw, 2, Fw, 3), (Fw, 0, 4, Bw, 0, Ew, 0)]

            def operands(n):
                a, lo, hi, b, m, o, at = PRODUCTS[n]
                w = hi - lo
                bR, bI = (z[:, m:m + 1, :].to_broadcast([P, w, HID]) for z in b)
                return (a[0][:, lo:hi, :], a[1][:, lo:hi, :], bR, bI, o[0][:, at:at + w, :], o[1][:, at:at + w, :],
                        [x[:, 0:w * HID].rearrange("p (w h) -> p w h", w=w) for x in (X1, X2)])

            half_n = NEXP // 2
            pieces = [(w_up[:, k * NEXP * EDIM:(k + 1) * NEXP * EDIM],
                       *(z[:, k].rearrange("p n e -> p (n e)") for z in (up_h, up_l))) for k in range(KT)]
            pieces += [(w_down[:, k * half_n * D:(k + 1) * half_n * D],
                        *(z[:, k * half_n:(k + 1) * half_n].rearrange("p n e -> p (n e)") for z in (dn_h, dn_l)))
                       for k in range(2)]
            pieces += [(w_small, ws_h[:, :], ws_l[:, :]), (sel_c, sel[:, :, :].rearrange("p a o -> p (a o)"), None)]
            SMALL = 4

            with nc.Block() as block:
                @block.sync
                def _(sp):
                    for h in range(2):
                        hs = slice(h * NST, (h + 1) * NST)
                        sp.dma_start(par[hs, 0, :], log_dt.partition_broadcast(NST)).then_inc(params_in, 16)
                        sp.dma_start(par[hs, 1, :], inv_a).then_inc(params_in, 16)
                        sp.dma_start(par[hs, 2, :], a_imag).then_inc(params_in, 16)
                        sp.dma_start(par[hs, 3, :], bT[0:NST, :]).then_inc(params_in, 16)
                        sp.dma_start(par[hs, 4, :], bT[NST:P, :]).then_inc(params_in, 16)
                    sp.dma_start(cols[:, :], cols_c).then_inc(cst_in, 16)
                    sp.dma_start(scal[:, 5:8], rby.partition_broadcast(P)).then_inc(cst_in, 16)
                    sp.dma_start(qkb[:, :, :], qk_bias).then_inc(cst_in, 16)
                    sp.dma_start(ident[:, :], ident_c).then_inc(cst_in, 16)
                    sp.dma_start(flat(row_b[:, :, :]), rows.partition_broadcast(P)).then_inc(cst_in, 16)
                    sp.dma_start(flat(frq[:, :, :]), freq.partition_broadcast(P)).then_inc(cst_in, 16)

                    def c_load(c, ring):
                        view = cT[:, bass.ds(c * CH, CH), :]
                        sp.dma_start(C[:, ring, 0], view).then_inc(c_in[ring], 16)
                        sp.dma_start(C[0:NST, ring, 1], view[NST:P]).then_inc(c_in[ring], 16)
                        sp.dma_start(C[NST:P, ring, 1], view[0:NST]).then_inc(c_in[ring], 16)

                    def k_store(c, ring):
                        for h in range(2):
                            for a in range(AHEAD):
                                dst = tok_dram[:, bass.ds(c * CH, CH), a * POWERS:(a + 1) * POWERS] \
                                    .rearrange("c (m two) b -> two c m b", two=2)[h]
                                sp.dma_start(dst, kout[64 * h + 16 * a:64 * h + 16 * a + 16, ring]) \
                                    .then_inc(k_stored[ring], 16)

                    c_load(0, 0)
                    c_load(1, 1)
                    with sp.Fori(0, NCH // 2 - 1) as turn:
                        for ring in range(2):
                            c = turn * 2
                            sp.wait_ge(g_done, c + (ring + 1))
                            c_load(c + (ring + 2), ring)
                            sp.wait_ge(k_copied, c + (ring + 1))
                            k_store(c + ring, ring)
                    for ring in range(2):
                        sp.wait_ge(k_copied, NCH - 1 + ring)
                        k_store(NCH - 2 + ring, ring)
                    for ring in range(2):
                        sp.wait_ge(k_stored[ring], NCH // 2 * 8 * 16)

                @block.scalar
                def _(act):
                    act.wait_ge(params_in, 160)
                    act.activation(par[:, 1, :], par[:, 1, :], ACT.Exp).then_inc(inv_exp, 1)
                    for n, (src, hi, _) in enumerate(pieces):
                        w = src.shape[1]
                        if n:
                            act.wait_ge(hi_split, n)
                            act.wait_ge(lo_split, n)
                        act.dma_start(stage[:, 0:w], src).then_inc(stage_in, 16)
                        act.wait_ge(stage_in, 16 * (n + 1))
                        if n == SMALL:
                            act.wait_ge(scal_ready, 1)
                            wo_stage = stage[:, 3 * KT * D:4 * KT * D]
                            act.activation(wo_stage, wo_stage, ACT.Identity, scale=scal[:, C_OUT:C_OUT + 1]) \
                                .then_inc(wo_scaled, 1)
                            act.wait_ge(wo_scaled, 1)
                        act.activation(hi, stage[:, 0:w], ACT.Copy).then_inc(hi_split, 1)

                    def copy_out(c, ring, first):
                        act.wait_ge(k_full, c + 1)
                        if not first:
                            act.wait_ge(k_stored[ring], (c - ring) * 64)
                        act.activation(kout[:, ring].rearrange("p m b -> p (m b)"), kps[:, ring, :],
                                       ACT.Copy).then_inc(k_copied, 1)

                    for ring in range(2):
                        copy_out(ring, ring, True)
                    with act.Fori(1, NCH // 2) as turn:
                        for ring in range(2):
                            copy_out(turn * 2 + ring, ring, False)
                    for i in range(NT):
                        act.wait_ge(pe_arg, i + 1)
                        act.activation(pe_tab[:, i, :], pe_tab[:, i, :], ACT.Sin).then_inc(pe_done, 1)

                @block.vector
                def _(dve):
                    count = [0]

                    def step(ins):
                        count[0] += 1
                        ins.then_inc(dve_step, 1)
                        dve.wait_ge(dve_step, count[0])

                    dve.wait_ge(cst_in, 96)
                    red, blue, yel = (scal[:, 5 + n:6 + n] for n in range(3))
                    tmp = t[:, 0, :]
                    step(dve.memset(minus_half[:, :], -0.5))
                    step(dve.tensor_scalar(tmp[:, 3:4], red, TENSION * DK, float(DK), ALU.mult, ALU.add))
                    dve.tensor_scalar(scal[:, C_EPS:C_EPS + 1], blue, 0.1 * LN_EPS, LN_EPS, ALU.mult, ALU.add) \
                        .then_inc(root_in, 1)
                    step(dve.tensor_scalar(scal[:, C_OUT:C_OUT + 1], yel, EPS_ADAPTIVE, 1.0, ALU.mult, ALU.add))
                    step(dve.tensor_scalar(scal[:, C_FREQ:C_FREQ + 1], yel, PHASE_MOD, 1.0, ALU.mult, ALU.add))
                    step(dve.tensor_scalar(tmp[:, 0:1], red, 0.1, 1.0, ALU.mult, ALU.add))
                    step(dve.scalar_tensor_tensor(scal[:, C_GAMMA:C_GAMMA + 1], yel, 0.05, tmp[:, 0:1],
                                                  ALU.mult, ALU.add))
                    step(dve.scalar_tensor_tensor(tmp[:, 1:2], blue, 0.05, tmp[:, 0:1], ALU.mult, ALU.add))
                    step(dve.scalar_tensor_tensor(tmp[:, 2:3], yel, 0.15, tmp[:, 1:2], ALU.mult, ALU.add))
                    step(dve.tensor_scalar(row_b[:, 2, :], row_b[:, 2, :], scal[:, C_GAMMA:C_GAMMA + 1], None,
                                           ALU.mult))
                    dve.wait_ge(root_done, 1)
                    step(dve.tensor_tensor(scal[:, C_LOGIT:C_LOGIT + 1], tmp[:, 2:3], tmp[:, 4:5], ALU.mult))
                    dve.tensor_scalar(qkb[:, :, 0], qkb[:, :, 0], scal[:, C_LOGIT:C_LOGIT + 1], None, ALU.mult) \
                        .then_inc(scal_ready, 1)
                    dve.wait_ge(scal_ready, 1)

                    dve.wait_ge(params_in, 160)
                    y, k, r, q, dt, num = par[:, 0, :], *(t[:, n, :] for n in range(1, 6))
                    step(dve.tensor_scalar(k, y, LOG2E, MAGIC, ALU.mult, ALU.add))
                    step(dve.tensor_scalar(k, k, MAGIC, -127.0, ALU.subtract, ALU.max))
                    step(dve.tensor_scalar(k, k, 128.0, None, ALU.min))
                    step(dve.scalar_tensor_tensor(r, k, -LN2_HI, y, ALU.mult, ALU.add))
                    step(dve.scalar_tensor_tensor(r, k, -LN2_LO, r, ALU.mult, ALU.add))
                    step(dve.tensor_scalar(q, r, 1.0 / 5040.0, None, ALU.mult))
                    for n in (720.0, 120.0, 24.0, 6.0, 2.0, 1.0):
                        step(dve.scalar_tensor_tensor(q, q, 1.0 / n, r, ALU.add, ALU.mult))
                    step(dve.tensor_scalar(k, k, 127.0, 8388608.0, ALU.add, ALU.mult))
                    step(dve.tensor_copy(ti[:, :], k))
                    step(dve.scalar_tensor_tensor(dt, q, 1.0, ti[:, :].bitcast(f32), ALU.add, ALU.mult))
                    dve.wait_ge(inv_exp, 1)
                    ah, bh, rd = k, r, q
                    b2, a2 = X1[:, 0:HID], X1[:, HID:2 * HID]
                    step(dve.scalar_tensor_tensor(ah, par[:, 1, :], -0.5, dt, ALU.mult, ALU.mult))
                    step(dve.scalar_tensor_tensor(bh, par[:, 2, :], 0.5, dt, ALU.mult, ALU.mult))
                    step(dve.tensor_tensor(b2, bh, bh, ALU.mult))
                    step(dve.tensor_tensor(a2, ah, ah, ALU.mult))
                    step(dve.tensor_tensor(num, a2, b2, ALU.add))
                    step(dve.tensor_scalar(num, num, -1.0, 1.0, ALU.mult, ALU.add))
                    step(dve.tensor_scalar(ah, ah, -1.0, 1.0, ALU.mult, ALU.add))
                    step(dve.tensor_tensor(ah, ah, ah, ALU.mult))
                    step(dve.tensor_tensor(ah, ah, b2, ALU.add))
                    step(dve.reciprocal(rd, ah))
                    step(dve.tensor_tensor(PR[:, 1, :], num, rd, ALU.mult))
                    step(dve.scalar_tensor_tensor(PI[:, 1, :], bh, 2.0, rd, ALU.mult, ALU.mult))
                    for z, v in ((PR, 1.0), (PI, 0.0), (QR, 1.0), (QI, 0.0), (FR, 1.0)):
                        step(dve.memset(z[:, 0, :], v))
                    dve.memset(FI[:, 0, :], 0.0).then_inc(base_ready, 1)
                    dve.wait_ge(base_ready, 1)

                    for n in range(len(PRODUCTS)):
                        if n:
                            dve.wait_ge(prod_im, n)
                        aR, aI, bR, bI, oR, _, (x, _) = operands(n)
                        step(dve.tensor_tensor(x, aI, bI, ALU.mult))
                        step(dve.tensor_tensor(oR, aR, bR, ALU.mult))
                        dve.tensor_tensor(oR, oR, x, ALU.subtract).then_inc(prod_re, 1)
                        dve.wait_ge(prod_re, n + 1)
                    dve.wait_ge(prod_im, len(PRODUCTS))
                    p1, p2, qr, qi = flat(P1[:, :, :]), flat(P2[:, :, :]), flat(QR[:, 0:FINE, :]), flat(QI[:, 0:FINE, :])
                    step(dve.tensor_scalar(p1, qr, cols[:, TOP:TOP + 1], None, ALU.mult))
                    step(dve.scalar_tensor_tensor(p1, qi, cols[:, BOT:BOT + 1], p1, ALU.mult, ALU.add))
                    step(dve.tensor_scalar(p2, qr, cols[:, BOT:BOT + 1], None, ALU.mult))
                    step(dve.scalar_tensor_tensor(p2, qi, cols[:, NTOP:NTOP + 1], p2, ALU.mult, ALU.add))
                    step(dve.tensor_scalar(flat(E1[:, :, :]), flat(E1[:, :, :]), cols[:, SIGN:SIGN + 1], 2.0,
                                           ALU.mult, ALU.mult))
                    dve.tensor_scalar(flat(E2[:, :, :]), flat(E2[:, :, :]), -2.0, None, ALU.mult) \
                        .then_inc(powers_done, 1)
                    dve.wait_ge(powers_done, 1)

                    def chunk(c, ring, first):
                        if not first:
                            dve.wait_ge(k_full, c - 1)
                        v, g = v_of(ring), g_of(ring)
                        dve.tensor_tensor(as_v(v), coarse(P1, c), fine(PR, c), ALU.mult).then_inc(v_done, 1)
                        dve.wait_ge(c_in[ring], (c - ring) * 24 + 48)
                        dve.tensor_tensor(as_g(g), chan(0, ring), ahead(E1, c), ALU.mult).then_inc(v_done, 1)
                        dve.wait_ge(v_pool, c + 1)
                        dve.wait_ge(v_done, c * 3 + 1)
                        dve.tensor_tensor(v, v, X1[:, :], ALU.add).then_inc(v_done, 1)
                        dve.wait_ge(g_pool, c + 1)
                        dve.wait_ge(v_done, c * 3 + 2)
                        dve.tensor_tensor(g, g, X2[:, :], ALU.add).then_inc(g_done, 1)

                    for ring in range(2):
                        chunk(ring, ring, True)
                    with dve.Fori(1, NCH // 2) as turn:
                        for ring in range(2):
                            chunk(turn * 2 + ring, ring, False)

                    den, kk = FR[:, 0, :], FI[:, 0, :]
                    step(dve.tensor_scalar(den, frq[:, 0, :], scal[:, C_FREQ:C_FREQ + 1], None, ALU.mult))
                    step(dve.reciprocal(den, den))
                    for i in range(NT):
                        ang = pe_tab[:, i, :]
                        step(dve.tensor_scalar(ang, den, cols[:, POS + i:POS + i + 1], None, ALU.mult))
                        step(dve.tensor_tensor(kk, ang, frq[:, 1, :], ALU.add))
                        step(dve.tensor_scalar(kk, kk, 1.0 / (2.0 * math.pi), MAGIC, ALU.mult, ALU.add))
                        step(dve.tensor_scalar(kk, kk, MAGIC, None, ALU.subtract))
                        step(dve.scalar_tensor_tensor(ang, kk, -TWO_PI_HI, ang, ALU.mult, ALU.add))
                        step(dve.scalar_tensor_tensor(ang, kk, -TWO_PI_LO, ang, ALU.mult, ALU.add))
                        step(dve.tensor_tensor(ang, ang, frq[:, 1, :], ALU.add))
                        dve.tensor_scalar(ang, ang, 3.1415925, -3.1415925, ALU.min, ALU.max).then_inc(pe_arg, 1)

                @block.gpsimd
                def _(pool):
                    count = [0]

                    def step(ins):
                        count[0] += 1
                        ins.then_inc(pool_step, 1)
                        pool.wait_ge(pool_step, count[0])

                    pool.wait_ge(root_in, 1)
                    pool.tensor_tensor(t[:, 0, 4:5], t[:, 0, 3:4], minus_half[:, 0:1], ALU.pow).then_inc(root_done, 1)
                    for n, (src, hi, lo) in enumerate(pieces):
                        if lo is not None:
                            pool.wait_ge(hi_split, n + 1)
                            pool.tensor_tensor(lo, stage[:, 0:src.shape[1]], hi.bitcast(f32), ALU.subtract) \
                                .then_inc(lo_split, 1)
                    pool.wait_ge(base_ready, 1)
                    for n in range(len(PRODUCTS)):
                        if n:
                            pool.wait_ge(prod_re, n)
                        aR, aI, bR, bI, _, oI, (_, x) = operands(n)
                        step(pool.tensor_tensor(x, aI, bR, ALU.mult))
                        step(pool.tensor_tensor(oI, aR, bI, ALU.mult))
                        pool.tensor_tensor(oI, oI, x, ALU.add).then_inc(prod_im, 1)
                        pool.wait_ge(prod_im, n + 1)
                    pool.wait_ge(powers_done, 1)

                    def chunk(c, ring, first):
                        if not first:
                            pool.wait_ge(v_done, c * 3)
                        pool.tensor_tensor(as_v(X1[:, :]), coarse(P2, c), fine(PI, c), ALU.mult).then_inc(v_pool, 1)
                        pool.wait_ge(c_in[ring], (c - ring) * 24 + 48)
                        if not first:
                            pool.wait_ge(g_done, c)
                        pool.tensor_tensor(as_g(X2[:, :]), chan(1, ring), ahead(E2, c), ALU.mult).then_inc(g_pool, 1)

                    chunk(0, 0, True)
                    chunk(1, 1, False)
                    with pool.Fori(1, NCH // 2) as turn:
                        for ring in range(2):
                            chunk(turn * 2 + ring, ring, False)

                @block.tensor
                def _(pe):
                    def chunk(c, ring, first):
                        pe.wait_ge(v_done, c * 3 + 3)
                        pe.wait_ge(g_done, c + 1)
                        if not first:
                            pe.wait_ge(k_copied, c - 1)
                        v = v_of(ring).rearrange("p (h b) -> p h b", h=CH)
                        g = g_of(ring).rearrange("p (h a) -> p h a", h=CH)
                        for hh in range(CH):
                            half, m = hh % 2, hh // 2
                            mm = pe.matmul(kps[64 * half:64 * half + 64, ring, m * POWERS:(m + 1) * POWERS],
                                           g[:, hh, :], v[:, hh, :], start=True, stop=True)
                        mm.then_inc(k_full, 1)

                    for ring in range(2):
                        chunk(ring, ring, True)
                    with pe.Fori(1, NCH // 2) as turn:
                        for ring in range(2):
                            chunk(turn * 2 + ring, ring, False)

        Qs, Ks = sb("Qs", [P, PAIRS, TOK], f32r), sb("Ks", [P, PAIRS, TOK], f32r)
        NP = 6
        probs = sb("probs", [P, NP, 2, TOK])
        gates = sb("gates", [P, 2, 2, TOK])
        x_in = sb("x_in", [P, NT, D])
        xa = sb("xa", [P, NT, D])
        xab = sb("xab", [P, NT, D])
        h2 = sb("h2", [P, NT, D])
        xT = sb("xT_h", [P, KT, TOK], f32r), sb("xT_l", [P, KT, TOK], f32r)
        hT = sb("hT_h", [P, KT, TOK], f32r), sb("hT_l", [P, KT, TOK], f32r)
        qk = [(sb(f"qk_h{m}", [P, 2, TOK], f32r), sb(f"qk_l{m}", [P, 2, TOK], f32r)) for m in range(KT)]
        v_aug = sb("v_aug", [P, NT, HEADS, 32])
        o_t = sb("o_t", [P, TOK])
        g_act, g_mul = sb("g_act", [P, 2, TOK]), sb("g_mul", [P, 2, TOK])
        act_h, act_l = sb("act_h", [P, 3, TOK], f32r), sb("act_l", [P, 3, TOK], f32r)
        stats, mv = sb("stats", [P, NT, 6]), sb("mv", [P, NT, 2])
        wait_carrier = sb("wait_carrier", [P, 1])
        eps_ln, eps_attn = sb("eps_ln", [P, NT]), sb("eps_attn", [P, NT])
        veps, rstd = sb("veps", [P, NT]), sb("rstd", [P, NT])
        m_neg = sb("m_neg", [P, NT, 2, PAIRS])
        o_rec = sb("o_rec", [P, NT * 4])
        l_max, l_sum = sb("l_max", [P, NT]), sb("l_sum", [P, NT])
        l_exp, gate = sb("l_exp", [P, NT, EXPERTS]), sb("gate", [P, NT, EXPERTS])
        pr, rest = sb("pr", [P, NT, EXPERTS + 8]), sb("rest", [P, NT, EXPERTS + 8])
        top8, found = sb("top8", [P, NT, 8]), sb("found", [P, NT, 8])
        qk_f = probs[:, 0]
        max_h, max_l = probs[0:HEADS, 4, 0, :].bitcast(f32r), probs[0:HEADS, 4, 1, :].bitcast(f32r)
        gate_t = probs[0:EXPERTS, 5, 0, :]

        ring = ps("ring", [P, 2, 2 * BANK])
        av_ps = ps("av_ps", [P, BANK])
        up_ps = ps("up_ps", [P, BANK])
        acc = ps("acc", [P, 2 * BANK])

        slot_full, slot_drained = [sem("slot_full0"), sem("slot_full1")], [sem("slot_drained0"), sem("slot_drained1")]
        x_loaded, xn_done, xa_ready, xab_ready, hb_ready = (sem(n) for n in (
            "x_loaded", "xn_done", "xa_ready", "xab_ready", "hb_ready"))
        stats_done, mv_done, veps_done, rstd_done = (sem(n) for n in ("stats_done", "mv_done", "veps_done", "rstd_done"))
        qk_scaled, qk_hi, qk_lo, max_stored = sem("qk_scaled"), sem("qk_hi"), sem("qk_lo"), sem("max_stored")
        av_done, ot_copied, rec_done = sem("av_done"), sem("ot_copied"), sem("rec_done")
        y_scaled, h2_ready, route, gate_ready = sem("y_scaled"), sem("h2_ready"), sem("route"), sem("gate_ready")
        gate_stored, gates_in, stored = sem("gate_stored"), [sem("gates_in0"), sem("gates_in1")], sem("stored")
        up_full, gelu_done, mul_done, hi_done, lo_done, down_done = (sem(n) for n in (
            "up_full", "gelu_done", "mul_done", "hi_done", "lo_done", "down_done"))
        res_ready, vinit, lmax_done = sem("res_ready"), sem("vinit"), sem("lmax_done")
        ROUTE = 6

        def psum(tag):
            return ring[:, slot(tag), :]

        def full(eng, tag, b):
            eng.wait_ge(slot_full[slot(tag)], full_at(tag, b))

        def drained(eng, tag, b):
            eng.wait_ge(slot_drained[slot(tag)], drained_at(tag, b))

        def half(eng, tag, b):
            eng.wait_ge(slot_drained[slot(tag)], half_at(tag, b))

        def wait_apart(dve, of, value):
            dve.wait_ge(of, value)
            dve.memset(wait_carrier[:, :], 0.0)

        def each_batch(eng, run):
            run(0, None)
            with eng.Fori(1, BATCH) as b:
                run(b, b - 1)
            run(None, BATCH - 1)

        with nc.Block() as block:
            @block.sync
            def _(sp):
                def run(b, f):
                    if b is not None:
                        if f is not None:
                            sp.wait_ge(hb_ready, b)
                        sp.dma_start(x_in[:, 0:2, :], tok_dram[b, :, :].rearrange("(i p) d -> p i d", p=P)
                                     if isinstance(b, int) else
                                     tok_dram[bass.ds(b, 1), :, :].rearrange("o (i p) d -> p (o i) d", p=P)) \
                            .then_inc(x_loaded, 16)
                        sp.dma_start(x_in[:, 2:3, :], txt[b:b + 1].rearrange("o p d -> p o d")
                                     if isinstance(b, int) else
                                     txt[bass.ds(b, 1), :, :].rearrange("o p d -> p o d")).then_inc(x_loaded, 16)
                    if f is not None:
                        sp.wait_ge(gate_stored, f * 16 + 16)
                        for c in range(EXPERTS // 2):
                            if c >= 2:
                                sp.wait_ge(mul_done, f * NEXP + 2 * c)
                            sp.dma_start(gates[:, c % 2], gate_dram[2 * c:2 * c + 2, :].partition_broadcast(P)) \
                                .then_inc(gates_in[c % 2], 16)
                    if b is not None:
                        drained(sp, "mT", b)
                        for n, src in enumerate((max_h, max_l)):
                            for e in range(2):
                                row = 64 * e + MROW + n
                                sp.dma_start(Qs[row:row + 1, :, :].bitcast(f32),
                                             src[8 * e:8 * e + 8, :].bitcast(f32)).then_inc(max_stored, 16)
                    if f is not None:
                        sp.wait_ge(res_ready, f + 1)
                        dst = out[f:f + 1] if isinstance(f, int) else out[bass.ds(f, 1), :, :]
                        sp.dma_start(dst.rearrange("o (i p) d -> p (o i) d", p=P), h2[:, :, :]).then_inc(stored, 16)
                    if b is not None:
                        drained(sp, "gT", b)
                        sp.dma_start(gate_dram[:, :], gate_t).then_inc(gate_stored, 16)

                each_batch(sp, run)
                sp.wait_ge(stored, BATCH * 16)

            @block.scalar
            def _(act):
                def gelu(n, f):
                    act.wait_ge(up_full, f * NEXP + (n + 1))
                    if n >= 2:
                        act.wait_ge(mul_done, f * NEXP + (n - 1))
                    act.activation(g_act[:, n % 2, :], up_ps[:, 0:TOK], ACT.Gelu).then_inc(gelu_done, 1)

                def high(tag, b, to):
                    full(act, tag, b)
                    act.activation(to, psum(tag).rearrange("p (k n) -> p k n", k=KT)[:, :, 0:TOK], ACT.Copy) \
                        .then_inc(slot_drained[slot(tag)], 1)

                def qk_out(m, b):
                    full(act, f"qk{m}", b)
                    if m:
                        act.wait_ge(qk_lo, b * KT + m)
                    act.activation(qk_f[:, 0, :], psum(f"qk{m}")[:, 0:TOK], ACT.Identity,
                                   bias=qkb[:, m, 0:1], scale=scal[:, C_LOGIT:C_LOGIT + 1])
                    act.activation(qk_f[:, 1, :], psum(f"qk{m}")[:, BANK:BANK + TOK], ACT.Identity,
                                   bias=qkb[:, m, 1:2]).then_inc(slot_drained[slot(f"qk{m}")], 2)

                def exps(r, b):
                    full(act, f"st{r}", b)
                    if r >= NP:
                        act.wait_ge(av_done, b * STEPS + (r - NP) // 2 + 1)
                    act.activation(probs[:, r % NP], psum(f"st{r}").rearrange("p (e n) -> p e n", e=2)[:, :, 0:TOK],
                                   ACT.Exp).then_inc(slot_drained[slot(f"st{r}")], 2)

                def run(b, f):
                    for what, n in PLAN if b is not None else FFN_PLAN:
                        if what == "f" and f is not None:
                            gelu(n, f)
                        elif what == "xT":
                            high("xT", b, xT[0][:, :, :])
                        elif what == "qk":
                            qk_out(n, b)
                        elif what == "sel":
                            full(act, f"sel{n}", b)
                            act.activation(Qs[:, n, :], psum(f"sel{n}")[:, 0:TOK], ACT.Copy) \
                                .then_inc(slot_drained[slot(f"sel{n}")], 1)
                    if b is None:
                        return
                    full(act, "mT", b)
                    act.activation(max_h, psum("mT")[0:HEADS, 0:TOK], ACT.Copy).then_inc(slot_drained[slot("mT")], 1)
                    for r in range(ROUNDS):
                        exps(r, b)
                    high("oT", b, xT[0][:, :, :])
                    high("hT", b, hT[0][:, :, :])
                    act.wait_ge(lmax_done, b + 1)
                    for i in range(NT):
                        ins = act.activation(l_exp[:, i, :], psum("logit")[:, i * EXPERTS:(i + 1) * EXPERTS], ACT.Exp,
                                             bias=l_max[:, i:i + 1])
                    ins.then_inc(slot_drained[slot("logit")], 2)

                each_batch(act, run)

            @block.vector
            def _(dve):
                def expert(n, f):
                    dve.wait_ge(gelu_done, f * NEXP + (n + 1))
                    if n >= 2:
                        dve.wait_ge(lo_done, f * NEXP + (n - 1))
                    if n < SHARED:
                        dve.tensor_copy(g_mul[:, n % 2, :], g_act[:, n % 2, :]).then_inc(mul_done, 1)
                    else:
                        q = n - SHARED
                        c = q // 2
                        dve.wait_ge(gates_in[c % 2], f * (4 * EXPERTS) + 16 * (c // 2 + 1))
                        dve.tensor_tensor(g_mul[:, n % 2, :], g_act[:, n % 2, :], gates[:, (q // 2) % 2, q % 2, :],
                                          ALU.mult).then_inc(mul_done, 1)
                    dve.wait_ge(mul_done, f * NEXP + (n + 1))
                    if n >= 3:
                        dve.wait_ge(down_done, f * NEXP + (n - 2))
                    dve.tensor_copy(act_h[:, n % 3, :], g_mul[:, n % 2, :]).then_inc(hi_done, 1)

                def low(tag, b, high, to):
                    half(dve, tag, b)
                    dve.tensor_tensor(to, psum(tag).rearrange("p (k n) -> p k n", k=KT)[:, :, 0:TOK],
                                      high.bitcast(f32), ALU.subtract).then_inc(slot_drained[slot(tag)], 1)

                def normalise(src, to, b, nth):
                    at = b * 3 + (nth + 1)
                    for i in range(NT):
                        ins = dve.bn_stats(stats[:, i, :], src[:, i, :])
                    ins.then_inc(stats_done, 1)
                    wait_apart(dve, stats_done, at)
                    for i in range(NT):
                        ins = dve.bn_aggr(mv[:, i, :], stats[:, i, :])
                    ins.then_inc(mv_done, 1)
                    dve.wait_ge(mv_done, at)
                    dve.wait_ge(rstd_done, at)
                    for i in range(NT):
                        ins = dve.tensor_scalar(to[:, i, :], src[:, i, :], mv[:, i, 0:1], rstd[:, i:i + 1],
                                                ALU.subtract, ALU.mult)
                    ins.then_inc(xn_done, 1)
                    dve.wait_ge(xn_done, at)

                def run(b, f):
                    if b is not None:
                        dve.wait_ge(x_loaded, b * 32 + 32)
                        normalise(x_in, xa, b, 0)
                        dve.tensor_tensor(xa[:, :, :], xa[:, :, :], pe_tab[:, :, :], ALU.add).then_inc(xa_ready, 1)
                    for what, n in PLAN if b is not None else FFN_PLAN:
                        if what == "f" and f is not None:
                            expert(n, f)
                        elif what == "xT":
                            low("xT", b, xT[0][:, :, :], xT[1][:, :, :])
                        elif what == "qk":
                            drained(dve, f"qk{n}", b)
                            dve.tensor_copy(qk[n][0][:, :, :], qk_f).then_inc(qk_hi, 1)
                        elif what == "v":
                            full(dve, "v", b)
                            for i in range(NT):
                                ins = dve.tensor_tensor(v_aug[:, i, :, 0:DK],
                                                        psum("v")[:, i * D:(i + 1) * D].rearrange("p (h d) -> p h d", h=HEADS),
                                                        row_b[:, 0, :].rearrange("p (h d) -> p h d", h=HEADS), ALU.add)
                            ins.then_inc(slot_drained[slot("v")], 2)
                        elif what == "sel":
                            full(dve, f"sel{n}", b)
                            dve.tensor_scalar(Ks[:, n, :], psum(f"sel{n}")[:, BANK:BANK + TOK],
                                              cols[:, ONES_ROW:ONES_ROW + 1], None, ALU.add) \
                                .then_inc(slot_drained[slot(f"sel{n}")], 1)
                        elif what == "s":
                            full(dve, f"s{n}", b)
                            dve.tensor_reduce(m_neg[:, n % NT, :, n // NT],
                                              psum(f"s{n}").rearrange("p (e n) -> p e n", e=2)[:, :, 0:TOK],
                                              AX.X, ALU.max, negate=True).then_inc(slot_drained[slot(f"s{n}")], 2)
                    if f is not None:
                        dve.wait_ge(down_done, f * NEXP + NEXP)
                        dve.tensor_tensor(h2[:, :, :].rearrange("p i d -> p (i d)"), acc[:, 0:NT * D],
                                          h2[:, :, :].rearrange("p i d -> p (i d)"), ALU.add).then_inc(res_ready, 1)
                    if b is None:
                        return
                    half(dve, "mT", b)
                    dve.tensor_tensor(max_l, psum("mT")[0:HEADS, 0:TOK], max_h.bitcast(f32), ALU.subtract) \
                        .then_inc(slot_drained[slot("mT")], 1)
                    for k in range(STEPS + 2):
                        if k >= 1 and (k - 1) % NT == NT - 1:
                            g = (k - 1) // NT
                            dve.wait_ge(av_done, b * STEPS + k)
                            if g:
                                full(dve, f"o{g - 1}", b)
                            dve.tensor_copy(o_t[:, :], av_ps[:, 0:TOK]).then_inc(ot_copied, 1)
                        if k >= 2 and (k - 2) % NT == NT - 1:
                            g = (k - 2) // NT
                            full(dve, f"o{g}", b)
                            heads = psum(f"o{g}")[:, 0:NT * P].rearrange("p (i j c) -> p i j c", i=NT, j=4)
                            rec = o_rec[:, :].rearrange("p (i j) -> p i j", i=NT)
                            dve.reciprocal(rec, heads[:, :, :, DK]).then_inc(rec_done, 1)
                            dve.wait_ge(rec_done, b * 4 + (g + 1))
                            for i in range(NT):
                                ins = dve.tensor_tensor(
                                    xa[:, i, 64 * g:64 * g + 64].rearrange("p (j d) -> p j d", j=4),
                                    heads[:, i, :, 0:DK], rec[:, i, :].unsqueeze(2).to_broadcast([P, 4, DK]), ALU.mult)
                            ins.then_inc(slot_drained[slot(f"o{g}")], 2)
                    low("oT", b, xT[0][:, :, :], xT[1][:, :, :])
                    full(dve, "wo", b)
                    dve.wait_ge(xab_ready, b + 1)
                    wide = xab[:, :, :].rearrange("p i d -> p (i d)")
                    dve.tensor_tensor(wide, psum("wo")[:, 0:NT * D], wide, ALU.add) \
                        .then_inc(slot_drained[slot("wo")], 2)
                    drained(dve, "wo", b)
                    normalise(xab, xa, b, 1)
                    gam = row_b[:, 2:3, :].to_broadcast([P, NT, D])
                    dve.tensor_tensor(xa[:, :, :], xa[:, :, :], gam, ALU.mult).then_inc(y_scaled, 1)
                    dve.wait_ge(y_scaled, b + 1)
                    dve.wait_ge(hb_ready, b + 1)
                    if f is not None:
                        dve.wait_ge(stored, b * 16)
                    dve.tensor_tensor(h2[:, :, :], xa[:, :, :], x_in[:, :, :], ALU.add).then_inc(h2_ready, 1)
                    dve.wait_ge(h2_ready, b + 1)
                    normalise(h2, xa, b, 2)
                    low("hT", b, hT[0][:, :, :], hT[1][:, :, :])

                    nth = [0]

                    def step(ins, apart=False):
                        nth[0] += 1
                        ins.then_inc(route, 1)
                        if apart:
                            wait_apart(dve, route, b * ROUTE + nth[0])
                        else:
                            dve.wait_ge(route, b * ROUTE + nth[0])

                    full(dve, "logit", b)
                    logits = psum("logit")[:, 0:NT * EXPERTS].rearrange("p (i x) -> p i x", i=NT)
                    dve.tensor_reduce(l_max[:, :], logits, AX.X, ALU.max, negate=True).then_inc(lmax_done, 1)
                    drained(dve, "logit", b)
                    step(dve.tensor_reduce(l_sum[:, :], l_exp[:, :, :], AX.X, ALU.add))
                    step(dve.reciprocal(l_sum[:, :], l_sum[:, :]))
                    step(dve.tensor_tensor(pr[:, :, 0:EXPERTS], l_exp[:, :, :],
                                           l_sum[:, :].unsqueeze(2).to_broadcast([P, NT, EXPERTS]), ALU.mult), True)
                    for i in range(NT):
                        ins = dve.max(top8[:, i, :], pr[:, i, :])
                    step(ins)
                    step(dve.tensor_copy(found[:, :, 0:TOPK], top8[:, :, 0:TOPK]), True)
                    for i in range(NT):
                        ins = dve.match_replace(rest[:, i, :], found[:, i, :], pr[:, i, :], 0.0)
                    step(ins)
                    dve.tensor_tensor(gate[:, :, :], pr[:, :, 0:EXPERTS], rest[:, :, 0:EXPERTS], ALU.subtract) \
                        .then_inc(gate_ready, 1)
                    full(dve, "gT", b)
                    dve.tensor_copy(gate_t, psum("gT")[0:EXPERTS, 0:TOK]).then_inc(slot_drained[slot("gT")], 2)

                dve.memset(v_aug[:, :, :, :], 0.0).then_inc(vinit, 1)
                dve.memset(pr[:, :, :], -1.0).then_inc(vinit, 1)
                dve.memset(found[:, :, :], -1.0).then_inc(vinit, 1)
                dve.memset(eps_ln[:, :], LN_EPS).then_inc(vinit, 1)
                dve.tensor_copy(eps_attn[:, :], scal[:, C_EPS:C_EPS + 1].to_broadcast([P, NT])).then_inc(vinit, 1)
                dve.wait_ge(vinit, 5)
                dve.memset(v_aug[:, :, :, DK:DK + 1], 1.0).then_inc(vinit, 1)
                dve.wait_ge(vinit, 6)
                each_batch(dve, run)

            @block.gpsimd
            def _(pool):
                def root(b, nth):
                    at = b * 3 + (nth + 1)
                    pool.wait_ge(mv_done, at)
                    pool.tensor_tensor(veps[:, :], mv[:, :, 1], eps_attn[:, :] if nth == 1 else eps_ln[:, :], ALU.add) \
                        .then_inc(veps_done, 1)
                    pool.wait_ge(veps_done, at)
                    pool.tensor_tensor(rstd[:, :], veps[:, :], minus_half[:, :], ALU.pow).then_inc(rstd_done, 1)

                def low(n, f):
                    pool.wait_ge(hi_done, f * NEXP + (n + 1))
                    pool.tensor_tensor(act_l[:, n % 3, :], g_mul[:, n % 2, :], act_h[:, n % 3, :].bitcast(f32),
                                       ALU.subtract).then_inc(lo_done, 1)

                def run(b, f):
                    if b is not None:
                        root(b, 0)
                        pool.wait_ge(xa_ready, b + 1)
                        pool.tensor_tensor(xab[:, :, :], xa[:, :, :], row_b[:, 1:2, :].to_broadcast([P, NT, D]),
                                           ALU.add).then_inc(xab_ready, 1)
                        pool.tensor_tensor(x_in[:, :, :], x_in[:, :, :], row_b[:, 3:4, :].to_broadcast([P, NT, D]),
                                           ALU.add).then_inc(hb_ready, 1)
                    for what, n in PLAN if b is not None else FFN_PLAN:
                        if what == "f" and f is not None:
                            low(n, f)
                        elif what == "qk":
                            pool.wait_ge(qk_hi, b * KT + (n + 1))
                            pool.tensor_tensor(qk[n][1][:, :, :], qk_f, qk[n][0][:, :, :].bitcast(f32),
                                               ALU.subtract).then_inc(qk_lo, 1)
                    if b is not None:
                        root(b, 1)
                        root(b, 2)

                pool.wait_ge(vinit, 6)
                each_batch(pool, run)

            @block.tensor
            def _(pe):
                def free(tag, b):
                    if not (isinstance(b, int) and before_at(tag, b) == 0):
                        pe.wait_ge(slot_drained[slot(tag)], before_at(tag, b))

                def done(ins, tag):
                    ins.then_inc(slot_full[slot(tag)], 1)

                def mm3(to, a, w, first=True, last=True, **more):
                    pe.matmul(to, a[0], w[0], start=first, stop=False, **more)
                    pe.matmul(to, a[0], w[1], start=False, stop=False, **more)
                    return pe.matmul(to, a[1], w[0], start=False, stop=last, **more)

                def turn(tag, src):
                    for i in range(NT):
                        for kt in range(KT):
                            ins = pe.transpose(psum(tag)[:, kt * BANK + i * P:kt * BANK + (i + 1) * P],
                                               src[:, i, kt * P:(kt + 1) * P], ident[:, :])
                    done(ins, tag)

                def by_rows(tag, xt, w, n):
                    for i in range(NT):
                        for kt in range(KT):
                            ins = mm3(psum(tag)[:, i * n:(i + 1) * n], [x[:, kt, i * P:(i + 1) * P] for x in xt],
                                      [z[:, kt, :] for z in w], kt == 0, kt == KT - 1)
                    done(ins, tag)

                def expert_up(n, f):
                    if not (isinstance(f, int) and f == 0 and n == 0):
                        pe.wait_ge(gelu_done, f * NEXP + n)
                    for kt in range(KT):
                        ins = mm3(up_ps[:, 0:TOK], (up_h[:, kt, n, :], up_l[:, kt, n, :]),
                                  [x[:, kt, :] for x in hT], kt == 0, kt == KT - 1)
                    ins.then_inc(up_full, 1)

                def expert_down(n, f):
                    pe.wait_ge(hi_done, f * NEXP + (n + 1))
                    pe.wait_ge(lo_done, f * NEXP + (n + 1))
                    for i in range(NT):
                        ins = mm3(acc[:, i * D:(i + 1) * D],
                                  [x[:, n % 3, i * P:(i + 1) * P] for x in (act_h, act_l)],
                                  (dn_h[:, n, :], dn_l[:, n, :]), n == 0 and i != 1, n == NEXP - 1,
                                  skip_group_check=True)
                    ins.then_inc(down_done, 1)

                def project(m, b):
                    free(f"qk{m}", b)
                    if m == 0:
                        drained(pe, "xT", b)
                    for n, w in enumerate((wq, wk)):
                        for kt in range(KT):
                            ins = mm3(psum(f"qk{m}")[:, n * BANK:n * BANK + TOK],
                                      [z[:, kt, m * P:(m + 1) * P] for z in w], [x[:, kt, :] for x in xT],
                                      kt == 0, kt == KT - 1)
                    done(ins, f"qk{m}")

                def stack(p, b):
                    m, at = p // 4, 32 * (p % 4)
                    free(f"sel{p}", b)
                    if p % 4 == 0:
                        pe.wait_ge(qk_hi, b * KT + (m + 1))
                        pe.wait_ge(qk_lo, b * KT + (m + 1))
                    for n, kinds in enumerate(((SEL_QH, SEL_QL), (SEL_KH, SEL_KL))):
                        for part, kind in enumerate(kinds):
                            ins = pe.matmul(psum(f"sel{p}")[:, n * BANK:n * BANK + TOK], sel[at:at + 32, kind, :],
                                            qk[m][part][at:at + 32, n, :], start=part == 0, stop=part == 1)
                    done(ins, f"sel{p}")

                def logits(r, b):
                    p, i = r // NT, r % NT
                    free(f"s{r}", b)
                    if r == 0:
                        drained(pe, "sel6", b)
                        drained(pe, "sel7", b)
                    for e in range(2):
                        rows_e = slice(64 * e, 64 * e + MROW)
                        ins = pe.matmul(psum(f"s{r}")[:, e * BANK:e * BANK + TOK], Qs[rows_e, p, i * P:(i + 1) * P],
                                        Ks[rows_e, p, :], start=True, stop=True)
                    done(ins, f"s{r}")

                def logits_t(r, b):
                    k = r // 2
                    p, i = 2 * (k // NT) + r % 2, k % NT
                    free(f"st{r}", b)
                    for e in range(2):
                        rows_e = slice(64 * e, 64 * e + 64)
                        ins = pe.matmul(psum(f"st{r}")[:, e * BANK:e * BANK + TOK], Ks[rows_e, p, i * P:(i + 1) * P],
                                        Qs[rows_e, p, :], start=True, stop=True)
                    done(ins, f"st{r}")

                def weigh(k, b):
                    g, i = k // NT, k % NT
                    drained(pe, f"st{2 * k}", b)
                    drained(pe, f"st{2 * k + 1}", b)
                    if i == 0 and g:
                        pe.wait_ge(ot_copied, b * 4 + g)
                    for j in range(4):
                        ins = pe.matmul(av_ps[32 * j:32 * j + 32, 0:TOK], v_aug[:, i, 4 * g + j, :],
                                        probs[:, (2 * k + j // 2) % NP, j % 2, :], start=i == 0, stop=i == NT - 1)
                    ins.then_inc(av_done, 1)

                def run(b, f):
                    for what, n in PLAN if b is not None else FFN_PLAN:
                        if what == "f" and f is not None:
                            expert_up(n, f)
                            if n >= 2:
                                expert_down(n - 2, f)
                        elif what == "xT":
                            free("xT", b)
                            pe.wait_ge(xa_ready, b + 1)
                            turn("xT", xa)
                        elif what == "qk":
                            project(n, b)
                        elif what == "v":
                            free("v", b)
                            by_rows("v", xT, wv, D)
                        elif what == "sel":
                            stack(n, b)
                        elif what == "s":
                            logits(n, b)
                    if f is not None:
                        expert_down(NEXP - 2, f)
                        expert_down(NEXP - 1, f)
                    if b is None:
                        return
                    free("mT", b)
                    drained(pe, f"s{ROUNDS - 1}", b)
                    drained(pe, f"s{ROUNDS - 2}", b)
                    for i in range(NT):
                        ins = pe.transpose(psum("mT")[0:HEADS, i * P:(i + 1) * P],
                                           m_neg[:, i].rearrange("p e q -> p (e q)"), ident[:, :])
                    done(ins, "mT")
                    pe.wait_ge(max_stored, b * 64 + 64)
                    for k in range(STEPS + 2):
                        if k < STEPS:
                            logits_t(2 * k, b)
                            logits_t(2 * k + 1, b)
                        if k >= 2 and (k - 2) % NT == NT - 1:
                            g = (k - 2) // NT
                            free(f"o{g}", b)
                            pe.wait_ge(ot_copied, b * 4 + (g + 1))
                            for i in range(NT):
                                ins = pe.transpose(psum(f"o{g}")[:, i * P:(i + 1) * P], o_t[:, i * P:(i + 1) * P],
                                                   ident[:, :])
                            done(ins, f"o{g}")
                        if 1 <= k <= STEPS:
                            weigh(k - 1, b)
                    free("oT", b)
                    drained(pe, "o3", b)
                    turn("oT", xa)
                    free("wo", b)
                    drained(pe, "oT", b)
                    by_rows("wo", xT, wo, D)
                    free("hT", b)
                    pe.wait_ge(xn_done, b * 3 + 3)
                    turn("hT", xa)
                    free("logit", b)
                    drained(pe, "hT", b)
                    by_rows("logit", hT, rw, EXPERTS)
                    free("gT", b)
                    pe.wait_ge(gate_ready, b + 1)
                    for i in range(NT):
                        ins = pe.transpose(psum("gT")[0:EXPERTS, i * P:(i + 1) * P], gate[:, i, :], ident[:, :])
                    done(ins, "gT")

                each_batch(pe, run)


def _constants():
    p = np.arange(P)
    sel = np.zeros((P, 4, P), np.float32)
    for kind, reps in ((SEL_QH, (0, 1)), (SEL_QL, (2,)), (SEL_KH, (0, 2)), (SEL_KL, (1,))):
        for k in range(P):
            for r in reps:
                sel[k, kind, 64 * (k % 32 // 16) + 16 * r + k % 16] = 1.0
    cols = np.zeros((P, NCOLS), np.float32)
    cols[:, TOP], cols[:, BOT] = p < 64, p >= 64
    cols[:, SIGN], cols[:, NTOP] = np.where(p < 64, 1.0, -1.0), -(p < 64).astype(np.float32)
    cols[:, ONES_ROW] = np.isin(p, (MROW, MROW + 1, 64 + MROW, 65 + MROW))
    for i in range(NT):
        cols[:, POS + i] = P * i + p
    even = np.repeat(np.arange(0, D, 2), 2)
    freq = np.stack([10000.0 ** (2.0 * even / D), np.where(np.arange(D) % 2, math.pi / 2, 0.0)]).astype(np.float32)
    return {"freq": freq.reshape(-1), "ident_c": np.eye(P, dtype=np.float32), "sel_c": sel.reshape(P, 4 * P),
            "cols_c": cols}


def kernel(x, txt, L0_tok_log_dt, L0_tok_inv_A_real, L0_tok_A_imag, L0_tok_B_ri, L0_attn_rby, L0_attn_Wq, L0_attn_bq,
           L0_attn_Wk, L0_attn_bk, L0_attn_Wv, L0_attn_bv, L0_attn_Wo, L0_attn_bo, L0_attn_ln_gamma,
           L0_attn_ln_beta, L0_ffn_shared_up, L0_ffn_shared_down, L0_ffn_routed_up, L0_ffn_routed_down,
           L0_ffn_router_w):
    import concourse.bacc as bacc
    from concourse.bass_utils import run_bass_kernel_spmd

    def transposed(w):
        w = np.asarray(w)
        return w.T.reshape(w.shape[1] // P, P, w.shape[0]).transpose(1, 0, 2).reshape(P, -1)

    up = np.concatenate([np.asarray(L0_ffn_shared_up), np.asarray(L0_ffn_routed_up)])
    down = np.concatenate([np.asarray(L0_ffn_shared_down), np.asarray(L0_ffn_routed_down)])
    arrays = {
        "cT": np.asarray(x).transpose(3, 2, 1, 0).reshape(2 * NST, HID, BATCH),
        "bT": np.asarray(L0_tok_B_ri).transpose(2, 1, 0).reshape(2 * NST, HID),
        "log_dt": np.asarray(L0_tok_log_dt),
        "inv_a": np.asarray(L0_tok_inv_A_real).T,
        "a_imag": np.asarray(L0_tok_A_imag).T,
        "txt": np.asarray(txt),
        "rby": np.asarray(L0_attn_rby),
        "qk_bias": np.stack([np.asarray(L0_attn_bq).reshape(KT, P), np.asarray(L0_attn_bk).reshape(KT, P)],
                            -1).transpose(1, 0, 2),
        "rows": np.concatenate([np.asarray(v) for v in (L0_attn_bv, L0_attn_bo, L0_attn_ln_gamma, L0_attn_ln_beta)]),
        "w_up": up.transpose(2, 0, 1).reshape(KT, P, NEXP * EDIM).transpose(1, 0, 2).reshape(P, -1),
        "w_down": down.transpose(2, 0, 1).reshape(EDIM, NEXP * D),
        "w_small": np.concatenate([transposed(w) for w in (L0_attn_Wq, L0_attn_Wk, L0_attn_Wv, L0_attn_Wo,
                                                           L0_ffn_router_w)], axis=1),
        **_constants(),
    }
    names = ["cT", "bT", "log_dt", "inv_a", "a_imag", "txt", "rby", "qk_bias", "rows", "freq", "w_up", "w_down",
             "w_small", "ident_c", "sel_c", "cols_c"]
    nc = bacc.Bacc("TRN2", target_bir_lowering=False, num_devices=1)
    feeds, aps = {}, {}
    for name in names:
        a = np.ascontiguousarray(arrays[name])
        feeds[f"in_{name}"] = a
        aps[name] = nc.dram_tensor(f"in_{name}", a.shape, mybir.dt.from_np(a.dtype), kind="ExternalInput").ap()
    out = nc.dram_tensor("out", (BATCH, TOK, D), mybir.dt.float32, kind="ExternalOutput").ap()
    fusion_kernel(nc, **aps, out=out)
    result = run_bass_kernel_spmd(nc, [feeds], core_ids=[0])
    return result.results[0]["out"]
```

```python
import math
from contextlib import ExitStack

import numpy as np

import concourse.bass as bass
from concourse import mybir

P = 128
BATCH, HID, NST, SEQ_L = 16, 256, 64, 256
TXT = 128
D = 256
TOK = HID + TXT
NT = TOK // P
KT = D // P
HEADS, DK = 16, 16
PAIRS = HEADS // 2
EXPERTS, SHARED, TOPK, EDIM = 16, 2, 4, 128
NEXP = EXPERTS + SHARED
AHEAD, POWERS, FINE = 4, 64, 8
CH = 16
NCH = HID // CH
BANK = 512
LN_EPS = 1e-5
PHASE_MOD = 0.1 * math.sin(2.0 * math.pi * 0.25)
EPS_ADAPTIVE = 0.1 * math.sin(2.0 * math.pi * 0.5)
TENSION = abs(1.0 - 1.0)
MAGIC = 1.5 * 2.0 ** 23
LOG2E, LN2_HI, LN2_LO = 1.4426950408889634, 0.693359375, -2.12194440054690581e-4
TWO_PI_HI = 6.28125
TWO_PI_LO = 2.0 * math.pi - TWO_PI_HI
WSMALL = 4 * KT * D + KT * EXPERTS

C_LOGIT, C_EPS, C_OUT, C_GAMMA, C_FREQ = range(5)
TOP, BOT, SIGN, NTOP, ONES_ROW, POS = range(6)
NCOLS = POS + NT

SEL_QH, SEL_QL, SEL_KH, SEL_KL = range(4)
MROW = 48

ROUNDS = PAIRS * NT
STEPS = ROUNDS // 2

FRONT = ("ln1", "xT", "q", "k", "v", "sel", "s", "mT")


def steps(text):
    named = []
    for word in text.split():
        what = word.rstrip("0123456789") if word not in ("ln1", "ln_h2") else word
        named += [(what, int(word[len(what):] or 0))]
    return named


PLAN = steps("""
    st0 st1 ln1 down8 st2 st3 av0 f10 down9 f11
    st4 st5 av1 xT st6 st7 av2 down10 q0
    st8 st9 o0 av3 k0 st10 st11 av4 f12 down11 f13
    st12 st13 av5 down12 q1 st14 st15 o1 av6 k1
    st16 st17 av7 f14 down13 f15 st18 st19 av8 down14
    st20 st21 o2 av9 st22 st23 av10 down15 av11 v0 v1 v2 o3
    oT f16 sel0 sel1 wo f17 sel2 sel3 ln_mean s0 sel4 down16 sel5 down17 fend ln_h2 s1 s2 sel6 s3 sel7 ln_out
    hT s4 s5 logit s6 F0 choose s7 F1 s8 gT s9 Down0 s10 Down1 s11
    s12 F2 s13 F3 s14 Down2 s15 F4 s16 Down3 s17 F5 s18 Down4 s19 F6 s20 Down5 s21 F7 s22 Down6 s23 F8 mT Down7 F9
""")
BEFORE = [step for step in PLAN if step[0] in FRONT]
FIRST = [step for step in PLAN if step[0] not in ("f", "down", "fend")]
LAST = [step for step in PLAN if step[0] not in FRONT]
AFTER = [step for step in PLAN if step[0] in ("f", "down", "fend")]


def products(plan):
    tags = []
    for what, n in plan:
        if what in ("st", "o", "q", "k", "sel", "s"):
            tags += [f"{what}{n}"]
        elif what == "v" and n == NT - 1 or what in ("xT", "oT", "wo", "hT", "logit", "mT", "gT"):
            tags += [what]
    return tags


RING = products(PLAN)
USES = len(RING) // 2
assert len(RING) % 2 == 0


def slot(tag):
    return RING.index(tag) % 2


def uses_in(tag, order):
    return sum(slot(other) == slot(tag) for other in order[:order.index(tag)])


def uses_before(tag, it):
    if isinstance(it, int) and it < 0:
        return uses_in(tag, products(BEFORE))
    order = products(LAST) if isinstance(it, int) and it == BATCH - 1 else RING
    at_first = sum(slot(other) == slot(tag) for other in products(BEFORE))
    return it * USES + (at_first + uses_in(tag, order))


def full_at(tag, it):
    return uses_before(tag, it) + 1


def drained_at(tag, it):
    return uses_before(tag, it) * 2 + 2


def half_at(tag, it):
    return uses_before(tag, it) * 2 + 1


def before_at(tag, it):
    return uses_before(tag, it) * 2


def fusion_kernel(nc, cT, bT, log_dt, inv_a, a_imag, txt, rby, qk_bias, rows, freq, w_up, w_down, w_small,
                  ident_c, sel_c, cols_c, out):
    f32, f32r, i32 = mybir.dt.float32, mybir.dt.float32r, mybir.dt.int32
    ALU, ACT, AX = mybir.AluOpType, mybir.ActivationFunctionType, mybir.AxisListType

    ctx = ExitStack()
    with ctx:
        def sb(name, shape, dt=f32, where=ctx):
            return where.enter_context(nc.sbuf_tensor(name, shape, dt))

        def ps(name, shape, where=ctx):
            return where.enter_context(nc.psum_tensor(name, shape, f32))

        def sem(name):
            return ctx.enter_context(nc.semaphore(name))

        tok_dram = nc.dram_tensor("tok_dram", (BATCH, HID, SEQ_L), f32).ap()
        gate_dram = nc.dram_tensor("gate_dram", (EXPERTS, TOK), f32).ap()

        up_h, up_l = sb("up_h", [P, KT, NEXP, EDIM], f32r), sb("up_l", [P, KT, NEXP, EDIM], f32r)
        dn_h, dn_l = sb("dn_h", [P, NEXP, D], f32r), sb("dn_l", [P, NEXP, D], f32r)
        ws_h, ws_l = sb("ws_h", [P, WSMALL], f32r), sb("ws_l", [P, WSMALL], f32r)
        ident = sb("ident", [P, P])
        sel = sb("sel", [P, 4, P], f32r)
        pe_tab = sb("pe_tab", [P, NT, D])
        row_b = sb("row_b", [P, 4, D])
        cols = sb("cols", [P, NCOLS])
        scal = sb("scal", [P, 8])
        qkb = sb("qkb", [P, 2, 2])
        minus_half = sb("minus_half", [P, NT])

        def weight(t, n):
            return t[:, n * KT * D:(n + 1) * KT * D].rearrange("p (k o) -> p k o", k=KT)

        wq, wk, wv, wo = ((weight(ws_h, n), weight(ws_l, n)) for n in range(4))
        rw = tuple(t[:, 4 * KT * D:].rearrange("p (k o) -> p k o", k=KT) for t in (ws_h, ws_l))

        params_in, cst_in, stage_in = sem("params_in"), sem("cst_in"), sem("stage_in")
        inv_exp, dve_step, pool_step, base_ready = sem("inv_exp"), sem("dve_step"), sem("pool_step"), sem("base_ready")
        prod_re, prod_im, powers_done = sem("prod_re"), sem("prod_im"), sem("powers_done")
        c_in = [sem("c_in0"), sem("c_in1")]
        v_done, g_done, v_pool, g_pool = sem("v_done"), sem("g_done"), sem("v_pool"), sem("g_pool")
        k_full, k_copied, k_stored = sem("k_full"), sem("k_copied"), [sem("k_stored0"), sem("k_stored1")]
        hi_split, lo_split, small_scaled = sem("hi_split"), sem("lo_split"), sem("small_scaled")
        root_in, root_done, scal_ready, pe_arg, pe_done = (sem(n) for n in (
            "root_in", "root_done", "scal_ready", "pe_arg", "pe_done"))

        tok = ExitStack()
        with tok:
            par = sb("par", [P, 5, HID], f32, tok)
            t = sb("t", [P, 6, HID], f32, tok)
            ti = sb("ti", [P, HID], i32, tok)
            frq = sb("frq", [P, 2, D], f32, tok)
            PR, PI = sb("PR", [P, 9, HID], f32, tok), sb("PI", [P, 9, HID], f32, tok)
            QR, QI = sb("QR", [P, 9, HID], f32, tok), sb("QI", [P, 9, HID], f32, tok)
            P1, P2 = sb("P1", [P, FINE, HID], f32, tok), sb("P2", [P, FINE, HID], f32, tok)
            FR, FI = sb("FR", [P, AHEAD, HID], f32, tok), sb("FI", [P, AHEAD, HID], f32, tok)
            E1, E2 = sb("E1", [P, AHEAD, HID], f32, tok), sb("E2", [P, AHEAD, HID], f32, tok)
            X1, X2 = sb("X1", [P, 4 * HID], f32, tok), sb("X2", [P, 4 * HID], f32, tok)
            C = sb("C", [P, 2, 2, CH, BATCH], f32, tok)
            kout = sb("kout", [P, 2, CH // 2, POWERS], f32, tok)
            stage = sb("stage", [P, NEXP * EDIM], f32, tok)
            kps = ps("kps", [P, 2, BANK], tok)

            def flat(z):
                return z.rearrange("p i h -> p (i h)")

            def v_of(ring):
                return flat(QR[:, 4 * ring:4 * ring + 4, :])

            def g_of(ring):
                return flat(QI[:, 4 * ring:4 * ring + 4, :])

            def as_v(z):
                return z.rearrange("p (h i j) -> p h i j", h=CH, i=FINE)

            def as_g(z):
                return z.rearrange("p (h a c) -> p h a c", h=CH, a=AHEAD)

            def coarse(z, c):
                return z[:, 0:FINE, bass.ds(c * CH, CH)].rearrange("p i h -> p h i").unsqueeze(3) \
                    .to_broadcast([P, CH, FINE, FINE])

            def fine(z, c):
                return z[:, 0:FINE, bass.ds(c * CH, CH)].rearrange("p j h -> p h j").unsqueeze(2) \
                    .to_broadcast([P, CH, FINE, FINE])

            def chan(swapped, ring):
                return C[:, ring, swapped].unsqueeze(2).to_broadcast([P, CH, AHEAD, BATCH])

            def ahead(z, c):
                return z[:, :, bass.ds(c * CH, CH)].rearrange("p a h -> p h a").unsqueeze(3) \
                    .to_broadcast([P, CH, AHEAD, BATCH])

            Pw, Qw, Fw, Ew = (PR, PI), (QR, QI), (FR, FI), (E1, E2)
            Bw = (par[:, 3:4], par[:, 4:5])
            PRODUCTS = [(Pw, 1, 2, Pw, 1, Pw, 2), (Pw, 1, 3, Pw, 2, Pw, 3), (Pw, 1, 5, Pw, 4, Pw, 5),
                        (Pw, 4, 5, Pw, 4, Qw, 1), (Qw, 1, 2, Qw, 1, Qw, 2), (Qw, 1, 3, Qw, 2, Qw, 3),
                        (Qw, 1, 5, Qw, 4, Qw, 5), (Qw, 4, 5, Qw, 4, Fw, 1), (Fw, 1, 2, Fw, 1, Fw, 2),
                        (Fw, 1, 2, Fw, 2, Fw, 3), (Fw, 0, 4, Bw, 0, Ew, 0)]

            def operands(n):
                a, lo, hi, b, m, o, at = PRODUCTS[n]
                w = hi - lo
                bR, bI = (z[:, m:m + 1, :].to_broadcast([P, w, HID]) for z in b)
                return (a[0][:, lo:hi, :], a[1][:, lo:hi, :], bR, bI, o[0][:, at:at + w, :], o[1][:, at:at + w, :],
                        [x[:, 0:w * HID].rearrange("p (w h) -> p w h", w=w) for x in (X1, X2)])

            half_n = NEXP // 2
            pieces = [(w_up[:, k * NEXP * EDIM:(k + 1) * NEXP * EDIM],
                       *(z[:, k].rearrange("p n e -> p (n e)") for z in (up_h, up_l))) for k in range(KT)]
            pieces += [(w_down[:, k * half_n * D:(k + 1) * half_n * D],
                        *(z[:, k * half_n:(k + 1) * half_n].rearrange("p n e -> p (n e)") for z in (dn_h, dn_l)))
                       for k in range(2)]
            pieces += [(w_small, ws_h[:, :], ws_l[:, :]), (sel_c, sel[:, :, :].rearrange("p a o -> p (a o)"), None)]
            SMALL = 4

            with nc.Block() as block:
                @block.sync
                def _(sp):
                    for h in range(2):
                        hs = slice(h * NST, (h + 1) * NST)
                        sp.dma_start(par[hs, 0, :], log_dt.partition_broadcast(NST)).then_inc(params_in, 16)
                        sp.dma_start(par[hs, 1, :], inv_a).then_inc(params_in, 16)
                        sp.dma_start(par[hs, 2, :], a_imag).then_inc(params_in, 16)
                        sp.dma_start(par[hs, 3, :], bT[0:NST, :]).then_inc(params_in, 16)
                        sp.dma_start(par[hs, 4, :], bT[NST:P, :]).then_inc(params_in, 16)
                    sp.dma_start(cols[:, :], cols_c).then_inc(cst_in, 16)
                    sp.dma_start(scal[:, 5:8], rby.partition_broadcast(P)).then_inc(cst_in, 16)
                    sp.dma_start(qkb[:, :, :], qk_bias).then_inc(cst_in, 16)
                    sp.dma_start(ident[:, :], ident_c).then_inc(cst_in, 16)
                    sp.dma_start(flat(row_b[:, :, :]), rows.partition_broadcast(P)).then_inc(cst_in, 16)
                    sp.dma_start(flat(frq[:, :, :]), freq.partition_broadcast(P)).then_inc(cst_in, 16)

                    def c_load(c, ring):
                        view = cT[:, bass.ds(c * CH, CH), :]
                        sp.dma_start(C[:, ring, 0], view).then_inc(c_in[ring], 16)
                        sp.dma_start(C[0:NST, ring, 1], view[NST:P]).then_inc(c_in[ring], 16)
                        sp.dma_start(C[NST:P, ring, 1], view[0:NST]).then_inc(c_in[ring], 16)

                    def k_store(c, ring):
                        for h in range(2):
                            for a in range(AHEAD):
                                dst = tok_dram[:, bass.ds(c * CH, CH), a * POWERS:(a + 1) * POWERS] \
                                    .rearrange("c (m two) b -> two c m b", two=2)[h]
                                sp.dma_start(dst, kout[64 * h + 16 * a:64 * h + 16 * a + 16, ring]) \
                                    .then_inc(k_stored[ring], 16)

                    c_load(0, 0)
                    c_load(1, 1)
                    with sp.Fori(0, NCH // 2 - 1) as turn:
                        for ring in range(2):
                            c = turn * 2
                            sp.wait_ge(g_done, c + (ring + 1))
                            c_load(c + (ring + 2), ring)
                            sp.wait_ge(k_copied, c + (ring + 1))
                            k_store(c + ring, ring)
                    for ring in range(2):
                        sp.wait_ge(k_copied, NCH - 1 + ring)
                        k_store(NCH - 2 + ring, ring)
                    for ring in range(2):
                        sp.wait_ge(k_stored[ring], NCH // 2 * 8 * 16)

                @block.scalar
                def _(act):
                    act.wait_ge(params_in, 160)
                    act.activation(par[:, 1, :], par[:, 1, :], ACT.Exp).then_inc(inv_exp, 1)
                    for n, (src, hi, _) in enumerate(pieces):
                        w = src.shape[1]
                        if n:
                            act.wait_ge(hi_split, n)
                            act.wait_ge(lo_split, n)
                        act.dma_start(stage[:, 0:w], src).then_inc(stage_in, 16)
                        act.wait_ge(stage_in, 16 * (n + 1))
                        if n == SMALL:
                            act.wait_ge(scal_ready, 1)
                            for m, factor in ((0, C_LOGIT), (3, C_OUT)):
                                part = stage[:, m * KT * D:(m + 1) * KT * D]
                                act.activation(part, part, ACT.Identity, scale=scal[:, factor:factor + 1]) \
                                    .then_inc(small_scaled, 1)
                            act.wait_ge(small_scaled, 2)
                        act.activation(hi, stage[:, 0:w], ACT.Copy).then_inc(hi_split, 1)

                    def copy_out(c, ring, first):
                        act.wait_ge(k_full, c + 1)
                        if not first:
                            act.wait_ge(k_stored[ring], (c - ring) * 64)
                        act.activation(kout[:, ring].rearrange("p m b -> p (m b)"), kps[:, ring, :],
                                       ACT.Copy).then_inc(k_copied, 1)

                    for ring in range(2):
                        copy_out(ring, ring, True)
                    with act.Fori(1, NCH // 2) as turn:
                        for ring in range(2):
                            copy_out(turn * 2 + ring, ring, False)
                    for i in range(NT):
                        act.wait_ge(pe_arg, i + 1)
                        act.activation(pe_tab[:, i, :], pe_tab[:, i, :], ACT.Sin).then_inc(pe_done, 1)

                @block.vector
                def _(dve):
                    count = [0]

                    def step(ins):
                        count[0] += 1
                        ins.then_inc(dve_step, 1)
                        dve.wait_ge(dve_step, count[0])

                    dve.wait_ge(cst_in, 96)
                    red, blue, yel = (scal[:, 5 + n:6 + n] for n in range(3))
                    tmp = t[:, 0, :]
                    step(dve.memset(minus_half[:, :], -0.5))
                    step(dve.tensor_scalar(tmp[:, 3:4], red, TENSION * DK, float(DK), ALU.mult, ALU.add))
                    dve.tensor_scalar(scal[:, C_EPS:C_EPS + 1], blue, 0.1 * LN_EPS, LN_EPS, ALU.mult, ALU.add) \
                        .then_inc(root_in, 1)
                    step(dve.tensor_scalar(scal[:, C_OUT:C_OUT + 1], yel, EPS_ADAPTIVE, 1.0, ALU.mult, ALU.add))
                    step(dve.tensor_scalar(scal[:, C_FREQ:C_FREQ + 1], yel, PHASE_MOD, 1.0, ALU.mult, ALU.add))
                    step(dve.tensor_scalar(tmp[:, 0:1], red, 0.1, 1.0, ALU.mult, ALU.add))
                    step(dve.scalar_tensor_tensor(scal[:, C_GAMMA:C_GAMMA + 1], yel, 0.05, tmp[:, 0:1],
                                                  ALU.mult, ALU.add))
                    step(dve.scalar_tensor_tensor(tmp[:, 1:2], blue, 0.05, tmp[:, 0:1], ALU.mult, ALU.add))
                    step(dve.scalar_tensor_tensor(tmp[:, 2:3], yel, 0.15, tmp[:, 1:2], ALU.mult, ALU.add))
                    step(dve.tensor_scalar(row_b[:, 2, :], row_b[:, 2, :], scal[:, C_GAMMA:C_GAMMA + 1], None,
                                           ALU.mult))
                    dve.wait_ge(root_done, 1)
                    step(dve.tensor_tensor(scal[:, C_LOGIT:C_LOGIT + 1], tmp[:, 2:3], tmp[:, 4:5], ALU.mult))
                    dve.tensor_scalar(qkb[:, :, 0], qkb[:, :, 0], scal[:, C_LOGIT:C_LOGIT + 1], None, ALU.mult) \
                        .then_inc(scal_ready, 1)
                    dve.wait_ge(scal_ready, 1)

                    dve.wait_ge(params_in, 160)
                    y, k, r, q, dt, num = par[:, 0, :], *(t[:, n, :] for n in range(1, 6))
                    step(dve.tensor_scalar(k, y, LOG2E, MAGIC, ALU.mult, ALU.add))
                    step(dve.tensor_scalar(k, k, MAGIC, -127.0, ALU.subtract, ALU.max))
                    step(dve.tensor_scalar(k, k, 128.0, None, ALU.min))
                    step(dve.scalar_tensor_tensor(r, k, -LN2_HI, y, ALU.mult, ALU.add))
                    step(dve.scalar_tensor_tensor(r, k, -LN2_LO, r, ALU.mult, ALU.add))
                    step(dve.tensor_scalar(q, r, 1.0 / 5040.0, None, ALU.mult))
                    for n in (720.0, 120.0, 24.0, 6.0, 2.0, 1.0):
                        step(dve.scalar_tensor_tensor(q, q, 1.0 / n, r, ALU.add, ALU.mult))
                    step(dve.tensor_scalar(k, k, 127.0, 8388608.0, ALU.add, ALU.mult))
                    step(dve.tensor_copy(ti[:, :], k))
                    step(dve.scalar_tensor_tensor(dt, q, 1.0, ti[:, :].bitcast(f32), ALU.add, ALU.mult))
                    dve.wait_ge(inv_exp, 1)
                    ah, bh, rd = k, r, q
                    b2, a2 = X1[:, 0:HID], X1[:, HID:2 * HID]
                    step(dve.scalar_tensor_tensor(ah, par[:, 1, :], -0.5, dt, ALU.mult, ALU.mult))
                    step(dve.scalar_tensor_tensor(bh, par[:, 2, :], 0.5, dt, ALU.mult, ALU.mult))
                    step(dve.tensor_tensor(b2, bh, bh, ALU.mult))
                    step(dve.tensor_tensor(a2, ah, ah, ALU.mult))
                    step(dve.tensor_tensor(num, a2, b2, ALU.add))
                    step(dve.tensor_scalar(num, num, -1.0, 1.0, ALU.mult, ALU.add))
                    step(dve.tensor_scalar(ah, ah, -1.0, 1.0, ALU.mult, ALU.add))
                    step(dve.tensor_tensor(ah, ah, ah, ALU.mult))
                    step(dve.tensor_tensor(ah, ah, b2, ALU.add))
                    step(dve.reciprocal(rd, ah))
                    step(dve.tensor_tensor(PR[:, 1, :], num, rd, ALU.mult))
                    step(dve.scalar_tensor_tensor(PI[:, 1, :], bh, 2.0, rd, ALU.mult, ALU.mult))
                    for z, v in ((PR, 1.0), (PI, 0.0), (QR, 1.0), (QI, 0.0), (FR, 1.0)):
                        step(dve.memset(z[:, 0, :], v))
                    dve.memset(FI[:, 0, :], 0.0).then_inc(base_ready, 1)
                    dve.wait_ge(base_ready, 1)

                    for n in range(len(PRODUCTS)):
                        if n:
                            dve.wait_ge(prod_im, n)
                        aR, aI, bR, bI, oR, _, (x, _) = operands(n)
                        step(dve.tensor_tensor(x, aI, bI, ALU.mult))
                        step(dve.tensor_tensor(oR, aR, bR, ALU.mult))
                        dve.tensor_tensor(oR, oR, x, ALU.subtract).then_inc(prod_re, 1)
                        dve.wait_ge(prod_re, n + 1)
                    dve.wait_ge(prod_im, len(PRODUCTS))
                    p1, p2, qr, qi = flat(P1[:, :, :]), flat(P2[:, :, :]), flat(QR[:, 0:FINE, :]), flat(QI[:, 0:FINE, :])
                    step(dve.tensor_scalar(p1, qr, cols[:, TOP:TOP + 1], None, ALU.mult))
                    step(dve.scalar_tensor_tensor(p1, qi, cols[:, BOT:BOT + 1], p1, ALU.mult, ALU.add))
                    step(dve.tensor_scalar(p2, qr, cols[:, BOT:BOT + 1], None, ALU.mult))
                    step(dve.scalar_tensor_tensor(p2, qi, cols[:, NTOP:NTOP + 1], p2, ALU.mult, ALU.add))
                    step(dve.tensor_scalar(flat(E1[:, :, :]), flat(E1[:, :, :]), cols[:, SIGN:SIGN + 1], 2.0,
                                           ALU.mult, ALU.mult))
                    dve.tensor_scalar(flat(E2[:, :, :]), flat(E2[:, :, :]), -2.0, None, ALU.mult) \
                        .then_inc(powers_done, 1)
                    dve.wait_ge(powers_done, 1)

                    def chunk(c, ring, first):
                        if not first:
                            dve.wait_ge(k_full, c - 1)
                        v, g = v_of(ring), g_of(ring)
                        dve.tensor_tensor(as_v(v), coarse(P1, c), fine(PR, c), ALU.mult).then_inc(v_done, 1)
                        dve.wait_ge(c_in[ring], (c - ring) * 24 + 48)
                        dve.tensor_tensor(as_g(g), chan(0, ring), ahead(E1, c), ALU.mult).then_inc(v_done, 1)
                        dve.wait_ge(v_pool, c + 1)
                        dve.wait_ge(v_done, c * 3 + 1)
                        dve.tensor_tensor(v, v, X1[:, :], ALU.add).then_inc(v_done, 1)
                        dve.wait_ge(g_pool, c + 1)
                        dve.wait_ge(v_done, c * 3 + 2)
                        dve.tensor_tensor(g, g, X2[:, :], ALU.add).then_inc(g_done, 1)

                    for ring in range(2):
                        chunk(ring, ring, True)
                    with dve.Fori(1, NCH // 2) as turn:
                        for ring in range(2):
                            chunk(turn * 2 + ring, ring, False)

                    den, kk = FR[:, 0, :], FI[:, 0, :]
                    step(dve.tensor_scalar(den, frq[:, 0, :], scal[:, C_FREQ:C_FREQ + 1], None, ALU.mult))
                    step(dve.reciprocal(den, den))
                    for i in range(NT):
                        ang = pe_tab[:, i, :]
                        step(dve.tensor_scalar(ang, den, cols[:, POS + i:POS + i + 1], None, ALU.mult))
                        step(dve.tensor_tensor(kk, ang, frq[:, 1, :], ALU.add))
                        step(dve.tensor_scalar(kk, kk, 1.0 / (2.0 * math.pi), MAGIC, ALU.mult, ALU.add))
                        step(dve.tensor_scalar(kk, kk, MAGIC, None, ALU.subtract))
                        step(dve.scalar_tensor_tensor(ang, kk, -TWO_PI_HI, ang, ALU.mult, ALU.add))
                        step(dve.scalar_tensor_tensor(ang, kk, -TWO_PI_LO, ang, ALU.mult, ALU.add))
                        step(dve.tensor_tensor(ang, ang, frq[:, 1, :], ALU.add))
                        dve.tensor_scalar(ang, ang, 3.1415925, -3.1415925, ALU.min, ALU.max).then_inc(pe_arg, 1)

                @block.gpsimd
                def _(pool):
                    count = [0]

                    def step(ins):
                        count[0] += 1
                        ins.then_inc(pool_step, 1)
                        pool.wait_ge(pool_step, count[0])

                    pool.wait_ge(root_in, 1)
                    pool.tensor_tensor(t[:, 0, 4:5], t[:, 0, 3:4], minus_half[:, 0:1], ALU.pow).then_inc(root_done, 1)
                    for n, (src, hi, lo) in enumerate(pieces):
                        if lo is not None:
                            pool.wait_ge(hi_split, n + 1)
                            pool.tensor_tensor(lo, stage[:, 0:src.shape[1]], hi.bitcast(f32), ALU.subtract) \
                                .then_inc(lo_split, 1)
                    pool.wait_ge(base_ready, 1)
                    for n in range(len(PRODUCTS)):
                        if n:
                            pool.wait_ge(prod_re, n)
                        aR, aI, bR, bI, _, oI, (_, x) = operands(n)
                        step(pool.tensor_tensor(x, aI, bR, ALU.mult))
                        step(pool.tensor_tensor(oI, aR, bI, ALU.mult))
                        pool.tensor_tensor(oI, oI, x, ALU.add).then_inc(prod_im, 1)
                        pool.wait_ge(prod_im, n + 1)
                    pool.wait_ge(powers_done, 1)

                    def chunk(c, ring, first):
                        if not first:
                            pool.wait_ge(v_done, c * 3)
                        pool.tensor_tensor(as_v(X1[:, :]), coarse(P2, c), fine(PI, c), ALU.mult).then_inc(v_pool, 1)
                        pool.wait_ge(c_in[ring], (c - ring) * 24 + 48)
                        if not first:
                            pool.wait_ge(g_done, c)
                        pool.tensor_tensor(as_g(X2[:, :]), chan(1, ring), ahead(E2, c), ALU.mult).then_inc(g_pool, 1)

                    chunk(0, 0, True)
                    chunk(1, 1, False)
                    with pool.Fori(1, NCH // 2) as turn:
                        for ring in range(2):
                            chunk(turn * 2 + ring, ring, False)

                @block.tensor
                def _(pe):
                    def chunk(c, ring, first):
                        pe.wait_ge(v_done, c * 3 + 3)
                        pe.wait_ge(g_done, c + 1)
                        if not first:
                            pe.wait_ge(k_copied, c - 1)
                        v = v_of(ring).rearrange("p (h b) -> p h b", h=CH)
                        g = g_of(ring).rearrange("p (h a) -> p h a", h=CH)
                        for hh in range(CH):
                            half, m = hh % 2, hh // 2
                            mm = pe.matmul(kps[64 * half:64 * half + 64, ring, m * POWERS:(m + 1) * POWERS],
                                           g[:, hh, :], v[:, hh, :], start=True, stop=True)
                        mm.then_inc(k_full, 1)

                    for ring in range(2):
                        chunk(ring, ring, True)
                    with pe.Fori(1, NCH // 2) as turn:
                        for ring in range(2):
                            chunk(turn * 2 + ring, ring, False)

        QK = sb("QK", [P, PAIRS, 2, TOK], f32r)
        Qs, Ks = QK[:, :, 0, :], QK[:, :, 1, :]
        NP = 4
        probs = sb("probs", [P, NP, 2, TOK])
        gates = sb("gates", [P, 2, 2, TOK])
        x_in = sb("x_in", [P, NT, D])
        hb = sb("hb", [P, NT, D])
        xn = sb("xn", [P, NT, D])
        xa = sb("xa", [P, NT, D])
        xab = sb("xab", [P, NT, D])
        h2 = sb("h2", [P, NT, D])
        xT = sb("xT_h", [P, KT, TOK], f32r), sb("xT_l", [P, KT, TOK], f32r)
        hT = sb("hT_h", [P, KT, TOK], f32r), sb("hT_l", [P, KT, TOK], f32r)
        qk = [(sb(f"qk_h{m}", [P, 2, TOK], f32r), sb(f"qk_l{m}", [P, 2, TOK], f32r)) for m in range(KT)]
        v_aug = sb("v_aug", [P, NT, HEADS, 32])
        o_t = sb("o_t", [P, TOK])
        g_act, g_mul = sb("g_act", [P, 2, TOK]), sb("g_mul", [P, 2, TOK])
        act_h, act_l = sb("act_h", [P, 3, TOK], f32r), sb("act_l", [P, 3, TOK], f32r)
        stats, mv = sb("stats", [P, NT, 6]), sb("mv", [P, NT, 2])
        wait_carrier = sb("wait_carrier", [P, 1])
        eps_ln, eps_attn = sb("eps_ln", [P, NT]), sb("eps_attn", [P, NT])
        veps, rstd = sb("veps", [P, NT]), sb("rstd", [P, NT])
        m_neg = sb("m_neg", [P, NT, 2, PAIRS])
        o_rec = sb("o_rec", [P, NT * 4])
        l_max, l_sum = sb("l_max", [P, NT]), sb("l_sum", [P, NT])
        l_exp, gate = sb("l_exp", [P, NT, EXPERTS]), sb("gate", [P, NT, EXPERTS])
        pr, rest = sb("pr", [P, NT, EXPERTS + 8]), sb("rest", [P, NT, EXPERTS + 8])
        top8, found = sb("top8", [P, NT, 8]), sb("found", [P, NT, 8])
        max_h, max_l = probs[0:HEADS, 2, 0, :].bitcast(f32r), probs[0:HEADS, 3, 0, :].bitcast(f32r)
        gate_t = probs[0:EXPERTS, 1, 0, :]

        ring = ps("ring", [P, 2, 2 * BANK])
        av_ps = ps("av_ps", [P, BANK])
        up_ps = ps("up_ps", [P, BANK])
        acc = ps("acc", [P, 2 * BANK])

        slot_full, slot_drained = [sem("slot_full0"), sem("slot_full1")], [sem("slot_drained0"), sem("slot_drained1")]
        x_loaded, x_ready, xab_ready, hb_ready = (sem(n) for n in ("x_loaded", "x_ready", "xab_ready", "hb_ready"))
        stats_done, mv_done, veps_done, rstd_done = (
            [sem(n + "_in"), sem(n + "_out")] for n in ("stats_done", "mv_done", "veps_done", "rstd_done"))
        centred, h2_normal = sem("centred"), sem("h2_normal")
        max_stored = sem("max_stored")
        av_done, ot_copied, rec_done = sem("av_done"), sem("ot_copied"), sem("rec_done")
        y_centred, h2_ready, route, gate_ready = sem("y_centred"), sem("h2_ready"), sem("route"), sem("gate_ready")
        gate_stored, gates_in, stored = sem("gate_stored"), [sem("gates_in0"), sem("gates_in1")], sem("stored")
        up_full, gelu_done, mul_done, hi_done, lo_done, down_done = (sem(n) for n in (
            "up_full", "gelu_done", "mul_done", "hi_done", "lo_done", "down_done"))
        acc_free, vinit, lmax_done = sem("acc_free"), sem("vinit"), sem("lmax_done")
        ROUTE = 6

        def psum(tag):
            return ring[:, slot(tag), :]

        def full(eng, tag, it):
            eng.wait_ge(slot_full[slot(tag)], full_at(tag, it))

        def drained(eng, tag, it):
            eng.wait_ge(slot_drained[slot(tag)], drained_at(tag, it))

        def half(eng, tag, it):
            eng.wait_ge(slot_drained[slot(tag)], half_at(tag, it))

        def is_first(b, n=0, upto=1):
            return isinstance(b, int) and b == 0 and n < upto

        def wait_apart(dve, of, value):
            dve.wait_ge(of, value)
            dve.memset(wait_carrier[:, :], 0.0)

        def each_batch(eng, run):
            run(BEFORE, -1)
            run(FIRST, 0)
            with eng.Fori(1, BATCH - 1) as it:
                run(PLAN, it)
            run(LAST, BATCH - 1)
            run(AFTER, BATCH)

        with nc.Block() as block:
            @block.sync
            def _(sp):
                def load_x(b):
                    image = tok_dram[b] if isinstance(b, int) else \
                        tok_dram[bass.ds(b, 1), :, :].rearrange("o c l -> (o c) l")
                    text = txt[b:b + 1] if isinstance(b, int) else txt[bass.ds(b, 1), :, :]
                    sp.dma_start(x_in[:, 0:2, :], image.rearrange("(i p) d -> p i d", p=P)).then_inc(x_loaded, 16)
                    sp.dma_start(x_in[:, 2:3, :], text.rearrange("o p d -> p o d")).then_inc(x_loaded, 16)

                def load_gates(c):
                    sp.dma_start(gates[:, c % 2], gate_dram[2 * c:2 * c + 2, :].partition_broadcast(P)) \
                        .then_inc(gates_in[c % 2], 16)

                def run(plan, it):
                    if plan is BEFORE:
                        load_x(0)
                    f = it - 1
                    if plan in (FIRST, PLAN):
                        sp.wait_ge(hb_ready, it + 1)
                        sp.wait_ge(x_ready, it + 1)
                        load_x(it + 1)
                    for what, n in plan:
                        if what in ("f", "F") and n % 2 == 0 and 4 <= n < NEXP - 2:
                            b = f if what == "f" else it
                            sp.wait_ge(hi_done, b * NEXP + n)
                            sp.wait_ge(lo_done, b * NEXP + n)
                            load_gates(n // 2)
                        elif what == "fend":
                            sp.wait_ge(acc_free, f + 2)
                            dst = out[f:f + 1] if isinstance(f, int) else out[bass.ds(f, 1), :, :]
                            sp.dma_start(dst.rearrange("o (i p) d -> p (o i) d", p=P), h2[:, :, :]) \
                                .then_inc(stored, 16)
                        elif what == "mT":
                            drained(sp, "mT", it)
                            for half_n, src in enumerate((max_h, max_l)):
                                for e in range(2):
                                    row = 64 * e + MROW + half_n
                                    sp.dma_start(Qs[row:row + 1, :, :].bitcast(f32),
                                                 src[8 * e:8 * e + 8, :].bitcast(f32)).then_inc(max_stored, 16)
                        elif what == "gT":
                            drained(sp, "gT", it)
                            sp.dma_start(gate_dram[:, :], gate_t).then_inc(gate_stored, 16)
                            if plan is not FIRST:
                                sp.wait_ge(hi_done, it * NEXP)
                                sp.wait_ge(lo_done, it * NEXP)
                            sp.wait_ge(gate_stored, it * 16 + 16)
                            load_gates(0)
                            load_gates(1)

                each_batch(sp, run)
                sp.wait_ge(stored, BATCH * 16)

            @block.scalar
            def _(act):
                def gelu(n, b):
                    act.wait_ge(up_full, b * NEXP + (n + 1))
                    if not is_first(b, n, 2):
                        act.wait_ge(hi_done, b * NEXP + (n - 1))
                        act.wait_ge(lo_done, b * NEXP + (n - 1))
                    act.activation(g_act[:, n % 2, :], up_ps[:, 0:TOK], ACT.Gelu).then_inc(gelu_done, 1)

                def high(tag, it, to):
                    full(act, tag, it)
                    act.activation(to, psum(tag).rearrange("p (k n) -> p k n", k=KT)[:, :, 0:TOK], ACT.Copy) \
                        .then_inc(slot_drained[slot(tag)], 1)

                def exps(r, it):
                    full(act, f"st{r}", it)
                    if r >= NP:
                        act.wait_ge(av_done, it * STEPS + ((r - NP) // 2 + 1))
                    act.activation(probs[:, r % NP], psum(f"st{r}").rearrange("p (e n) -> p e n", e=2)[:, :, 0:TOK],
                                   ACT.Exp).then_inc(slot_drained[slot(f"st{r}")], 2)

                def run(plan, it):
                    for what, n in plan:
                        if what == "f":
                            gelu(n, it - 1)
                        elif what == "F":
                            gelu(n, it)
                        elif what == "xT":
                            high("xT", it, xT[0][:, :, :])
                        elif what in ("q", "k"):
                            full(act, f"{what}{n}", it)
                            m = ("q", "k").index(what)
                            act.activation(qk[n][0][:, m, :], psum(f"{what}{n}")[:, 0:TOK], ACT.Identity,
                                           bias=qkb[:, n, m:m + 1]).then_inc(slot_drained[slot(f"{what}{n}")], 1)
                        elif what == "sel":
                            full(act, f"sel{n}", it)
                            act.activation(QK[:, n], psum(f"sel{n}").rearrange("p (m n) -> p m n", m=2)[:, :, 0:TOK],
                                           ACT.Identity, bias=cols[:, ONES_ROW:ONES_ROW + 1]) \
                                .then_inc(slot_drained[slot(f"sel{n}")], 2)
                        elif what == "mT":
                            full(act, "mT", it)
                            act.activation(max_h, psum("mT")[0:HEADS, 0:TOK], ACT.Copy) \
                                .then_inc(slot_drained[slot("mT")], 1)
                        elif what == "st":
                            exps(n, it)
                        elif what == "oT":
                            high("oT", it, xT[0][:, :, :])
                        elif what == "hT":
                            high("hT", it, hT[0][:, :, :])
                        elif what == "logit":
                            act.wait_ge(lmax_done, it + 1)
                            for i in range(NT):
                                ins = act.activation(l_exp[:, i, :], psum("logit")[:, i * EXPERTS:(i + 1) * EXPERTS],
                                                     ACT.Exp, bias=l_max[:, i:i + 1])
                            ins.then_inc(slot_drained[slot("logit")], 2)

                each_batch(act, run)

            @block.vector
            def _(dve):
                def wait_gates(n, b):
                    c = (n - SHARED) // 2
                    dve.wait_ge(gates_in[c % 2], b * (4 * EXPERTS) + 16 * (c // 2 + 1))

                def expert(n, b):
                    to, a = act_h[:, n % 3, :], g_act[:, n % 2, :]
                    dve.wait_ge(gelu_done, b * NEXP + (n + 1))
                    if n >= 3:
                        dve.wait_ge(down_done, b * NEXP + (n - 2))
                    if n < SHARED:
                        dve.tensor_copy(to, a).then_inc(hi_done, 1)
                    else:
                        wait_gates(n, b)
                        q = n - SHARED
                        dve.tensor_tensor(to, a, gates[:, (q // 2) % 2, q % 2, :], ALU.mult).then_inc(hi_done, 1)

                def low(tag, it, high, to):
                    half(dve, tag, it)
                    dve.tensor_tensor(to, psum(tag).rearrange("p (k n) -> p k n", k=KT)[:, :, 0:TOK],
                                      high.bitcast(f32), ALU.subtract).then_inc(slot_drained[slot(tag)], 1)

                def moments(src, kind, at):
                    for i in range(NT):
                        ins = dve.bn_stats(stats[:, i, :], src[:, i, :])
                    ins.then_inc(stats_done[kind], 1)
                    wait_apart(dve, stats_done[kind], at)
                    for i in range(NT):
                        ins = dve.bn_aggr(mv[:, i, :], stats[:, i, :])
                    ins.then_inc(mv_done[kind], 1)
                    dve.wait_ge(mv_done[kind], at)

                def copy_heads(g, it):
                    dve.wait_ge(av_done, it * STEPS + NT * (g + 1))
                    if g:
                        full(dve, f"o{g - 1}", it)
                    dve.tensor_copy(o_t[:, :], av_ps[:, 0:TOK]).then_inc(ot_copied, 1)

                def divide(g, it):
                    full(dve, f"o{g}", it)
                    heads = psum(f"o{g}")[:, 0:NT * P].rearrange("p (i j c) -> p i j c", i=NT, j=4)
                    rec = o_rec[:, :].rearrange("p (i j) -> p i j", i=NT)
                    dve.reciprocal(rec, heads[:, :, :, DK]).then_inc(rec_done, 1)
                    dve.wait_ge(rec_done, it * 4 + (g + 1))
                    for i in range(NT):
                        ins = dve.tensor_tensor(
                            xa[:, i, 64 * g:64 * g + 64].rearrange("p (j d) -> p j d", j=4),
                            heads[:, i, :, 0:DK], rec[:, i, :].unsqueeze(2).to_broadcast([P, 4, DK]), ALU.mult)
                    ins.then_inc(slot_drained[slot(f"o{g}")], 2)

                def choose(it):
                    nth = [0]

                    def step(ins, apart=False):
                        nth[0] += 1
                        ins.then_inc(route, 1)
                        if apart:
                            wait_apart(dve, route, it * ROUTE + nth[0])
                        else:
                            dve.wait_ge(route, it * ROUTE + nth[0])

                    drained(dve, "logit", it)
                    step(dve.tensor_reduce(l_sum[:, :], l_exp[:, :, :], AX.X, ALU.add))
                    step(dve.reciprocal(l_sum[:, :], l_sum[:, :]))
                    step(dve.tensor_tensor(pr[:, :, 0:EXPERTS], l_exp[:, :, :],
                                           l_sum[:, :].unsqueeze(2).to_broadcast([P, NT, EXPERTS]), ALU.mult), True)
                    for i in range(NT):
                        ins = dve.max(top8[:, i, :], pr[:, i, :])
                    step(ins)
                    step(dve.tensor_copy(found[:, :, 0:TOPK], top8[:, :, 0:TOPK]), True)
                    for i in range(NT):
                        ins = dve.match_replace(rest[:, i, :], found[:, i, :], pr[:, i, :], 0.0)
                    step(ins)
                    dve.tensor_tensor(gate[:, :, :], pr[:, :, 0:EXPERTS], rest[:, :, 0:EXPERTS], ALU.subtract) \
                        .then_inc(gate_ready, 1)

                def run(plan, it):
                    for what, n in plan:
                        if what == "f":
                            expert(n, it - 1)
                        elif what == "F":
                            expert(n, it)
                        elif what == "ln1":
                            dve.wait_ge(x_loaded, it * 32 + 64)
                            if plan is not BEFORE:
                                dve.wait_ge(xab_ready, it + 1)
                            moments(x_in, 0, it + 2)
                            for i in range(NT):
                                ins = dve.tensor_scalar(xn[:, i, :], x_in[:, i, :], mv[:, i, 0:1], None, ALU.subtract)
                            ins.then_inc(centred, 1)
                            dve.wait_ge(centred, it + 2)
                            dve.wait_ge(rstd_done[0], it + 2)
                            for i in range(NT):
                                ins = dve.scalar_tensor_tensor(xn[:, i, :], xn[:, i, :], rstd[:, i:i + 1],
                                                               pe_tab[:, i, :], ALU.mult, ALU.add)
                            ins.then_inc(x_ready, 1)
                        elif what == "xT":
                            low("xT", it, xT[0][:, :, :], xT[1][:, :, :])
                        elif what in ("q", "k"):
                            half(dve, f"{what}{n}", it)
                            m = ("q", "k").index(what)
                            dve.scalar_tensor_tensor(qk[n][1][:, m, :], psum(f"{what}{n}")[:, 0:TOK],
                                                     qkb[:, n, m:m + 1], qk[n][0][:, m, :].bitcast(f32),
                                                     ALU.add, ALU.subtract) \
                                .then_inc(slot_drained[slot(f"{what}{n}")], 1)
                        elif what == "v" and n == NT - 1:
                            full(dve, "v", it)
                            for i in range(NT):
                                ins = dve.tensor_tensor(v_aug[:, i, :, 0:DK],
                                                        psum("v")[:, i * D:(i + 1) * D].rearrange("p (h d) -> p h d", h=HEADS),
                                                        row_b[:, 0, :].rearrange("p (h d) -> p h d", h=HEADS), ALU.add)
                            ins.then_inc(slot_drained[slot("v")], 2)
                        elif what == "s":
                            full(dve, f"s{n}", it)
                            dve.tensor_reduce(m_neg[:, n % NT, :, n // NT],
                                              psum(f"s{n}").rearrange("p (e n) -> p e n", e=2)[:, :, 0:TOK],
                                              AX.X, ALU.max, negate=True).then_inc(slot_drained[slot(f"s{n}")], 2)
                        elif what == "fend":
                            dve.wait_ge(down_done, it * NEXP)
                            flat2 = h2[:, :, :].rearrange("p i d -> p (i d)")
                            dve.tensor_tensor(flat2, acc[:, 0:NT * D], flat2, ALU.add).then_inc(acc_free, 1)
                        elif what == "mT":
                            half(dve, "mT", it)
                            dve.tensor_tensor(max_l, psum("mT")[0:HEADS, 0:TOK], max_h.bitcast(f32), ALU.subtract) \
                                .then_inc(slot_drained[slot("mT")], 1)
                        elif what == "av" and n % NT == NT - 1:
                            copy_heads(n // NT, it)
                        elif what == "o":
                            divide(n, it)
                        elif what == "oT":
                            low("oT", it, xT[0][:, :, :], xT[1][:, :, :])
                        elif what == "wo":
                            full(dve, "wo", it)
                            dve.wait_ge(xab_ready, it + 1)
                            wide = xab[:, :, :].rearrange("p i d -> p (i d)")
                            dve.tensor_tensor(wide, psum("wo")[:, 0:NT * D], wide, ALU.add) \
                                .then_inc(slot_drained[slot("wo")], 2)
                            drained(dve, "wo", it)
                        elif what == "ln_mean":
                            moments(xab, 1, it * 2 + 1)
                        elif what == "ln_h2":
                            for i in range(NT):
                                ins = dve.scalar_tensor_tensor(xa[:, i, :], xab[:, i, :], mv[:, i, 0:1],
                                                               row_b[:, 2, :], ALU.subtract, ALU.mult)
                            ins.then_inc(y_centred, 1)
                            dve.wait_ge(y_centred, it + 1)
                            dve.wait_ge(rstd_done[1], it * 2 + 1)
                            dve.wait_ge(hb_ready, it + 1)
                            if plan is not FIRST:
                                dve.wait_ge(stored, it * 16)
                            for i in range(NT):
                                ins = dve.scalar_tensor_tensor(h2[:, i, :], xa[:, i, :], rstd[:, i:i + 1],
                                                               hb[:, i, :], ALU.mult, ALU.add)
                            ins.then_inc(h2_ready, 1)
                            dve.wait_ge(h2_ready, it + 1)
                            moments(h2, 1, it * 2 + 2)
                        elif what == "ln_out":
                            dve.wait_ge(rstd_done[1], it * 2 + 2)
                            for i in range(NT):
                                ins = dve.tensor_scalar(xa[:, i, :], h2[:, i, :], mv[:, i, 0:1], rstd[:, i:i + 1],
                                                        ALU.subtract, ALU.mult)
                            ins.then_inc(h2_normal, 1)
                        elif what == "hT":
                            low("hT", it, hT[0][:, :, :], hT[1][:, :, :])
                        elif what == "logit":
                            full(dve, "logit", it)
                            dve.tensor_reduce(l_max[:, :],
                                              psum("logit")[:, 0:NT * EXPERTS].rearrange("p (i x) -> p i x", i=NT),
                                              AX.X, ALU.max, negate=True).then_inc(lmax_done, 1)
                        elif what == "choose":
                            choose(it)
                        elif what == "gT":
                            full(dve, "gT", it)
                            dve.tensor_copy(gate_t, psum("gT")[0:EXPERTS, 0:TOK]).then_inc(slot_drained[slot("gT")], 2)

                dve.memset(v_aug[:, :, :, :], 0.0).then_inc(vinit, 1)
                dve.memset(pr[:, :, :], -1.0).then_inc(vinit, 1)
                dve.memset(found[:, :, :], -1.0).then_inc(vinit, 1)
                dve.memset(eps_ln[:, :], LN_EPS).then_inc(vinit, 1)
                dve.tensor_copy(eps_attn[:, :], scal[:, C_EPS:C_EPS + 1].to_broadcast([P, NT])).then_inc(vinit, 1)
                dve.wait_ge(vinit, 5)
                dve.memset(v_aug[:, :, :, DK:DK + 1], 1.0).then_inc(vinit, 1)
                dve.wait_ge(vinit, 6)
                dve.memset(wait_carrier[:, :], 0.0).then_inc(acc_free, 1)
                each_batch(dve, run)

            @block.gpsimd
            def _(pool):
                def root(kind, at, eps):
                    pool.wait_ge(mv_done[kind], at)
                    pool.tensor_tensor(veps[:, :], mv[:, :, 1], eps[:, :], ALU.add).then_inc(veps_done[kind], 1)
                    pool.wait_ge(veps_done[kind], at)
                    pool.tensor_tensor(rstd[:, :], veps[:, :], minus_half[:, :], ALU.pow).then_inc(rstd_done[kind], 1)

                def low(n, b):
                    g, at = g_act[:, n % 2, :], b * NEXP + (n + 1)
                    pool.wait_ge(gelu_done, at)
                    if n >= SHARED:
                        q = n - SHARED
                        c = q // 2
                        pool.wait_ge(gates_in[c % 2], b * (4 * EXPERTS) + 16 * (c // 2 + 1))
                        pool.tensor_tensor(g_mul[:, n % 2, :], g, gates[:, c % 2, q % 2, :], ALU.mult) \
                            .then_inc(mul_done, 1)
                        pool.wait_ge(mul_done, b * EXPERTS + (q + 1))
                        g = g_mul[:, n % 2, :]
                    pool.wait_ge(hi_done, at)
                    pool.tensor_tensor(act_l[:, n % 3, :], g, act_h[:, n % 3, :].bitcast(f32), ALU.subtract) \
                        .then_inc(lo_done, 1)

                def residual(b):
                    pool.wait_ge(x_ready, b + 1)
                    pool.tensor_tensor(xab[:, :, :], xn[:, :, :], row_b[:, 1:2, :].to_broadcast([P, NT, D]),
                                       ALU.add).then_inc(xab_ready, 1)

                def tokens_beta(b):
                    pool.tensor_tensor(hb[:, :, :], x_in[:, :, :], row_b[:, 3:4, :].to_broadcast([P, NT, D]),
                                       ALU.add).then_inc(hb_ready, 1)

                def run(plan, it):
                    for what, n in plan:
                        if what == "f":
                            low(n, it - 1)
                        elif what == "F":
                            low(n, it)
                        elif what == "ln1":
                            root(0, it + 2, eps_ln)
                            if plan is BEFORE:
                                residual(0)
                                tokens_beta(0)
                        elif what == "ln_mean":
                            root(1, it * 2 + 1, eps_attn)
                        elif what == "ln_h2":
                            root(1, it * 2 + 2, eps_ln)
                            if plan is not LAST:
                                pool.wait_ge(h2_ready, it + 1)
                                residual(it + 1)
                                tokens_beta(it + 1)

                pool.wait_ge(vinit, 6)
                each_batch(pool, run)

            @block.tensor
            def _(pe):
                def free(tag, it):
                    if not (isinstance(it, int) and before_at(tag, it) == 0):
                        pe.wait_ge(slot_drained[slot(tag)], before_at(tag, it))

                def done(ins, tag):
                    ins.then_inc(slot_full[slot(tag)], 1)

                def mm3(to, a, w, first=True, last=True, **more):
                    pe.matmul(to, a[0], w[0], start=first, stop=False, **more)
                    pe.matmul(to, a[0], w[1], start=False, stop=False, **more)
                    return pe.matmul(to, a[1], w[0], start=False, stop=last, **more)

                def turn(tag, src):
                    for i in range(NT):
                        for kt in range(KT):
                            ins = pe.transpose(psum(tag)[:, kt * BANK + i * P:kt * BANK + (i + 1) * P],
                                               src[:, i, kt * P:(kt + 1) * P], ident[:, :])
                    done(ins, tag)

                def by_rows(tag, xt, w, n, tiles=range(NT)):
                    for i in tiles:
                        for kt in range(KT):
                            ins = mm3(psum(tag)[:, i * n:(i + 1) * n], [x[:, kt, i * P:(i + 1) * P] for x in xt],
                                      [z[:, kt, :] for z in w], kt == 0, kt == KT - 1)
                    if NT - 1 in tiles:
                        done(ins, tag)

                def expert_up(n, b):
                    if not is_first(b, n, 1):
                        pe.wait_ge(gelu_done, b * NEXP + n)
                    for kt in range(KT):
                        ins = mm3(up_ps[:, 0:TOK], (up_h[:, kt, n, :], up_l[:, kt, n, :]),
                                  [x[:, kt, :] for x in hT], kt == 0, kt == KT - 1)
                    ins.then_inc(up_full, 1)

                def expert_down(n, b):
                    pe.wait_ge(hi_done, b * NEXP + (n + 1))
                    pe.wait_ge(lo_done, b * NEXP + (n + 1))
                    if n == 0:
                        pe.wait_ge(acc_free, b + 1)
                    for i in range(NT):
                        ins = mm3(acc[:, i * D:(i + 1) * D],
                                  [x[:, n % 3, i * P:(i + 1) * P] for x in (act_h, act_l)],
                                  (dn_h[:, n, :], dn_l[:, n, :]), n == 0 and i != 1, n == NEXP - 1,
                                  skip_group_check=True)
                    ins.then_inc(down_done, 1)

                def project(what, m, it):
                    tag = f"{what}{m}"
                    free(tag, it)
                    if tag == "q0":
                        drained(pe, "xT", it)
                    w = wq if what == "q" else wk
                    for kt in range(KT):
                        ins = mm3(psum(tag)[:, 0:TOK], [z[:, kt, m * P:(m + 1) * P] for z in w],
                                  [x[:, kt, :] for x in xT], kt == 0, kt == KT - 1)
                    done(ins, tag)

                def stack(p, it):
                    m, at = p // 4, 32 * (p % 4)
                    free(f"sel{p}", it)
                    others = [tag for tag in (f"q{m}", f"k{m}") if slot(tag) != slot(f"sel{p}")]
                    if p % 4 == 0 and others:
                        drained(pe, others[-1], it)
                    for n, kinds in enumerate(((SEL_QH, SEL_QL), (SEL_KH, SEL_KL))):
                        for part, kind in enumerate(kinds):
                            ins = pe.matmul(psum(f"sel{p}")[:, n * BANK:n * BANK + TOK], sel[at:at + 32, kind, :],
                                            qk[m][part][at:at + 32, n, :], start=part == 0, stop=part == 1)
                    done(ins, f"sel{p}")

                def logits(r, it):
                    p, i = r // NT, r % NT
                    free(f"s{r}", it)
                    if i == 0:
                        drained(pe, f"sel{p}", it)
                    for e in range(2):
                        rows_e = slice(64 * e, 64 * e + MROW)
                        ins = pe.matmul(psum(f"s{r}")[:, e * BANK:e * BANK + TOK], Qs[rows_e, p, i * P:(i + 1) * P],
                                        Ks[rows_e, p, :], start=True, stop=True)
                    done(ins, f"s{r}")

                def logits_t(r, it):
                    k = r // 2
                    p, i = 2 * (k // NT) + r % 2, k % NT
                    free(f"st{r}", it)
                    for e in range(2):
                        rows_e = slice(64 * e, 64 * e + 64)
                        ins = pe.matmul(psum(f"st{r}")[:, e * BANK:e * BANK + TOK], Ks[rows_e, p, i * P:(i + 1) * P],
                                        Qs[rows_e, p, :], start=True, stop=True)
                    done(ins, f"st{r}")

                def weigh(k, it):
                    g, i = k // NT, k % NT
                    drained(pe, f"st{2 * k}", it)
                    drained(pe, f"st{2 * k + 1}", it)
                    if i == 0 and g:
                        pe.wait_ge(ot_copied, it * 4 + g)
                    for j in range(4):
                        ins = pe.matmul(av_ps[32 * j:32 * j + 32, 0:TOK], v_aug[:, i, 4 * g + j, :],
                                        probs[:, (2 * k + j // 2) % NP, j % 2, :], start=i == 0, stop=i == NT - 1)
                    ins.then_inc(av_done, 1)

                def run(plan, it):
                    for what, n in plan:
                        if what == "f":
                            expert_up(n, it - 1)
                        elif what == "down":
                            expert_down(n, it - 1)
                        elif what == "F":
                            expert_up(n, it)
                        elif what == "Down":
                            expert_down(n, it)
                        elif what == "xT":
                            free("xT", it)
                            pe.wait_ge(x_ready, it + 2)
                            turn("xT", xn)
                        elif what in ("q", "k"):
                            project(what, n, it)
                        elif what == "v":
                            if n == 0:
                                free("v", it)
                            by_rows("v", xT, wv, D, (n,))
                        elif what == "sel":
                            stack(n, it)
                        elif what == "s":
                            logits(n, it)
                        elif what == "mT":
                            free("mT", it)
                            drained(pe, f"s{ROUNDS - 1}", it)
                            drained(pe, f"s{ROUNDS - 2}", it)
                            for i in range(NT):
                                ins = pe.transpose(psum("mT")[0:HEADS, i * P:(i + 1) * P],
                                                   m_neg[:, i].rearrange("p e q -> p (e q)"), ident[:, :])
                            done(ins, "mT")
                        elif what == "st":
                            if n == 0:
                                pe.wait_ge(max_stored, it * 64 + 64)
                            logits_t(n, it)
                        elif what == "o":
                            free(f"o{n}", it)
                            pe.wait_ge(ot_copied, it * 4 + (n + 1))
                            for i in range(NT):
                                ins = pe.transpose(psum(f"o{n}")[:, i * P:(i + 1) * P], o_t[:, i * P:(i + 1) * P],
                                                   ident[:, :])
                            done(ins, f"o{n}")
                        elif what == "av":
                            weigh(n, it)
                        elif what == "oT":
                            free("oT", it)
                            drained(pe, "o3", it)
                            turn("oT", xa)
                        elif what == "wo":
                            free("wo", it)
                            drained(pe, "oT", it)
                            by_rows("wo", xT, wo, D)
                        elif what == "hT":
                            free("hT", it)
                            pe.wait_ge(h2_normal, it + 1)
                            turn("hT", xa)
                        elif what == "logit":
                            free("logit", it)
                            drained(pe, "hT", it)
                            by_rows("logit", hT, rw, EXPERTS)
                        elif what == "gT":
                            free("gT", it)
                            pe.wait_ge(gate_ready, it + 1)
                            for i in range(NT):
                                ins = pe.transpose(psum("gT")[0:EXPERTS, i * P:(i + 1) * P], gate[:, i, :],
                                                   ident[:, :])
                            done(ins, "gT")

                each_batch(pe, run)


def _constants():
    p = np.arange(P)
    sel = np.zeros((P, 4, P), np.float32)
    for kind, reps in ((SEL_QH, (0, 1)), (SEL_QL, (2,)), (SEL_KH, (0, 2)), (SEL_KL, (1,))):
        for k in range(P):
            for r in reps:
                sel[k, kind, 64 * (k % 32 // 16) + 16 * r + k % 16] = 1.0
    cols = np.zeros((P, NCOLS), np.float32)
    cols[:, TOP], cols[:, BOT] = p < 64, p >= 64
    cols[:, SIGN], cols[:, NTOP] = np.where(p < 64, 1.0, -1.0), -(p < 64).astype(np.float32)
    cols[:, ONES_ROW] = np.isin(p, (MROW, MROW + 1, 64 + MROW, 65 + MROW))
    for i in range(NT):
        cols[:, POS + i] = P * i + p
    even = np.repeat(np.arange(0, D, 2), 2)
    freq = np.stack([10000.0 ** (2.0 * even / D), np.where(np.arange(D) % 2, math.pi / 2, 0.0)]).astype(np.float32)
    return {"freq": freq.reshape(-1), "ident_c": np.eye(P, dtype=np.float32), "sel_c": sel.reshape(P, 4 * P),
            "cols_c": cols}


def kernel(x, txt, L0_tok_log_dt, L0_tok_inv_A_real, L0_tok_A_imag, L0_tok_B_ri, L0_attn_rby, L0_attn_Wq, L0_attn_bq,
           L0_attn_Wk, L0_attn_bk, L0_attn_Wv, L0_attn_bv, L0_attn_Wo, L0_attn_bo, L0_attn_ln_gamma,
           L0_attn_ln_beta, L0_ffn_shared_up, L0_ffn_shared_down, L0_ffn_routed_up, L0_ffn_routed_down,
           L0_ffn_router_w):
    import concourse.bacc as bacc
    from concourse.bass_utils import run_bass_kernel_spmd

    def transposed(w):
        w = np.asarray(w)
        return w.T.reshape(w.shape[1] // P, P, w.shape[0]).transpose(1, 0, 2).reshape(P, -1)

    up = np.concatenate([np.asarray(L0_ffn_shared_up), np.asarray(L0_ffn_routed_up)])
    down = np.concatenate([np.asarray(L0_ffn_shared_down), np.asarray(L0_ffn_routed_down)])
    arrays = {
        "cT": np.asarray(x).transpose(3, 2, 1, 0).reshape(2 * NST, HID, BATCH),
        "bT": np.asarray(L0_tok_B_ri).transpose(2, 1, 0).reshape(2 * NST, HID),
        "log_dt": np.asarray(L0_tok_log_dt),
        "inv_a": np.asarray(L0_tok_inv_A_real).T,
        "a_imag": np.asarray(L0_tok_A_imag).T,
        "txt": np.asarray(txt),
        "rby": np.asarray(L0_attn_rby),
        "qk_bias": np.stack([np.asarray(L0_attn_bq).reshape(KT, P), np.asarray(L0_attn_bk).reshape(KT, P)],
                            -1).transpose(1, 0, 2),
        "rows": np.concatenate([np.asarray(v) for v in (L0_attn_bv, L0_attn_bo, L0_attn_ln_gamma, L0_attn_ln_beta)]),
        "w_up": up.transpose(2, 0, 1).reshape(KT, P, NEXP * EDIM).transpose(1, 0, 2).reshape(P, -1),
        "w_down": down.transpose(2, 0, 1).reshape(EDIM, NEXP * D),
        "w_small": np.concatenate([transposed(w) for w in (L0_attn_Wq, L0_attn_Wk, L0_attn_Wv, L0_attn_Wo,
                                                           L0_ffn_router_w)], axis=1),
        **_constants(),
    }
    names = ["cT", "bT", "log_dt", "inv_a", "a_imag", "txt", "rby", "qk_bias", "rows", "freq", "w_up", "w_down",
             "w_small", "ident_c", "sel_c", "cols_c"]
    nc = bacc.Bacc("TRN2", target_bir_lowering=False, num_devices=1)
    feeds, aps = {}, {}
    for name in names:
        a = np.ascontiguousarray(arrays[name])
        feeds[f"in_{name}"] = a
        aps[name] = nc.dram_tensor(f"in_{name}", a.shape, mybir.dt.from_np(a.dtype), kind="ExternalInput").ap()
    out = nc.dram_tensor("out", (BATCH, TOK, D), mybir.dt.float32, kind="ExternalOutput").ap()
    fusion_kernel(nc, **aps, out=out)
    result = run_bass_kernel_spmd(nc, [feeds], core_ids=[0])
    return result.results[0]["out"]
```

```python
import math
from contextlib import ExitStack

import numpy as np

import concourse.bass as bass
from concourse import mybir

P = 128
BATCH, HID, NST, SEQ_L = 16, 256, 64, 256
TXT = 128
D = 256
TOK = HID + TXT
NT = TOK // P
KT = D // P
HEADS, DK = 16, 16
PAIRS = HEADS // 2
EXPERTS, SHARED, TOPK, EDIM = 16, 2, 4, 128
NEXP = EXPERTS + SHARED
AHEAD, POWERS, FINE = 4, 64, 8
CH = 16
NCH = HID // CH
BANK = 512
LN_EPS = 1e-5
PHASE_MOD = 0.1 * math.sin(2.0 * math.pi * 0.25)
EPS_ADAPTIVE = 0.1 * math.sin(2.0 * math.pi * 0.5)
TENSION = abs(1.0 - 1.0)
MAGIC = 1.5 * 2.0 ** 23
LOG2E, LN2_HI, LN2_LO = 1.4426950408889634, 0.693359375, -2.12194440054690581e-4
TWO_PI_HI = 6.28125
TWO_PI_LO = 2.0 * math.pi - TWO_PI_HI
WSMALL = 4 * KT * D + KT * EXPERTS
WPIECE = NEXP * D // 4

C_LOGIT, C_EPS, C_OUT, C_GAMMA, C_FREQ = range(5)
SIGN, ONES_ROW, POS = range(3)
NCOLS = POS + NT

SEL_QH, SEL_QL, SEL_KH, SEL_KL = range(4)
MROW = 48

ROUNDS = PAIRS * NT
STEPS = ROUNDS // 2

FRONT = ("ln1", "xT", "q", "k", "v", "sel", "s", "mT")


def steps(text):
    named = []
    for word in text.split():
        what = word.rstrip("0123456789") if word not in ("ln1", "ln_h2") else word
        named += [(what, int(word[len(what):] or 0))]
    return named


PLAN = steps("""
    down5 f8 down6 f9 st0 down7 ln1 st1 st2 st3 f10 av0 st4 down8 st5 av1 xT0 down9
    av2 xT1 st6 st7 down10 st8 o0 st9 f11 av3 f12 st10 st11 q0 av4 st12 st13 av5
    k0 st14 st15 av6 st16 f13 down11 st17 down12 av7 f14 o1 av8 st18 st19 down13 q1 st20
    av9 st21 st22 o2 down14 st23 k1 av10 av11 sel0 o3 v0 v1 v2 oT f15 sel1 wo
    sel2 f16 ln_mean s0 f17 sel3 ln_h2 down15 sel4 sel5 down16 sel6 sel7 s1 ln_out s2 s3 s4
    hT down17 s5 lT s6 s7 logit s8 fend s9 choose F0 s10 F1 s11 gT s12 Down0
    s13 s14 F2 F3 s15 Down1 s16 F4 s17 Down2 F5 s18 Down3 s19 F6 s20 s21 Down4
    s22 s23 F7 mT
""")
BEFORE = [step for step in PLAN if step[0] in FRONT]
FIRST = [step for step in PLAN if step[0] not in ("f", "down", "fend")]
LAST = [step for step in PLAN if step[0] not in FRONT]
AFTER = [step for step in PLAN if step[0] in ("f", "down", "fend")]


SIDE = ("xT", "q", "k", "o", "logit", "gT")
EXPERT = ("f", "F")


def products(plan):
    tags = []
    for what, n in plan:
        if what in ("st", "o", "xT", "q", "k", "sel", "s"):
            tags += [f"{what}{n}"]
        elif what == "v" and n == NT - 1 or what in ("oT", "wo", "hT", "lT", "logit", "mT", "gT"):
            tags += [what]
    return tags


def at_side(tag):
    return tag.rstrip("0123456789") in SIDE


RING = [tag for tag in products(PLAN) if not at_side(tag)]
assert len(RING) % 2 == 0


def slot(tag):
    return 2 if at_side(tag) else RING.index(tag) % 2


def uses_in(slot_of, tags):
    return sum(slot(tag) == slot_of for tag in tags)


def uses_before(tag, it):
    of = slot(tag)
    if isinstance(it, int) and it < 0:
        before = products(BEFORE)
        return uses_in(of, before[:before.index(tag)])
    order = products(LAST) if isinstance(it, int) and it == BATCH - 1 else products(PLAN)
    start = uses_in(of, products(BEFORE)) + uses_in(of, order[:order.index(tag)])
    return it * uses_in(of, products(PLAN)) + start


def full_at(tag, it):
    return uses_before(tag, it) + 1


def drained_at(tag, it):
    return uses_before(tag, it) * 2 + 2


def half_at(tag, it):
    return uses_before(tag, it) * 2 + 1


def before_at(tag, it):
    return uses_before(tag, it) * 2


def fusion_kernel(nc, cT, bT, log_dt, inv_a, a_imag, txt, rby, qk_bias, rows, freq, w_up, w_down, w_small,
                  ident_c, sel_c, cols_c, out):
    f32, f32r, i32 = mybir.dt.float32, mybir.dt.float32r, mybir.dt.int32
    ALU, ACT, AX = mybir.AluOpType, mybir.ActivationFunctionType, mybir.AxisListType

    ctx = ExitStack()
    with ctx:
        def sb(name, shape, dt=f32, where=ctx):
            return where.enter_context(nc.sbuf_tensor(name, shape, dt))

        def ps(name, shape, where=ctx):
            return where.enter_context(nc.psum_tensor(name, shape, f32))

        def sem(name):
            return ctx.enter_context(nc.semaphore(name))

        tok_dram = nc.dram_tensor("tok_dram", (BATCH, HID, SEQ_L), f32).ap()
        gate_dram = nc.dram_tensor("gate_dram", (EXPERTS, TOK), f32).ap()

        up_h, up_l = sb("up_h", [P, KT, NEXP, EDIM], f32r), sb("up_l", [P, KT, NEXP, EDIM], f32r)
        dn_h, dn_l = sb("dn_h", [P, NEXP, D], f32r), sb("dn_l", [P, NEXP, D], f32r)
        ws_h, ws_l = sb("ws_h", [P, WSMALL], f32r), sb("ws_l", [P, WSMALL], f32r)
        ident = sb("ident", [P, P])
        sel = sb("sel", [P, 4, P], f32r)
        pe_tab = sb("pe_tab", [P, NT, D])
        row_b = sb("row_b", [P, 4, D])
        cols = sb("cols", [P, NCOLS])
        scal = sb("scal", [P, 8])
        qkb = sb("qkb", [P, 2, 2])
        minus_half = sb("minus_half", [P, NT])

        def weight(t, n):
            return t[:, n * KT * D:(n + 1) * KT * D].rearrange("p (k o) -> p k o", k=KT)

        wq, wk, wv, wo = ((weight(ws_h, n), weight(ws_l, n)) for n in range(4))
        rw = tuple(t[:, 4 * KT * D:].rearrange("p (k o) -> p k o", k=KT) for t in (ws_h, ws_l))

        params_in, b_in, rby_in, cst_in = sem("params_in"), sem("b_in"), sem("rby_in"), sem("cst_in")
        stage_in, pool_split, dve_split = [sem("stage_in0"), sem("stage_in1")], sem("pool_split"), sem("dve_split")
        inv_exp, dve_step, base_ready = sem("inv_exp"), sem("dve_step"), sem("base_ready")
        prod_re, prod_im, prod_pool, powers_done = (sem(n) for n in ("prod_re", "prod_im", "prod_pool", "powers_done"))
        p1_ready, p2_ready, sel_in, sel_done = sem("p1_ready"), sem("p2_ready"), sem("sel_in"), sem("sel_done")
        c_in = [sem("c_in0"), sem("c_in1")]
        v_done, g_done, v_pool, g_pool = sem("v_done"), sem("g_done"), sem("v_pool"), sem("g_pool")
        k_full, k_copied, k_stored = sem("k_full"), sem("k_copied"), [sem("k_stored0"), sem("k_stored1")]
        hi_split, small_scaled = sem("hi_split"), sem("small_scaled")
        root_in, root_done, scal_ready, pe_arg = (sem(n) for n in ("root_in", "root_done", "scal_ready", "pe_arg"))

        tok = ExitStack()
        with tok:
            par = sb("par", [P, 5, HID], f32, tok)
            t = sb("t", [P, 6, HID], f32, tok)
            ti = sb("ti", [P, HID], i32, tok)
            frq = sb("frq", [P, 2, D], f32, tok)
            PR, PI = sb("PR", [P, 9, HID], f32, tok), sb("PI", [P, 9, HID], f32, tok)
            QR, QI = sb("QR", [P, 9, HID], f32, tok), sb("QI", [P, 9, HID], f32, tok)
            P1, P2 = sb("P1", [P, FINE, HID], f32, tok), sb("P2", [P, FINE, HID], f32, tok)
            FR, FI = sb("FR", [P, AHEAD, HID], f32, tok), sb("FI", [P, AHEAD, HID], f32, tok)
            E1, E2 = sb("E1", [P, AHEAD, HID], f32, tok), sb("E2", [P, AHEAD, HID], f32, tok)
            X1, X2 = sb("X1", [P, 4 * HID], f32, tok), sb("X2", [P, 4 * HID], f32, tok)
            C = sb("C", [P, 2, 2, CH, BATCH], f32, tok)
            kout = sb("kout", [P, 2, CH // 2, POWERS], f32, tok)
            stage = sb("stage", [P, 2, WPIECE], f32, tok)
            kps = ps("kps", [P, 2, BANK], tok)

            def flat(z):
                return z.rearrange("p i h -> p (i h)")

            def v_of(ring):
                return flat(QR[:, 4 * ring:4 * ring + 4, :])

            def g_of(ring):
                return flat(QI[:, 4 * ring:4 * ring + 4, :])

            def as_v(z):
                return z.rearrange("p (h i j) -> p h i j", h=CH, i=FINE)

            def as_g(z):
                return z.rearrange("p (h a c) -> p h a c", h=CH, a=AHEAD)

            def coarse(z, c):
                return z[:, 0:FINE, bass.ds(c * CH, CH)].rearrange("p i h -> p h i").unsqueeze(3) \
                    .to_broadcast([P, CH, FINE, FINE])

            def fine(z, c):
                return z[:, 0:FINE, bass.ds(c * CH, CH)].rearrange("p j h -> p h j").unsqueeze(2) \
                    .to_broadcast([P, CH, FINE, FINE])

            def chan(swapped, ring):
                return C[:, ring, swapped].unsqueeze(2).to_broadcast([P, CH, AHEAD, BATCH])

            def ahead(z, c):
                return z[:, :, bass.ds(c * CH, CH)].rearrange("p a h -> p h a").unsqueeze(3) \
                    .to_broadcast([P, CH, AHEAD, BATCH])

            Pw, Qw, Fw, Ew = (PR, PI), (QR, QI), (FR, FI), (E1, E2)
            Bw = (par[:, 3:4], par[:, 4:5])
            PRODUCTS = [(Pw, 1, 2, Pw, 1, Pw, 2), (Pw, 1, 3, Pw, 2, Pw, 3), (Pw, 1, 5, Pw, 4, Pw, 5),
                        (Pw, 4, 5, Pw, 4, Qw, 1), (Qw, 1, 2, Qw, 1, Qw, 2), (Qw, 1, 3, Qw, 2, Qw, 3),
                        (Qw, 1, 5, Qw, 4, Qw, 5), (Qw, 4, 5, Qw, 4, Fw, 1), (Fw, 1, 2, Fw, 1, Fw, 2),
                        (Fw, 1, 2, Fw, 2, Fw, 3), (Fw, 0, 4, Bw, 0, Ew, 0)]

            def operands(n):
                a, lo, hi, b, m, o, at = PRODUCTS[n]
                w = hi - lo
                bR, bI = (z[:, m:m + 1, :].to_broadcast([P, w, HID]) for z in b)
                return (a[0][:, lo:hi, :], a[1][:, lo:hi, :], bR, bI, o[0][:, at:at + w, :], o[1][:, at:at + w, :],
                        [x[:, 0:w * HID].rearrange("p (w h) -> p w h", w=w) for x in (X1, X2)])

            def in_pieces(src, hi, lo, after):
                w = src.shape[1] // len(after)
                return [(src[:, k * w:(k + 1) * w], hi[:, k * w:(k + 1) * w], lo[:, k * w:(k + 1) * w], at)
                        for k, at in enumerate(after)]

            pieces = in_pieces(w_up, *(z[:, :, :, :].rearrange("p k n e -> p (k n e)") for z in (up_h, up_l)), [None] * 4)
            SMALL = len(pieces)
            pieces += in_pieces(w_small, ws_h, ws_l, (3, 4))
            pieces += in_pieces(w_down, *(z[:, :, :].rearrange("p n d -> p (n d)") for z in (dn_h, dn_l)), (6, 7, 9, 10))

            def piece_split(eng, n):
                src, hi, lo, _ = pieces[n]
                eng.wait_ge(hi_split, n + 1)
                return eng.tensor_tensor(lo, stage[:, n % 2, 0:src.shape[1]], hi.bitcast(f32), ALU.subtract)

            def k_store(eng, c, ring, h):
                for a in range(AHEAD):
                    dst = tok_dram[:, bass.ds(c * CH, CH), a * POWERS:(a + 1) * POWERS] \
                        .rearrange("c (m two) b -> two c m b", two=2)[h]
                    eng.dma_start(dst, kout[64 * h + 16 * a:64 * h + 16 * a + 16, ring]).then_inc(k_stored[ring], 16)

            with nc.Block() as block:
                @block.sync
                def _(sp):
                    for h in range(2):
                        hs = slice(h * NST, (h + 1) * NST)
                        sp.dma_start(par[hs, 0, :], log_dt.partition_broadcast(NST)).then_inc(params_in, 16)
                        sp.dma_start(par[hs, 1, :], inv_a).then_inc(params_in, 16)
                        sp.dma_start(par[hs, 2, :], a_imag).then_inc(params_in, 16)
                    for h in range(2):
                        hs = slice(h * NST, (h + 1) * NST)
                        sp.dma_start(par[hs, 3, :], bT[0:NST, :]).then_inc(b_in, 16)
                        sp.dma_start(par[hs, 4, :], bT[NST:P, :]).then_inc(b_in, 16)
                    sp.dma_start(cols[:, :], cols_c).then_inc(cst_in, 16)
                    sp.dma_start(ident[:, :], ident_c).then_inc(cst_in, 16)
                    sp.dma_start(flat(frq[:, :, :]), freq.partition_broadcast(P)).then_inc(cst_in, 16)
                    sp.dma_start(flat(FR[:, 0:2, :]), sel_c).then_inc(sel_in, 16)

                    def c_load(c, ring):
                        sp.dma_start(C[:, ring], cT[:, :, bass.ds(c * CH, CH), :]).then_inc(c_in[ring], 16)

                    c_load(0, 0)
                    c_load(1, 1)
                    with sp.Fori(0, NCH // 2 - 1) as turn:
                        for ring in range(2):
                            c = turn * 2
                            sp.wait_ge(g_done, c + (ring + 1))
                            c_load(c + (ring + 2), ring)
                            sp.wait_ge(k_copied, c + (ring + 1))
                            k_store(sp, c + ring, ring, 0)
                    for ring in range(2):
                        sp.wait_ge(k_copied, NCH - 1 + ring)
                        k_store(sp, NCH - 2 + ring, ring, 0)
                    for ring in range(2):
                        sp.wait_ge(k_stored[ring], NCH // 2 * 8 * 16)

                @block.scalar
                def _(act):
                    act.dma_start(scal[:, 5:8], rby.partition_broadcast(P)).then_inc(rby_in, 16)
                    act.dma_start(qkb[:, :, :], qk_bias).then_inc(rby_in, 16)
                    act.dma_start(flat(row_b[:, :, :]), rows.partition_broadcast(P)).then_inc(rby_in, 16)
                    for n in range(2):
                        act.dma_start(stage[:, n, 0:pieces[n][0].shape[1]], pieces[n][0]).then_inc(stage_in[n], 16)
                    act.wait_ge(params_in, 96)
                    act.activation(par[:, 1, :], par[:, 1, :], ACT.Exp).then_inc(inv_exp, 1)
                    act.wait_ge(sel_in, 16)
                    act.activation(sel[:, :, :].rearrange("p a o -> p (a o)"), flat(FR[:, 0:2, :]), ACT.Copy) \
                        .then_inc(sel_done, 1)
                    for n, (src, hi, _, _) in enumerate(pieces):
                        ring, w = n % 2, src.shape[1]
                        if n >= 2:
                            if pieces[n - 2][3] is None:
                                act.wait_ge(pool_split, n - 1)
                            else:
                                act.wait_ge(dve_split, n - 1 - SMALL)
                            act.dma_start(stage[:, ring, 0:w], src).then_inc(stage_in[ring], 16)
                        if n == len(pieces) - 2:
                            act.wait_ge(prod_re, len(PRODUCTS) - 4)
                            act.wait_ge(prod_im, len(PRODUCTS) - 4)
                            qr, qi = flat(QR[:, 0:FINE, :]), flat(QI[:, 0:FINE, :])
                            act.activation(flat(P2[:, :, :])[0:NST], qi[0:NST], ACT.Copy, scale=-1.0)
                            act.activation(flat(P2[:, :, :])[NST:P], qr[NST:P], ACT.Copy).then_inc(p2_ready, 1)
                        act.wait_ge(stage_in[ring], 16 * (n // 2 + 1))
                        if n in (SMALL, SMALL + 1):
                            act.wait_ge(scal_ready, 1)
                            w_at, factor = ((0, C_LOGIT), (3 * KT * D - WSMALL // 2, C_OUT))[n - SMALL]
                            part = stage[:, ring, w_at:w_at + KT * D]
                            act.activation(part, part, ACT.Identity, scale=scal[:, factor:factor + 1]) \
                                .then_inc(small_scaled, 1)
                            act.wait_ge(small_scaled, n - SMALL + 1)
                        act.activation(hi, stage[:, ring, 0:w], ACT.Copy).then_inc(hi_split, 1)

                    def copy_out(c, ring, first):
                        act.wait_ge(k_full, c + 1)
                        if not first:
                            act.wait_ge(k_stored[ring], (c - ring) * 64)
                        act.activation(kout[:, ring].rearrange("p m b -> p (m b)"), kps[:, ring, :],
                                       ACT.Copy).then_inc(k_copied, 1)
                        act.wait_ge(k_copied, c + 1)
                        k_store(act, c, ring, 1)

                    for ring in range(2):
                        copy_out(ring, ring, True)
                    with act.Fori(1, NCH // 2) as turn:
                        for ring in range(2):
                            copy_out(turn * 2 + ring, ring, False)
                    act.wait_ge(pe_arg, 1)
                    act.activation(pe_tab[:, :, :], pe_tab[:, :, :], ACT.Sin)

                @block.vector
                def _(dve):
                    count = [0]

                    def step(ins):
                        count[0] += 1
                        ins.then_inc(dve_step, 1)
                        dve.wait_ge(dve_step, count[0])

                    dve.wait_ge(rby_in, 48)
                    red, blue, yel = (scal[:, 5 + n:6 + n] for n in range(3))
                    tmp = t[:, 0, :]
                    step(dve.memset(minus_half[:, :], -0.5))
                    step(dve.tensor_scalar(tmp[:, 3:4], red, TENSION * DK, float(DK), ALU.mult, ALU.add))
                    dve.tensor_scalar(scal[:, C_EPS:C_EPS + 1], blue, 0.1 * LN_EPS, LN_EPS, ALU.mult, ALU.add) \
                        .then_inc(root_in, 1)
                    step(dve.tensor_scalar(scal[:, C_OUT:C_OUT + 1], yel, EPS_ADAPTIVE, 1.0, ALU.mult, ALU.add))
                    step(dve.tensor_scalar(scal[:, C_FREQ:C_FREQ + 1], yel, PHASE_MOD, 1.0, ALU.mult, ALU.add))
                    step(dve.tensor_scalar(tmp[:, 0:1], red, 0.1, 1.0, ALU.mult, ALU.add))
                    step(dve.scalar_tensor_tensor(scal[:, C_GAMMA:C_GAMMA + 1], yel, 0.05, tmp[:, 0:1],
                                                  ALU.mult, ALU.add))
                    step(dve.scalar_tensor_tensor(tmp[:, 1:2], blue, 0.05, tmp[:, 0:1], ALU.mult, ALU.add))
                    step(dve.scalar_tensor_tensor(tmp[:, 2:3], yel, 0.15, tmp[:, 1:2], ALU.mult, ALU.add))
                    step(dve.tensor_scalar(row_b[:, 2, :], row_b[:, 2, :], scal[:, C_GAMMA:C_GAMMA + 1], None,
                                           ALU.mult))
                    dve.wait_ge(root_done, 1)
                    step(dve.tensor_tensor(scal[:, C_LOGIT:C_LOGIT + 1], tmp[:, 2:3], tmp[:, 4:5], ALU.mult))
                    dve.tensor_scalar(qkb[:, :, 0], qkb[:, :, 0], scal[:, C_LOGIT:C_LOGIT + 1], None, ALU.mult) \
                        .then_inc(scal_ready, 1)
                    dve.wait_ge(scal_ready, 1)

                    dve.wait_ge(params_in, 96)
                    y, k, r, q, dt, num = par[:, 0, :], *(t[:, n, :] for n in range(1, 6))
                    step(dve.tensor_scalar(k, y, LOG2E, MAGIC, ALU.mult, ALU.add))
                    step(dve.tensor_scalar(k, k, MAGIC, -127.0, ALU.subtract, ALU.max))
                    step(dve.tensor_scalar(k, k, 128.0, None, ALU.min))
                    step(dve.scalar_tensor_tensor(r, k, -LN2_HI, y, ALU.mult, ALU.add))
                    step(dve.scalar_tensor_tensor(r, k, -LN2_LO, r, ALU.mult, ALU.add))
                    step(dve.tensor_scalar(q, r, 1.0 / 5040.0, None, ALU.mult))
                    for n in (720.0, 120.0, 24.0, 6.0, 2.0, 1.0):
                        step(dve.scalar_tensor_tensor(q, q, 1.0 / n, r, ALU.add, ALU.mult))
                    step(dve.tensor_scalar(k, k, 127.0, 8388608.0, ALU.add, ALU.mult))
                    step(dve.tensor_copy(ti[:, :], k))
                    step(dve.scalar_tensor_tensor(dt, q, 1.0, ti[:, :].bitcast(f32), ALU.add, ALU.mult))
                    dve.wait_ge(inv_exp, 1)
                    ah, bh, rd = k, r, q
                    b2, a2 = X1[:, 0:HID], X1[:, HID:2 * HID]
                    step(dve.scalar_tensor_tensor(ah, par[:, 1, :], -0.5, dt, ALU.mult, ALU.mult))
                    step(dve.scalar_tensor_tensor(bh, par[:, 2, :], 0.5, dt, ALU.mult, ALU.mult))
                    step(dve.tensor_tensor(b2, bh, bh, ALU.mult))
                    step(dve.tensor_tensor(a2, ah, ah, ALU.mult))
                    step(dve.tensor_tensor(num, a2, b2, ALU.add))
                    step(dve.tensor_scalar(num, num, -1.0, 1.0, ALU.mult, ALU.add))
                    step(dve.tensor_scalar(ah, ah, -1.0, 1.0, ALU.mult, ALU.add))
                    step(dve.tensor_tensor(ah, ah, ah, ALU.mult))
                    step(dve.tensor_tensor(ah, ah, b2, ALU.add))
                    step(dve.reciprocal(rd, ah))
                    step(dve.tensor_tensor(PR[:, 1, :], num, rd, ALU.mult))
                    step(dve.scalar_tensor_tensor(PI[:, 1, :], bh, 2.0, rd, ALU.mult, ALU.mult))
                    dve.wait_ge(sel_done, 1)
                    for z, v in ((PR, 1.0), (PI, 0.0), (QR, 1.0), (QI, 0.0), (FR, 1.0)):
                        step(dve.memset(z[:, 0, :], v))
                    dve.memset(FI[:, 0, :], 0.0).then_inc(base_ready, 1)
                    dve.wait_ge(base_ready, 1)

                    dve.wait_ge(b_in, 64)
                    for n in range(len(PRODUCTS)):
                        aR, aI, bR, bI, oR, oI, (x, y) = operands(n)
                        dve.tensor_tensor(x, aI, bI, ALU.mult)
                        step(dve.tensor_tensor(oR, aR, bR, ALU.mult))
                        dve.tensor_tensor(oR, oR, x, ALU.subtract).then_inc(prod_re, 1)
                        dve.wait_ge(prod_pool, n + 1)
                        dve.tensor_tensor(oI, oI, y, ALU.add).then_inc(prod_im, 1)
                        dve.wait_ge(prod_re, n + 1)
                        dve.wait_ge(prod_im, n + 1)
                        for piece in range(len(pieces)):
                            if pieces[piece][3] == n:
                                piece_split(dve, piece).then_inc(dve_split, 1)
                    p1, qr, qi = flat(P1[:, :, :]), flat(QR[:, 0:FINE, :]), flat(QI[:, 0:FINE, :])
                    dve.tensor_copy(p1[0:NST], qr[0:NST])
                    dve.tensor_copy(p1[NST:P], qi[NST:P]).then_inc(p1_ready, 1)
                    dve.wait_ge(cst_in, 48)
                    dve.tensor_scalar(flat(E1[:, :, :]), flat(E1[:, :, :]), cols[:, SIGN:SIGN + 1], 2.0,
                                      ALU.mult, ALU.mult)
                    dve.tensor_scalar(flat(E2[:, :, :]), flat(E2[:, :, :]), -2.0, None, ALU.mult) \
                        .then_inc(powers_done, 1)
                    dve.wait_ge(p1_ready, 1)
                    dve.wait_ge(p2_ready, 1)
                    dve.wait_ge(powers_done, 1)

                    def chunk(c, ring, first):
                        if not first:
                            dve.wait_ge(k_full, c - 1)
                        v, g = v_of(ring), g_of(ring)
                        dve.tensor_tensor(as_v(v), coarse(P1, c), fine(PR, c), ALU.mult).then_inc(v_done, 1)
                        dve.wait_ge(c_in[ring], (c - ring) * 8 + 16)
                        dve.tensor_tensor(as_g(g), chan(0, ring), ahead(E1, c), ALU.mult).then_inc(v_done, 1)
                        dve.wait_ge(v_pool, c + 1)
                        dve.wait_ge(v_done, c * 3 + 1)
                        dve.tensor_tensor(v, v, X1[:, :], ALU.add).then_inc(v_done, 1)
                        dve.wait_ge(g_pool, c + 1)
                        dve.wait_ge(v_done, c * 3 + 2)
                        dve.tensor_tensor(g, g, X2[:, :], ALU.add).then_inc(g_done, 1)

                    for ring in range(2):
                        chunk(ring, ring, True)
                    with dve.Fori(1, NCH // 2) as turn:
                        for ring in range(2):
                            chunk(turn * 2 + ring, ring, False)

                    den, ang, turns = FR[:, 0, :], pe_tab[:, :, :], E1[:, 0:NT, :]
                    quarter = frq[:, 1:2, :].to_broadcast([P, NT, D])
                    step(dve.tensor_scalar(den, frq[:, 0, :], scal[:, C_FREQ:C_FREQ + 1], None, ALU.mult))
                    step(dve.reciprocal(den, den))
                    for i in range(NT):
                        ins = dve.tensor_scalar(pe_tab[:, i, :], den, cols[:, POS + i:POS + i + 1], None, ALU.mult)
                    step(ins)
                    step(dve.tensor_tensor(turns, ang, quarter, ALU.add))
                    step(dve.tensor_scalar(turns, turns, 1.0 / (2.0 * math.pi), MAGIC, ALU.mult, ALU.add))
                    step(dve.tensor_scalar(turns, turns, MAGIC, None, ALU.subtract))
                    step(dve.scalar_tensor_tensor(ang, turns, -TWO_PI_HI, ang, ALU.mult, ALU.add))
                    step(dve.scalar_tensor_tensor(ang, turns, -TWO_PI_LO, ang, ALU.mult, ALU.add))
                    step(dve.tensor_tensor(ang, ang, quarter, ALU.add))
                    dve.tensor_scalar(ang, ang, 3.1415925, -3.1415925, ALU.min, ALU.max).then_inc(pe_arg, 1)

                @block.gpsimd
                def _(pool):
                    pool.wait_ge(root_in, 1)
                    pool.tensor_tensor(t[:, 0, 4:5], t[:, 0, 3:4], minus_half[:, 0:1], ALU.pow).then_inc(root_done, 1)
                    for n in range(SMALL):
                        piece_split(pool, n).then_inc(pool_split, 1)
                    pool.wait_ge(base_ready, 1)
                    pool.wait_ge(b_in, 64)
                    for n in range(len(PRODUCTS)):
                        if n:
                            pool.wait_ge(prod_re, n)
                            pool.wait_ge(prod_im, n)
                        aR, aI, bR, bI, _, oI, (_, y) = operands(n)
                        pool.tensor_tensor(y, aI, bR, ALU.mult)
                        pool.tensor_tensor(oI, aR, bI, ALU.mult).then_inc(prod_pool, 1)
                    pool.wait_ge(p2_ready, 1)
                    pool.wait_ge(powers_done, 1)

                    def chunk(c, ring, first):
                        if not first:
                            pool.wait_ge(v_done, c * 3)
                        pool.tensor_tensor(as_v(X1[:, :]), coarse(P2, c), fine(PI, c), ALU.mult).then_inc(v_pool, 1)
                        pool.wait_ge(c_in[ring], (c - ring) * 8 + 16)
                        if not first:
                            pool.wait_ge(g_done, c)
                        pool.tensor_tensor(as_g(X2[:, :]), chan(1, ring), ahead(E2, c), ALU.mult).then_inc(g_pool, 1)

                    chunk(0, 0, True)
                    chunk(1, 1, False)
                    with pool.Fori(1, NCH // 2) as turn:
                        for ring in range(2):
                            chunk(turn * 2 + ring, ring, False)

                @block.tensor
                def _(pe):
                    def chunk(c, ring, first):
                        pe.wait_ge(v_done, c * 3 + 3)
                        pe.wait_ge(g_done, c + 1)
                        if not first:
                            pe.wait_ge(k_copied, c - 1)
                        v = v_of(ring).rearrange("p (h b) -> p h b", h=CH)
                        g = g_of(ring).rearrange("p (h a) -> p h a", h=CH)
                        for hh in range(CH):
                            half, m = hh % 2, hh // 2
                            mm = pe.matmul(kps[64 * half:64 * half + 64, ring, m * POWERS:(m + 1) * POWERS],
                                           g[:, hh, :], v[:, hh, :], start=True, stop=True)
                        mm.then_inc(k_full, 1)

                    for ring in range(2):
                        chunk(ring, ring, True)
                    with pe.Fori(1, NCH // 2) as turn:
                        for ring in range(2):
                            chunk(turn * 2 + ring, ring, False)

        QK = sb("QK", [P, PAIRS, 2, TOK], f32r)
        Qs, Ks = QK[:, :, 0, :], QK[:, :, 1, :]
        NP = 4
        probs = sb("probs", [P, NP, 2, TOK])
        gates = sb("gates", [P, 2, 2, TOK])
        x_in = sb("x_in", [P, NT, D])
        hb = sb("hb", [P, NT, D])
        xn = sb("xn", [P, NT, D])
        xa = sb("xa", [P, NT, D])
        xab = sb("xab", [P, NT, D])
        h2 = sb("h2", [P, NT, D])
        res = sb("res", [P, NT * D])
        xT = sb("xT_h", [P, KT, TOK], f32r), sb("xT_l", [P, KT, TOK], f32r)
        hT = sb("hT_h", [P, KT, TOK], f32r), sb("hT_l", [P, KT, TOK], f32r)
        qk = [(sb(f"qk_h{m}", [P, 2, TOK], f32r), sb(f"qk_l{m}", [P, 2, TOK], f32r)) for m in range(KT)]
        v_aug = sb("v_aug", [P, NT, HEADS, 32])
        o_t = sb("o_t", [P, TOK])
        g_act, g_mul = sb("g_act", [P, 2, TOK]), sb("g_mul", [P, TOK])
        act_h, act_l = sb("act_h", [P, 3, TOK], f32r), sb("act_l", [P, 3, TOK], f32r)
        stats, mv = sb("stats", [P, NT, 6]), sb("mv", [P, NT, 2])
        wait_carrier = sb("wait_carrier", [P, 1])
        eps_ln, eps_attn = sb("eps_ln", [P, NT]), sb("eps_attn", [P, NT])
        veps, rstd = sb("veps", [P, NT]), sb("rstd", [P, NT])
        m_neg = sb("m_neg", [P, NT, 2, PAIRS])
        o_rec = sb("o_rec", [P, NT * 4])
        l_max, l_sum = sb("l_max", [P, NT]), sb("l_sum", [P, NT])
        l_exp, gate = sb("l_exp", [P, NT, EXPERTS]), sb("gate", [P, NT, EXPERTS])
        pr, rest = sb("pr", [P, NT, EXPERTS + 8]), sb("rest", [P, NT, EXPERTS + 8])
        top8, found = sb("top8", [P, NT, 8]), sb("found", [P, NT, 8])
        max_h, max_l = probs[0:HEADS, 2, 0, :].bitcast(f32r), probs[0:HEADS, 3, 0, :].bitcast(f32r)
        l_t = probs[0:EXPERTS, 0, 0, :]
        gate_t = probs[0:EXPERTS, 1, 0, :]

        ring = ps("ring", [P, 2, 2 * BANK])
        av_ps = ps("av_ps", [P, BANK])
        side = ps("side", [P, BANK])
        acc = ps("acc", [P, 2 * BANK])

        slot_full, slot_drained = ([sem(f"slot_{what}{n}") for n in range(3)] for what in ("full", "drained"))
        x_loaded, x_ready, xab_ready, hb_ready = (sem(n) for n in ("x_loaded", "x_ready", "xab_ready", "hb_ready"))
        stats_done, mv_done, veps_done, rstd_done = (
            [sem(n + "_in"), sem(n + "_out")] for n in ("stats_done", "mv_done", "veps_done", "rstd_done"))
        centred, h2_normal = sem("centred"), sem("h2_normal")
        max_stored = sem("max_stored")
        av_done, ot_copied, rec_done = sem("av_done"), sem("ot_copied"), sem("rec_done")
        y_centred, h2_ready, route, gate_ready = sem("y_centred"), sem("h2_ready"), sem("route"), sem("gate_ready")
        gate_stored, gates_in, stored = sem("gate_stored"), [sem("gates_in0"), sem("gates_in1")], sem("stored")
        up_full, gelu_done, mul_done, hi_done, lo_done, down_done = (sem(n) for n in (
            "up_full", "gelu_done", "mul_done", "hi_done", "lo_done", "down_done"))
        acc_free, vinit, lmax_done = sem("acc_free"), sem("vinit"), sem("lmax_done")
        res_copied = sem("res_copied")
        ROUTE = 6

        def psum(tag):
            return side[:, :] if slot(tag) == 2 else ring[:, slot(tag), :]

        def full(eng, tag, it):
            eng.wait_ge(slot_full[slot(tag)], full_at(tag, it))

        def drained(eng, tag, it):
            eng.wait_ge(slot_drained[slot(tag)], drained_at(tag, it))

        def half(eng, tag, it):
            eng.wait_ge(slot_drained[slot(tag)], half_at(tag, it))

        def is_first(b, n=0, upto=1):
            return isinstance(b, int) and b == 0 and n < upto

        def wait_apart(dve, of, value):
            dve.wait_ge(of, value)
            dve.memset(wait_carrier[:, :], 0.0)

        def each_batch(eng, run):
            run(BEFORE, -1)
            run(FIRST, 0)
            with eng.Fori(1, BATCH - 1) as it:
                run(PLAN, it)
            run(LAST, BATCH - 1)
            run(AFTER, BATCH)

        with nc.Block() as block:
            @block.sync
            def _(sp):
                def load_x(b):
                    image = tok_dram[b] if isinstance(b, int) else \
                        tok_dram[bass.ds(b, 1), :, :].rearrange("o c l -> (o c) l")
                    text = txt[b:b + 1] if isinstance(b, int) else txt[bass.ds(b, 1), :, :]
                    sp.dma_start(x_in[:, 0:2, :], image.rearrange("(i p) d -> p i d", p=P)).then_inc(x_loaded, 16)
                    sp.dma_start(x_in[:, 2:3, :], text.rearrange("o p d -> p o d")).then_inc(x_loaded, 16)

                def load_gates(c):
                    sp.dma_start(gates[:, c % 2], gate_dram[2 * c:2 * c + 2, :].partition_broadcast(P)) \
                        .then_inc(gates_in[c % 2], 16)

                def run(plan, it):
                    if plan is BEFORE:
                        load_x(0)
                    f = it - 1
                    if plan in (FIRST, PLAN):
                        sp.wait_ge(hb_ready, it + 1)
                        sp.wait_ge(x_ready, it + 1)
                        load_x(it + 1)
                    for what, n in plan:
                        if what in ("f", "F") and n % 2 == 0 and 4 <= n < NEXP - 2:
                            b = f if what == "f" else it
                            sp.wait_ge(hi_done, b * NEXP + n)
                            sp.wait_ge(lo_done, b * NEXP + n)
                            load_gates(n // 2)
                        elif what == "fend":
                            sp.wait_ge(acc_free, f + 2)
                            dst = out[f:f + 1] if isinstance(f, int) else out[bass.ds(f, 1), :, :]
                            sp.dma_start(dst.rearrange("o (i p) d -> p (o i) d", p=P),
                                         res[:, :].rearrange("p (i d) -> p i d", i=NT)) \
                                .then_inc(stored, 16)
                        elif what == "mT":
                            drained(sp, "mT", it)
                            for half_n, src in enumerate((max_h, max_l)):
                                for e in range(2):
                                    row = 64 * e + MROW + half_n
                                    sp.dma_start(Qs[row:row + 1, :, :].bitcast(f32),
                                                 src[8 * e:8 * e + 8, :].bitcast(f32)).then_inc(max_stored, 16)
                        elif what == "gT":
                            drained(sp, "gT", it)
                            sp.dma_start(gate_dram[:, :], gate_t).then_inc(gate_stored, 16)
                            if plan is not FIRST:
                                sp.wait_ge(hi_done, it * NEXP)
                                sp.wait_ge(lo_done, it * NEXP)
                            sp.wait_ge(gate_stored, it * 16 + 16)
                            load_gates(0)
                            load_gates(1)

                each_batch(sp, run)
                sp.wait_ge(stored, BATCH * 16)

            @block.scalar
            def _(act):
                def gelu(n, b):
                    act.wait_ge(up_full, b * NEXP + (n + 1))
                    if not is_first(b, n, 2):
                        act.wait_ge(hi_done, b * NEXP + (n - 1))
                        act.wait_ge(lo_done, b * NEXP + (n - 1))
                    act.activation(g_act[:, n % 2, :], side[:, 0:TOK], ACT.Gelu).then_inc(gelu_done, 1)

                def high(tag, it, to):
                    full(act, tag, it)
                    act.activation(to, psum(tag).rearrange("p (k n) -> p k n", k=KT)[:, :, 0:TOK], ACT.Copy) \
                        .then_inc(slot_drained[slot(tag)], 1)

                def exps(r, it):
                    full(act, f"st{r}", it)
                    if r >= NP:
                        act.wait_ge(av_done, it * STEPS + ((r - NP) // 2 + 1))
                    act.activation(probs[:, r % NP], psum(f"st{r}").rearrange("p (e n) -> p e n", e=2)[:, :, 0:TOK],
                                   ACT.Exp).then_inc(slot_drained[slot(f"st{r}")], 2)

                def run(plan, it):
                    for what, n in plan:
                        if what == "f":
                            gelu(n, it - 1)
                        elif what == "F":
                            gelu(n, it)
                        elif what == "xT":
                            full(act, f"xT{n}", it)
                            act.activation(xT[0][:, n, :], psum(f"xT{n}")[:, 0:TOK], ACT.Copy) \
                                .then_inc(slot_drained[slot(f"xT{n}")], 1)
                        elif what in ("q", "k"):
                            full(act, f"{what}{n}", it)
                            m = ("q", "k").index(what)
                            act.activation(qk[n][0][:, m, :], psum(f"{what}{n}")[:, 0:TOK], ACT.Identity,
                                           bias=qkb[:, n, m:m + 1]).then_inc(slot_drained[slot(f"{what}{n}")], 1)
                        elif what == "sel":
                            full(act, f"sel{n}", it)
                            act.activation(QK[:, n], psum(f"sel{n}").rearrange("p (m n) -> p m n", m=2)[:, :, 0:TOK],
                                           ACT.Identity, bias=cols[:, ONES_ROW:ONES_ROW + 1]) \
                                .then_inc(slot_drained[slot(f"sel{n}")], 2)
                        elif what == "mT":
                            full(act, "mT", it)
                            act.activation(max_h, psum("mT")[0:HEADS, 0:TOK], ACT.Copy) \
                                .then_inc(slot_drained[slot("mT")], 1)
                        elif what == "st":
                            exps(n, it)
                        elif what == "oT":
                            high("oT", it, xT[0][:, :, :])
                        elif what == "hT":
                            high("hT", it, hT[0][:, :, :])
                        elif what == "lT":
                            full(act, "lT", it)
                            act.activation(l_t, psum("lT")[0:EXPERTS, 0:TOK], ACT.Copy) \
                                .then_inc(slot_drained[slot("lT")], 2)
                        elif what == "logit":
                            act.wait_ge(lmax_done, it + 1)
                            for i in range(NT):
                                ins = act.activation(l_exp[:, i, :], psum("logit")[:, i * EXPERTS:(i + 1) * EXPERTS],
                                                     ACT.Exp, bias=l_max[:, i:i + 1])
                            ins.then_inc(slot_drained[slot("logit")], 2)

                        elif what == "gT":
                            act.wait_ge(h2_ready, it + 1)
                            if plan is not FIRST:
                                act.wait_ge(stored, it * 16)
                            act.activation(res[:, :], h2[:, :, :].rearrange("p i d -> p (i d)"), ACT.Copy) \
                                .then_inc(res_copied, 1)

                each_batch(act, run)

            @block.vector
            def _(dve):
                def wait_gates(n, b):
                    c = (n - SHARED) // 2
                    dve.wait_ge(gates_in[c % 2], b * (4 * EXPERTS) + 16 * (c // 2 + 1))

                def expert(n, b):
                    to, a = act_h[:, n % 3, :], g_act[:, n % 2, :]
                    dve.wait_ge(gelu_done, b * NEXP + (n + 1))
                    if n >= 3:
                        dve.wait_ge(down_done, b * NEXP + (n - 2))
                    if n < SHARED:
                        dve.tensor_copy(to, a).then_inc(hi_done, 1)
                    else:
                        wait_gates(n, b)
                        q = n - SHARED
                        dve.tensor_tensor(to, a, gates[:, (q // 2) % 2, q % 2, :], ALU.mult).then_inc(hi_done, 1)

                def low(tag, it, high, to):
                    half(dve, tag, it)
                    dve.tensor_tensor(to, psum(tag).rearrange("p (k n) -> p k n", k=KT)[:, :, 0:TOK],
                                      high.bitcast(f32), ALU.subtract).then_inc(slot_drained[slot(tag)], 1)

                def moments(src, kind, at):
                    for i in range(NT):
                        ins = dve.bn_stats(stats[:, i, :], src[:, i, :])
                    ins.then_inc(stats_done[kind], 1)
                    wait_apart(dve, stats_done[kind], at)
                    for i in range(NT):
                        ins = dve.bn_aggr(mv[:, i, :], stats[:, i, :])
                    ins.then_inc(mv_done[kind], 1)
                    dve.wait_ge(mv_done[kind], at)

                def copy_heads(g, it):
                    dve.wait_ge(av_done, it * STEPS + NT * (g + 1))
                    if g:
                        full(dve, f"o{g - 1}", it)
                    dve.tensor_copy(o_t[:, :], av_ps[:, 0:TOK]).then_inc(ot_copied, 1)

                def divide(g, it):
                    full(dve, f"o{g}", it)
                    heads = psum(f"o{g}")[:, 0:NT * P].rearrange("p (i j c) -> p i j c", i=NT, j=4)
                    rec = o_rec[:, :].rearrange("p (i j) -> p i j", i=NT)
                    dve.reciprocal(rec, heads[:, :, :, DK]).then_inc(rec_done, 1)
                    dve.wait_ge(rec_done, it * 4 + (g + 1))
                    for i in range(NT):
                        ins = dve.tensor_tensor(
                            xa[:, i, 64 * g:64 * g + 64].rearrange("p (j d) -> p j d", j=4),
                            heads[:, i, :, 0:DK], rec[:, i, :].unsqueeze(2).to_broadcast([P, 4, DK]), ALU.mult)
                    ins.then_inc(slot_drained[slot(f"o{g}")], 2)

                def choose(it):
                    nth = [0]

                    def step(ins, apart=False):
                        nth[0] += 1
                        ins.then_inc(route, 1)
                        if apart:
                            wait_apart(dve, route, it * ROUTE + nth[0])
                        else:
                            dve.wait_ge(route, it * ROUTE + nth[0])

                    drained(dve, "logit", it)
                    step(dve.tensor_reduce(l_sum[:, :], l_exp[:, :, :], AX.X, ALU.add))
                    step(dve.reciprocal(l_sum[:, :], l_sum[:, :]))
                    step(dve.tensor_tensor(pr[:, :, 0:EXPERTS], l_exp[:, :, :],
                                           l_sum[:, :].unsqueeze(2).to_broadcast([P, NT, EXPERTS]), ALU.mult), True)
                    for i in range(NT):
                        ins = dve.max(top8[:, i, :], pr[:, i, :])
                    step(ins)
                    step(dve.tensor_copy(found[:, :, 0:TOPK], top8[:, :, 0:TOPK]), True)
                    for i in range(NT):
                        ins = dve.match_replace(rest[:, i, :], found[:, i, :], pr[:, i, :], 0.0)
                    step(ins)
                    dve.tensor_tensor(gate[:, :, :], pr[:, :, 0:EXPERTS], rest[:, :, 0:EXPERTS], ALU.subtract) \
                        .then_inc(gate_ready, 1)

                def run(plan, it):
                    for what, n in plan:
                        if what == "f":
                            expert(n, it - 1)
                        elif what == "F":
                            expert(n, it)
                        elif what == "ln1":
                            dve.wait_ge(x_loaded, it * 32 + 64)
                            if plan is not BEFORE:
                                dve.wait_ge(xab_ready, it + 1)
                            moments(x_in, 0, it + 2)
                            for i in range(NT):
                                ins = dve.tensor_scalar(xn[:, i, :], x_in[:, i, :], mv[:, i, 0:1], None, ALU.subtract)
                            ins.then_inc(centred, 1)
                            dve.wait_ge(centred, it + 2)
                            dve.wait_ge(rstd_done[0], it + 2)
                            for i in range(NT):
                                ins = dve.scalar_tensor_tensor(xn[:, i, :], xn[:, i, :], rstd[:, i:i + 1],
                                                               pe_tab[:, i, :], ALU.mult, ALU.add)
                            ins.then_inc(x_ready, 1)
                        elif what == "xT":
                            half(dve, f"xT{n}", it)
                            dve.tensor_tensor(xT[1][:, n, :], psum(f"xT{n}")[:, 0:TOK], xT[0][:, n, :].bitcast(f32),
                                              ALU.subtract).then_inc(slot_drained[slot(f"xT{n}")], 1)
                        elif what in ("q", "k"):
                            half(dve, f"{what}{n}", it)
                            m = ("q", "k").index(what)
                            dve.scalar_tensor_tensor(qk[n][1][:, m, :], psum(f"{what}{n}")[:, 0:TOK],
                                                     qkb[:, n, m:m + 1], qk[n][0][:, m, :].bitcast(f32),
                                                     ALU.add, ALU.subtract) \
                                .then_inc(slot_drained[slot(f"{what}{n}")], 1)
                        elif what == "v" and n == NT - 1:
                            full(dve, "v", it)
                            for i in range(NT):
                                ins = dve.tensor_tensor(v_aug[:, i, :, 0:DK],
                                                        psum("v")[:, i * D:(i + 1) * D].rearrange("p (h d) -> p h d", h=HEADS),
                                                        row_b[:, 0, :].rearrange("p (h d) -> p h d", h=HEADS), ALU.add)
                            ins.then_inc(slot_drained[slot("v")], 2)
                        elif what == "s":
                            full(dve, f"s{n}", it)
                            dve.tensor_reduce(m_neg[:, n % NT, :, n // NT],
                                              psum(f"s{n}").rearrange("p (e n) -> p e n", e=2)[:, :, 0:TOK],
                                              AX.X, ALU.max, negate=True).then_inc(slot_drained[slot(f"s{n}")], 2)
                        elif what == "fend":
                            dve.wait_ge(down_done, it * NEXP)
                            dve.wait_ge(res_copied, it)
                            dve.tensor_tensor(res[:, :], acc[:, 0:NT * D], res[:, :], ALU.add).then_inc(acc_free, 1)
                        elif what == "mT":
                            half(dve, "mT", it)
                            dve.tensor_tensor(max_l, psum("mT")[0:HEADS, 0:TOK], max_h.bitcast(f32), ALU.subtract) \
                                .then_inc(slot_drained[slot("mT")], 1)
                        elif what == "av" and n % NT == NT - 1:
                            copy_heads(n // NT, it)
                        elif what == "o":
                            divide(n, it)
                        elif what == "oT":
                            low("oT", it, xT[0][:, :, :], xT[1][:, :, :])
                        elif what == "wo":
                            full(dve, "wo", it)
                            dve.wait_ge(xab_ready, it + 1)
                            wide = xab[:, :, :].rearrange("p i d -> p (i d)")
                            dve.tensor_tensor(wide, psum("wo")[:, 0:NT * D], wide, ALU.add) \
                                .then_inc(slot_drained[slot("wo")], 2)
                            drained(dve, "wo", it)
                        elif what == "ln_mean":
                            moments(xab, 1, it * 2 + 1)
                        elif what == "ln_h2":
                            for i in range(NT):
                                ins = dve.scalar_tensor_tensor(xa[:, i, :], xab[:, i, :], mv[:, i, 0:1],
                                                               row_b[:, 2, :], ALU.subtract, ALU.mult)
                            ins.then_inc(y_centred, 1)
                            dve.wait_ge(y_centred, it + 1)
                            dve.wait_ge(rstd_done[1], it * 2 + 1)
                            dve.wait_ge(hb_ready, it + 1)
                            if plan is not FIRST:
                                dve.wait_ge(res_copied, it)
                            for i in range(NT):
                                ins = dve.scalar_tensor_tensor(h2[:, i, :], xa[:, i, :], rstd[:, i:i + 1],
                                                               hb[:, i, :], ALU.mult, ALU.add)
                            ins.then_inc(h2_ready, 1)
                            dve.wait_ge(h2_ready, it + 1)
                            moments(h2, 1, it * 2 + 2)
                        elif what == "ln_out":
                            dve.wait_ge(rstd_done[1], it * 2 + 2)
                            for i in range(NT):
                                ins = dve.tensor_scalar(xa[:, i, :], h2[:, i, :], mv[:, i, 0:1], rstd[:, i:i + 1],
                                                        ALU.subtract, ALU.mult)
                            ins.then_inc(h2_normal, 1)
                        elif what == "hT":
                            low("hT", it, hT[0][:, :, :], hT[1][:, :, :])
                        elif what == "logit":
                            full(dve, "logit", it)
                            dve.tensor_reduce(l_max[:, :],
                                              psum("logit")[:, 0:NT * EXPERTS].rearrange("p (i x) -> p i x", i=NT),
                                              AX.X, ALU.max, negate=True).then_inc(lmax_done, 1)
                        elif what == "choose":
                            choose(it)
                        elif what == "gT":
                            full(dve, "gT", it)
                            dve.tensor_copy(gate_t, psum("gT")[0:EXPERTS, 0:TOK]).then_inc(slot_drained[slot("gT")], 2)

                dve.memset(v_aug[:, :, :, :], 0.0).then_inc(vinit, 1)
                dve.memset(pr[:, :, :], -1.0).then_inc(vinit, 1)
                dve.memset(found[:, :, :], -1.0).then_inc(vinit, 1)
                dve.memset(eps_ln[:, :], LN_EPS).then_inc(vinit, 1)
                dve.tensor_copy(eps_attn[:, :], scal[:, C_EPS:C_EPS + 1].to_broadcast([P, NT])).then_inc(vinit, 1)
                dve.wait_ge(vinit, 5)
                dve.memset(v_aug[:, :, :, DK:DK + 1], 1.0).then_inc(vinit, 1)
                dve.wait_ge(vinit, 6)
                dve.memset(wait_carrier[:, :], 0.0).then_inc(acc_free, 1)
                each_batch(dve, run)

            @block.gpsimd
            def _(pool):
                def root(kind, at, eps):
                    pool.wait_ge(mv_done[kind], at)
                    pool.tensor_tensor(veps[:, :], mv[:, :, 1], eps[:, :], ALU.add).then_inc(veps_done[kind], 1)
                    pool.wait_ge(veps_done[kind], at)
                    pool.tensor_tensor(rstd[:, :], veps[:, :], minus_half[:, :], ALU.pow).then_inc(rstd_done[kind], 1)

                def low(n, b):
                    g, at = g_act[:, n % 2, :], b * NEXP + (n + 1)
                    pool.wait_ge(gelu_done, at)
                    if n >= SHARED:
                        q = n - SHARED
                        c = q // 2
                        pool.wait_ge(gates_in[c % 2], b * (4 * EXPERTS) + 16 * (c // 2 + 1))
                        pool.wait_ge(lo_done, at - 1)
                        pool.tensor_tensor(g_mul[:, :], g, gates[:, c % 2, q % 2, :], ALU.mult) \
                            .then_inc(mul_done, 1)
                        pool.wait_ge(mul_done, b * EXPERTS + (q + 1))
                        g = g_mul[:, :]
                    pool.wait_ge(hi_done, at)
                    pool.tensor_tensor(act_l[:, n % 3, :], g, act_h[:, n % 3, :].bitcast(f32), ALU.subtract) \
                        .then_inc(lo_done, 1)

                def residual(b):
                    pool.wait_ge(x_ready, b + 1)
                    pool.tensor_tensor(xab[:, :, :], xn[:, :, :], row_b[:, 1:2, :].to_broadcast([P, NT, D]),
                                       ALU.add).then_inc(xab_ready, 1)

                def tokens_beta(b):
                    pool.tensor_tensor(hb[:, :, :], x_in[:, :, :], row_b[:, 3:4, :].to_broadcast([P, NT, D]),
                                       ALU.add).then_inc(hb_ready, 1)

                def run(plan, it):
                    for what, n in plan:
                        if what == "f":
                            low(n, it - 1)
                        elif what == "F":
                            low(n, it)
                        elif what == "ln1":
                            root(0, it + 2, eps_ln)
                            if plan is BEFORE:
                                residual(0)
                                tokens_beta(0)
                        elif what == "ln_mean":
                            root(1, it * 2 + 1, eps_attn)
                        elif what == "ln_h2":
                            root(1, it * 2 + 2, eps_ln)
                        elif what == "logit" and plan is not LAST:
                            pool.wait_ge(h2_ready, it + 1)
                            residual(it + 1)
                            tokens_beta(it + 1)

                pool.wait_ge(vinit, 6)
                each_batch(pool, run)

            @block.tensor
            def _(pe):
                def free(tag, it):
                    if not (isinstance(it, int) and before_at(tag, it) == 0):
                        pe.wait_ge(slot_drained[slot(tag)], before_at(tag, it))

                def done(ins, tag):
                    ins.then_inc(slot_full[slot(tag)], 1)

                def mm3(to, a, w, first=True, last=True, **more):
                    pe.matmul(to, a[0], w[0], start=first, stop=False, **more)
                    pe.matmul(to, a[0], w[1], start=False, stop=False, **more)
                    return pe.matmul(to, a[1], w[0], start=False, stop=last, **more)

                def turn(tag, src):
                    for i in range(NT):
                        for kt in range(KT):
                            ins = pe.transpose(psum(tag)[:, kt * BANK + i * P:kt * BANK + (i + 1) * P],
                                               src[:, i, kt * P:(kt + 1) * P], ident[:, :])
                    done(ins, tag)

                def by_rows(tag, xt, w, n, tiles=range(NT)):
                    for i in tiles:
                        for kt in range(KT):
                            ins = mm3(psum(tag)[:, i * n:(i + 1) * n], [x[:, kt, i * P:(i + 1) * P] for x in xt],
                                      [z[:, kt, :] for z in w], kt == 0, kt == KT - 1)
                    if NT - 1 in tiles:
                        done(ins, tag)

                def expert_up(n, b):
                    for kt in range(KT):
                        ins = mm3(side[:, 0:TOK], (up_h[:, kt, n, :], up_l[:, kt, n, :]),
                                  [x[:, kt, :] for x in hT], kt == 0, kt == KT - 1)
                    ins.then_inc(up_full, 1)

                def expert_down(n, b):
                    pe.wait_ge(hi_done, b * NEXP + (n + 1))
                    pe.wait_ge(lo_done, b * NEXP + (n + 1))
                    if n == 0:
                        pe.wait_ge(acc_free, b + 1)
                    for i in range(NT):
                        ins = mm3(acc[:, i * D:(i + 1) * D],
                                  [x[:, n % 3, i * P:(i + 1) * P] for x in (act_h, act_l)],
                                  (dn_h[:, n, :], dn_l[:, n, :]), n == 0 and i != 1, n == NEXP - 1,
                                  skip_group_check=True)
                    ins.then_inc(down_done, 1)

                def project(what, m, it):
                    tag = f"{what}{m}"
                    w = wq if what == "q" else wk
                    for kt in range(KT):
                        ins = mm3(psum(tag)[:, 0:TOK], [z[:, kt, m * P:(m + 1) * P] for z in w],
                                  [x[:, kt, :] for x in xT], kt == 0, kt == KT - 1)
                    done(ins, tag)

                def stack(p, it):
                    m, at = p // 4, 32 * (p % 4)
                    free(f"sel{p}", it)
                    if p % 4 == 0:
                        drained(pe, f"k{m}", it)
                    for n, kinds in enumerate(((SEL_QH, SEL_QL), (SEL_KH, SEL_KL))):
                        for part, kind in enumerate(kinds):
                            ins = pe.matmul(psum(f"sel{p}")[:, n * BANK:n * BANK + TOK], sel[at:at + 32, kind, :],
                                            qk[m][part][at:at + 32, n, :], start=part == 0, stop=part == 1)
                    done(ins, f"sel{p}")

                def logits(r, it):
                    p, i = r // NT, r % NT
                    free(f"s{r}", it)
                    if i == 0:
                        drained(pe, f"sel{p}", it)
                    for e in range(2):
                        rows_e = slice(64 * e, 64 * e + MROW)
                        ins = pe.matmul(psum(f"s{r}")[:, e * BANK:e * BANK + TOK], Qs[rows_e, p, i * P:(i + 1) * P],
                                        Ks[rows_e, p, :], start=True, stop=True)
                    done(ins, f"s{r}")

                def logits_t(r, it):
                    k = r // 2
                    p, i = 2 * (k // NT) + r % 2, k % NT
                    free(f"st{r}", it)
                    for e in range(2):
                        rows_e = slice(64 * e, 64 * e + 64)
                        ins = pe.matmul(psum(f"st{r}")[:, e * BANK:e * BANK + TOK], Ks[rows_e, p, i * P:(i + 1) * P],
                                        Qs[rows_e, p, :], start=True, stop=True)
                    done(ins, f"st{r}")

                def weigh(k, it):
                    g, i = k // NT, k % NT
                    drained(pe, f"st{2 * k}", it)
                    drained(pe, f"st{2 * k + 1}", it)
                    if i == 0 and g:
                        pe.wait_ge(ot_copied, it * 4 + g)
                    for j in range(4):
                        ins = pe.matmul(av_ps[32 * j:32 * j + 32, 0:TOK], v_aug[:, i, 4 * g + j, :],
                                        probs[:, (2 * k + j // 2) % NP, j % 2, :], start=i == 0, stop=i == NT - 1)
                    ins.then_inc(av_done, 1)

                def side_free(plan, at, it):
                    users = [step for step in plan[:at] if step[0] in SIDE + EXPERT]
                    if not users:
                        if plan is BEFORE:
                            return
                        users = [step for step in (BEFORE if plan is FIRST else PLAN) if step[0] in SIDE + EXPERT]
                        it = it - 1
                    what, n = users[-1]
                    if what in EXPERT:
                        pe.wait_ge(gelu_done, (it - 1 if what == "f" else it) * NEXP + (n + 1))
                    else:
                        drained(pe, what if what in ("logit", "gT") else f"{what}{n}", it)

                def run(plan, it):
                    for at, (what, n) in enumerate(plan):
                        if what in SIDE + EXPERT:
                            side_free(plan, at, it)
                        if what == "f":
                            expert_up(n, it - 1)
                        elif what == "down":
                            expert_down(n, it - 1)
                        elif what == "F":
                            expert_up(n, it)
                        elif what == "Down":
                            expert_down(n, it)
                        elif what == "xT":
                            pe.wait_ge(x_ready, it + 2)
                            for i in range(NT):
                                ins = pe.transpose(psum(f"xT{n}")[:, i * P:(i + 1) * P], xn[:, i, n * P:(n + 1) * P],
                                                   ident[:, :])
                            done(ins, f"xT{n}")
                        elif what in ("q", "k"):
                            project(what, n, it)
                        elif what == "v":
                            if n == 0:
                                free("v", it)
                            by_rows("v", xT, wv, D, (n,))
                        elif what == "sel":
                            stack(n, it)
                        elif what == "s":
                            logits(n, it)
                        elif what == "mT":
                            free("mT", it)
                            drained(pe, f"s{ROUNDS - 1}", it)
                            drained(pe, f"s{ROUNDS - 2}", it)
                            for i in range(NT):
                                ins = pe.transpose(psum("mT")[0:HEADS, i * P:(i + 1) * P],
                                                   m_neg[:, i].rearrange("p e q -> p (e q)"), ident[:, :])
                            done(ins, "mT")
                        elif what == "st":
                            if n == 0:
                                pe.wait_ge(max_stored, it * 64 + 64)
                            logits_t(n, it)
                        elif what == "o":
                            pe.wait_ge(ot_copied, it * 4 + (n + 1))
                            for i in range(NT):
                                ins = pe.transpose(psum(f"o{n}")[:, i * P:(i + 1) * P], o_t[:, i * P:(i + 1) * P],
                                                   ident[:, :])
                            done(ins, f"o{n}")
                        elif what == "av":
                            weigh(n, it)
                        elif what == "oT":
                            free("oT", it)
                            drained(pe, "o3", it)
                            turn("oT", xa)
                        elif what == "wo":
                            free("wo", it)
                            drained(pe, "oT", it)
                            by_rows("wo", xT, wo, D)
                        elif what == "hT":
                            free("hT", it)
                            pe.wait_ge(h2_normal, it + 1)
                            turn("hT", xa)
                        elif what == "logit":
                            drained(pe, "lT", it)
                            for i in range(NT):
                                ins = pe.matmul(psum("logit")[:, i * EXPERTS:(i + 1) * EXPERTS],
                                                l_t[:, i * P:(i + 1) * P], ident[0:EXPERTS, 0:EXPERTS],
                                                start=True, stop=True)
                            done(ins, "logit")
                        elif what == "lT":
                            free("lT", it)
                            drained(pe, "hT", it)
                            for kt in range(KT):
                                ins = mm3(psum("lT")[0:EXPERTS, 0:TOK], [z[:, kt, :] for z in rw],
                                          [x[:, kt, :] for x in hT], kt == 0, kt == KT - 1)
                            done(ins, "lT")
                        elif what == "gT":
                            pe.wait_ge(gate_ready, it + 1)
                            for i in range(NT):
                                ins = pe.transpose(psum("gT")[0:EXPERTS, i * P:(i + 1) * P], gate[:, i, :],
                                                   ident[:, :])
                            done(ins, "gT")

                each_batch(pe, run)


def _constants():
    p = np.arange(P)
    sel = np.zeros((P, 4, P), np.float32)
    for kind, reps in ((SEL_QH, (0, 1)), (SEL_QL, (2,)), (SEL_KH, (0, 2)), (SEL_KL, (1,))):
        for k in range(P):
            for r in reps:
                sel[k, kind, 64 * (k % 32 // 16) + 16 * r + k % 16] = 1.0
    cols = np.zeros((P, NCOLS), np.float32)
    cols[:, SIGN] = np.where(p < 64, 1.0, -1.0)
    cols[:, ONES_ROW] = np.isin(p, (MROW, MROW + 1, 64 + MROW, 65 + MROW))
    for i in range(NT):
        cols[:, POS + i] = P * i + p
    even = np.repeat(np.arange(0, D, 2), 2)
    freq = np.stack([10000.0 ** (2.0 * even / D), np.where(np.arange(D) % 2, math.pi / 2, 0.0)]).astype(np.float32)
    return {"freq": freq.reshape(-1), "ident_c": np.eye(P, dtype=np.float32), "sel_c": sel.reshape(P, 4 * P),
            "cols_c": cols}


def kernel(x, txt, L0_tok_log_dt, L0_tok_inv_A_real, L0_tok_A_imag, L0_tok_B_ri, L0_attn_rby, L0_attn_Wq, L0_attn_bq,
           L0_attn_Wk, L0_attn_bk, L0_attn_Wv, L0_attn_bv, L0_attn_Wo, L0_attn_bo, L0_attn_ln_gamma,
           L0_attn_ln_beta, L0_ffn_shared_up, L0_ffn_shared_down, L0_ffn_routed_up, L0_ffn_routed_down,
           L0_ffn_router_w):
    import concourse.bacc as bacc
    from concourse.bass_utils import run_bass_kernel_spmd

    def transposed(w):
        w = np.asarray(w)
        return w.T.reshape(w.shape[1] // P, P, w.shape[0]).transpose(1, 0, 2).reshape(P, -1)

    up = np.concatenate([np.asarray(L0_ffn_shared_up), np.asarray(L0_ffn_routed_up)])
    down = np.concatenate([np.asarray(L0_ffn_shared_down), np.asarray(L0_ffn_routed_down)])
    c_ri = np.asarray(x).transpose(3, 2, 1, 0)
    arrays = {
        "cT": np.stack([c_ri, c_ri[::-1]]).transpose(1, 2, 0, 3, 4).reshape(2 * NST, 2, HID, BATCH),
        "bT": np.asarray(L0_tok_B_ri).transpose(2, 1, 0).reshape(2 * NST, HID),
        "log_dt": np.asarray(L0_tok_log_dt),
        "inv_a": np.asarray(L0_tok_inv_A_real).T,
        "a_imag": np.asarray(L0_tok_A_imag).T,
        "txt": np.asarray(txt),
        "rby": np.asarray(L0_attn_rby),
        "qk_bias": np.stack([np.asarray(L0_attn_bq).reshape(KT, P), np.asarray(L0_attn_bk).reshape(KT, P)],
                            -1).transpose(1, 0, 2),
        "rows": np.concatenate([np.asarray(v) for v in (L0_attn_bv, L0_attn_bo, L0_attn_ln_gamma, L0_attn_ln_beta)]),
        "w_up": up.transpose(2, 0, 1).reshape(KT, P, NEXP * EDIM).transpose(1, 0, 2).reshape(P, -1),
        "w_down": down.transpose(2, 0, 1).reshape(EDIM, NEXP * D),
        "w_small": np.concatenate([transposed(w) for w in (L0_attn_Wq, L0_attn_Wk, L0_attn_Wv, L0_attn_Wo,
                                                           L0_ffn_router_w)], axis=1),
        **_constants(),
    }
    names = ["cT", "bT", "log_dt", "inv_a", "a_imag", "txt", "rby", "qk_bias", "rows", "freq", "w_up", "w_down",
             "w_small", "ident_c", "sel_c", "cols_c"]
    nc = bacc.Bacc("TRN2", target_bir_lowering=False, num_devices=1)
    feeds, aps = {}, {}
    for name in names:
        a = np.ascontiguousarray(arrays[name])
        feeds[f"in_{name}"] = a
        aps[name] = nc.dram_tensor(f"in_{name}", a.shape, mybir.dt.from_np(a.dtype), kind="ExternalInput").ap()
    out = nc.dram_tensor("out", (BATCH, TOK, D), mybir.dt.float32, kind="ExternalOutput").ap()
    fusion_kernel(nc, **aps, out=out)
    result = run_bass_kernel_spmd(nc, [feeds], core_ids=[0])
    return result.results[0]["out"]
```
